# Optimizing a Trainium2 kernel written in Bass

```python
import numpy as np
import jax
import jax.numpy as jnp

def _softmax(x, axis=-1):
    return jax.nn.softmax(x, axis=axis)

def _gelu(x):
    return jax.nn.gelu(x, approximate=True)

def _silu(x):
    return jax.nn.silu(x)

def _sigmoid(x):
    return jax.nn.sigmoid(x)

def _layernorm(x, axis=-1, eps=1e-05):
    m = jnp.mean(x, axis=axis, keepdims=True)
    v = jnp.var(x, axis=axis, keepdims=True)
    return (x - m) / jnp.sqrt(v + eps)

def _scatter_add(tgt, idx, src, axis=0):
    return tgt.at[idx].add(src)

def _segment_sum(src, seg, n):
    return jax.ops.segment_sum(src, seg, n)
kernel_name = 'mk_early_fusion_d2_tok_img256_r4_1aaf5f'

def setup_inputs(seed: int=0):
    np.random.seed(seed)
    _w = jnp.asarray

    def _rec_inputs():
        import jax
        import jax.numpy as jnp
        _rk = jax.random.key(seed)
        x = 7.22013e-05 + 1.00017 * jax.random.normal(jax.random.fold_in(_rk, 1), (4, 1, 1024, 64), jnp.float32)
        txt = 10 + 10 * jax.random.normal(jax.random.fold_in(_rk, 2), (4, 32, 64), jnp.float32)
        return (x, txt)
    x, txt = _rec_inputs()

    def _L0_tok_setup():
        import jax, jax.numpy as jnp
        import numpy as np
        T, D_IN, D_INT, D_OUT, B = (1024, 64, 64, 64, 8)
        key = jax.random.key(seed)
        ks = jax.random.split(key, 12)
        s_in = 1.0 / np.sqrt(D_IN)
        s_int = 1.0 / np.sqrt(D_INT)
        return {'x_batched': jax.random.normal(ks[0], (B, 1, T, D_IN), dtype=jnp.float32), 'd_gamma_batched': jax.random.uniform(ks[1], (T, T), dtype=jnp.float32), 'Wq': jax.random.uniform(ks[2], (D_IN, D_INT), jnp.float32, -s_in, s_in), 'bq': jax.random.uniform(ks[3], (D_INT,), jnp.float32, -s_in, s_in), 'Wk': jax.random.uniform(ks[4], (D_IN, D_INT), jnp.float32, -s_in, s_in), 'bk': jax.random.uniform(ks[5], (D_INT,), jnp.float32, -s_in, s_in), 'Wv': jax.random.uniform(ks[6], (D_IN, D_INT), jnp.float32, -s_in, s_in), 'bv': jax.random.uniform(ks[7], (D_INT,), jnp.float32, -s_in, s_in), 'Wo': jax.random.uniform(ks[8], (D_INT, D_OUT), jnp.float32, -s_int, s_int), 'bo': jax.random.uniform(ks[9], (D_OUT,), jnp.float32, -s_int, s_int), 'prelu_a': jnp.float32(0.25)}
    _L0_tok_all = _L0_tok_setup()
    _L0_tok_in = {k: v for k, v in _L0_tok_all.items() if k in ('d_gamma_batched', 'Wq', 'bq', 'Wk', 'bk', 'Wv', 'bv', 'Wo', 'bo', 'prelu_a')}
    del _L0_tok_all

    def _L0_attn_setup():
        import jax, jax.numpy as jnp
        import numpy as np
        import math
        NUM_HEADS = 8
        HEAD_SIZE = 32

        def get_alibi_slopes(n_heads):

            def pow2_slopes(n):
                start = 2.0 ** (-2.0 ** (-(math.log2(n) - 3)))
                ratio = start
                return [start * ratio ** i for i in range(n)]
            if math.log2(n_heads).is_integer():
                return np.array(pow2_slopes(n_heads), dtype=np.float32)
            cp2 = 2 ** math.floor(math.log2(n_heads))
            extra = pow2_slopes(2 * cp2)[0::2][:n_heads - cp2]
            return np.array(pow2_slopes(cp2) + extra, dtype=np.float32)
        ALIBI_SLOPES = jnp.asarray(get_alibi_slopes(NUM_HEADS))
        key = jax.random.key(seed)
        ks = jax.random.split(key, 6)
        B, T, C = (32, 128, 64)
        s = 1.0 / math.sqrt(C)
        return {'x': jax.random.normal(ks[0], (B, T, C), dtype=jnp.float32), 'Wq': jax.random.normal(ks[1], (C, NUM_HEADS * HEAD_SIZE), dtype=jnp.float32) * s, 'Wk': jax.random.normal(ks[2], (C, NUM_HEADS * HEAD_SIZE), dtype=jnp.float32) * s, 'Wv': jax.random.normal(ks[3], (C, NUM_HEADS * HEAD_SIZE), dtype=jnp.float32) * s, 'Wo': jax.random.normal(ks[4], (NUM_HEADS * HEAD_SIZE, C), dtype=jnp.float32) * s, 'bo': jax.random.normal(ks[5], (C,), dtype=jnp.float32) * 0.01}
    _L0_attn_all = _L0_attn_setup()
    _L0_attn_in = {k: v for k, v in _L0_attn_all.items() if k in ('Wq', 'Wk', 'Wv', 'Wo', 'bo')}
    del _L0_attn_all

    def _L0_ffn_setup():
        import jax, jax.numpy as jnp
        import numpy as np
        B, H, E, IN, OUT = (1024, 1, 8, 64, 64)

        @jax.custom_vjp
        def bin_active(x):
            return jnp.sign(x)

        def _ba_fwd(x):
            return (jnp.sign(x), x)

        def _ba_bwd(x, g):
            return (g * (jnp.abs(x) <= 1.0).astype(g.dtype),)
        bin_active.defvjp(_ba_fwd, _ba_bwd)

        @jax.custom_vjp
        def bin_gate(x):
            return (x > 0.5).astype(x.dtype)

        def _bg_fwd(x):
            return ((x > 0.5).astype(x.dtype), None)

        def _bg_bwd(_, g):
            return (g,)
        bin_gate.defvjp(_bg_fwd, _bg_bwd)
        key = jax.random.key(seed)
        k1, k2, k3, k4, k5 = jax.random.split(key, 5)
        x = jax.random.normal(k1, (B, H, IN), dtype=jnp.float32)
        weight = jax.random.normal(k2, (H, E, IN, OUT), dtype=jnp.float32) * 0.05
        proj_w = jax.random.normal(k3, (E, IN), dtype=jnp.float32) * 0.05
        proj_b = jax.random.normal(k4, (E,), dtype=jnp.float32) * 0.05
        scale = jax.random.normal(k5, (H, 1, OUT), dtype=jnp.float32) * 0.1
        return {'x': x, 'weight': weight, 'proj_w': proj_w, 'proj_b': proj_b, 'scale': scale}
    _L0_ffn_all = _L0_ffn_setup()
    _L0_ffn_in = {k: v for k, v in _L0_ffn_all.items() if k in ('weight', 'proj_w', 'proj_b', 'scale')}
    del _L0_ffn_all

    def _L1_attn_setup():
        import jax, jax.numpy as jnp
        import numpy as np
        GAMMA = 0.96875
        B, S, D = (4, 1024, 64)

        def _decay_mask(seq_len: int, gamma: float, dtype=jnp.float32) -> jnp.ndarray:
            i = jnp.arange(seq_len)
            diff = i[:, None] - i[None, :]
            lower = diff >= 0
            vals = jnp.exp(diff.astype(dtype) * jnp.log(jnp.asarray(gamma, dtype)))
            return jnp.where(lower, vals, jnp.zeros((), dtype))
        key = jax.random.key(seed)
        k1, k2, k3, k4 = jax.random.split(key, 4)
        scale = 1.0 / np.sqrt(D)
        return {'x': jax.random.normal(k1, (B, S, D), dtype=jnp.float32), 'Wq': jax.random.normal(k2, (D, D), dtype=jnp.float32) * scale, 'Wk': jax.random.normal(k3, (D, D), dtype=jnp.float32) * scale, 'Wv': jax.random.normal(k4, (D, D), dtype=jnp.float32) * scale}
    _L1_attn_all = _L1_attn_setup()
    _L1_attn_in = {k: v for k, v in _L1_attn_all.items() if k in ('Wq', 'Wk', 'Wv')}
    del _L1_attn_all

    def _L1_ffn_setup():
        import jax, jax.numpy as jnp
        import numpy as np
        B, N, D = (16, 1024, 64)
        NUM_EXPERTS, TOP_K, HEADS = (4, 2, 4)
        N_EDGES = 262144
        LN_EPS = 1e-05

        def _layernorm(x, g, b):
            mu = x.mean(-1, keepdims=True)
            var = ((x - mu) ** 2).mean(-1, keepdims=True)
            return (x - mu) * jax.lax.rsqrt(var + LN_EPS) * g + b

        def _forward(x, edge_index, W_gat, att_src, att_dst, b_gat, ln_gamma, ln_beta, W1, b1, W2, b2):
            Bc, Nc, Dc = x.shape
            M = Bc * Nc
            x_flat = x.reshape(M, Dc)
            h = (x_flat @ W_gat).reshape(M, HEADS, NUM_EXPERTS)
            loops = jnp.arange(M, dtype=edge_index.dtype)
            src = jnp.concatenate([edge_index[0], loops])
            dst = jnp.concatenate([edge_index[1], loops])
            a_src = (h * att_src).sum(-1)
            a_dst = (h * att_dst).sum(-1)
            e = jax.nn.leaky_relu(a_src[src] + a_dst[dst], negative_slope=0.2)
            e_max = jax.ops.segment_max(e, dst, num_segments=M)
            ee = jnp.exp(e - e_max[dst])
            denom = jax.ops.segment_sum(ee, dst, num_segments=M)
            alpha = ee / (denom[dst] + 1e-16)
            msg = h[src] * alpha[:, :, None]
            agg = jax.ops.segment_sum(msg, dst, num_segments=M).reshape(M, HEADS * NUM_EXPERTS) + b_gat
            scores = _layernorm(agg, ln_gamma, ln_beta).reshape(M, HEADS, NUM_EXPERTS).mean(1)
            scores = scores.reshape(Bc, Nc, NUM_EXPERTS)
            topk_s, topk_i = jax.lax.top_k(scores, TOP_K)
            w = jax.nn.softmax(topk_s, axis=-1)
            out = jnp.zeros_like(x)
            for ei in range(NUM_EXPERTS):
                g = jnp.where(topk_i == ei, w, 0.0).sum(-1)
                hh = jax.nn.gelu(x @ W1[ei] + b1[ei], approximate=False)
                out = out + g[..., None] * (hh @ W2[ei] + b2[ei])
            return out
        key = jax.random.key(seed)
        ks = jax.random.split(key, 8)
        s = 0.05
        return {'x': jax.random.normal(ks[0], (B, N, D), jnp.float32), 'W_gat': jax.random.normal(ks[1], (D, HEADS * NUM_EXPERTS), jnp.float32) * s, 'att_src': jax.random.normal(ks[2], (HEADS, NUM_EXPERTS), jnp.float32) * s, 'att_dst': jax.random.normal(ks[3], (HEADS, NUM_EXPERTS), jnp.float32) * s, 'b_gat': jnp.zeros((HEADS * NUM_EXPERTS,), jnp.float32), 'ln_gamma': jnp.ones((HEADS * NUM_EXPERTS,), jnp.float32), 'ln_beta': jnp.zeros((HEADS * NUM_EXPERTS,), jnp.float32), 'W1': jax.random.normal(ks[4], (NUM_EXPERTS, D, 2 * D), jnp.float32) * s, 'b1': jnp.zeros((NUM_EXPERTS, 2 * D), jnp.float32), 'W2': jax.random.normal(ks[5], (NUM_EXPERTS, 2 * D, D), jnp.float32) * s, 'b2': jnp.zeros((NUM_EXPERTS, D), jnp.float32), 'edge_index': jax.random.randint(ks[6], (2, N_EDGES), 0, B * N, jnp.int32)}
    _L1_ffn_all = _L1_ffn_setup()
    _L1_ffn_in = {k: v for k, v in _L1_ffn_all.items() if k in ('W_gat', 'att_src', 'att_dst', 'b_gat', 'ln_gamma', 'ln_beta', 'W1', 'b1', 'W2', 'b2', 'edge_index')}
    del _L1_ffn_all
    return {'x': x, 'txt': txt, 'L0_tok_d_gamma_batched': _L0_tok_in['d_gamma_batched'], 'L0_tok_Wq': _L0_tok_in['Wq'], 'L0_tok_bq': _L0_tok_in['bq'], 'L0_tok_Wk': _L0_tok_in['Wk'], 'L0_tok_bk': _L0_tok_in['bk'], 'L0_tok_Wv': _L0_tok_in['Wv'], 'L0_tok_bv': _L0_tok_in['bv'], 'L0_tok_Wo': _L0_tok_in['Wo'], 'L0_tok_bo': _L0_tok_in['bo'], 'L0_tok_prelu_a': _L0_tok_in['prelu_a'], 'L0_attn_Wq': _L0_attn_in['Wq'], 'L0_attn_Wk': _L0_attn_in['Wk'], 'L0_attn_Wv': _L0_attn_in['Wv'], 'L0_attn_Wo': _L0_attn_in['Wo'], 'L0_attn_bo': _L0_attn_in['bo'], 'L0_ffn_weight': _L0_ffn_in['weight'], 'L0_ffn_proj_w': _L0_ffn_in['proj_w'], 'L0_ffn_proj_b': _L0_ffn_in['proj_b'], 'L0_ffn_scale': _L0_ffn_in['scale'], 'L1_attn_Wq': _L1_attn_in['Wq'], 'L1_attn_Wk': _L1_attn_in['Wk'], 'L1_attn_Wv': _L1_attn_in['Wv'], 'L1_ffn_W_gat': _L1_ffn_in['W_gat'], 'L1_ffn_att_src': _L1_ffn_in['att_src'], 'L1_ffn_att_dst': _L1_ffn_in['att_dst'], 'L1_ffn_b_gat': _L1_ffn_in['b_gat'], 'L1_ffn_ln_gamma': _L1_ffn_in['ln_gamma'], 'L1_ffn_ln_beta': _L1_ffn_in['ln_beta'], 'L1_ffn_W1': _L1_ffn_in['W1'], 'L1_ffn_b1': _L1_ffn_in['b1'], 'L1_ffn_W2': _L1_ffn_in['W2'], 'L1_ffn_b2': _L1_ffn_in['b2'], 'L1_ffn_edge_index': _L1_ffn_in['edge_index']}

def reference(x, txt, L0_tok_d_gamma_batched, L0_tok_Wq, L0_tok_bq, L0_tok_Wk, L0_tok_bk, L0_tok_Wv, L0_tok_bv, L0_tok_Wo, L0_tok_bo, L0_tok_prelu_a, L0_attn_Wq, L0_attn_Wk, L0_attn_Wv, L0_attn_Wo, L0_attn_bo, L0_ffn_weight, L0_ffn_proj_w, L0_ffn_proj_b, L0_ffn_scale, L1_attn_Wq, L1_attn_Wk, L1_attn_Wv, L1_ffn_W_gat, L1_ffn_att_src, L1_ffn_att_dst, L1_ffn_b_gat, L1_ffn_ln_gamma, L1_ffn_ln_beta, L1_ffn_W1, L1_ffn_b1, L1_ffn_W2, L1_ffn_b2, L1_ffn_edge_index):
    import jax
    import jax.numpy as jnp

    def _L0_tok_ref(x_batched, d_gamma_batched, Wq, bq, Wk, bk, Wv, bv, Wo, bo, prelu_a):
        import jax, jax.numpy as jnp
        import numpy as np
        T, D_IN, D_INT, D_OUT, B = (1024, 64, 64, 64, 8)
        x = x_batched.reshape(x_batched.shape[0], T, D_IN)
        q = x @ Wq + bq
        k = x @ Wk + bk
        v = x @ Wv + bv
        scores = jnp.einsum('btd,bsd->bts', q, k)
        retained = jnp.einsum('bts,bsd->btd', d_gamma_batched * scores, v)
        y = retained @ Wo + bo
        out = jnp.where(y >= 0, y, prelu_a * y)
        return out

    def _L0_attn_ref(x, Wq, Wk, Wv, Wo, bo):
        import jax, jax.numpy as jnp
        import numpy as np
        import math
        NUM_HEADS = 8
        HEAD_SIZE = 32

        def get_alibi_slopes(n_heads):

            def pow2_slopes(n):
                start = 2.0 ** (-2.0 ** (-(math.log2(n) - 3)))
                ratio = start
                return [start * ratio ** i for i in range(n)]
            if math.log2(n_heads).is_integer():
                return np.array(pow2_slopes(n_heads), dtype=np.float32)
            cp2 = 2 ** math.floor(math.log2(n_heads))
            extra = pow2_slopes(2 * cp2)[0::2][:n_heads - cp2]
            return np.array(pow2_slopes(cp2) + extra, dtype=np.float32)
        ALIBI_SLOPES = jnp.asarray(get_alibi_slopes(NUM_HEADS))
        B, T, C = x.shape
        H, D = (NUM_HEADS, HEAD_SIZE)
        q = (x @ Wq).reshape(B, T, H, D).transpose(0, 2, 1, 3)
        k = (x @ Wk).reshape(B, T, H, D).transpose(0, 2, 1, 3)
        v = (x @ Wv).reshape(B, T, H, D).transpose(0, 2, 1, 3)
        scale = 1.0 / math.sqrt(D)
        wei = jnp.einsum('bhtd,bhsd->bhts', q, k) * scale
        pos = jnp.arange(T)
        rel = (pos[None, :] - pos[:, None]).astype(jnp.float32)
        bias = ALIBI_SLOPES[:, None, None] * rel[None, :, :]
        wei = wei + bias[None]
        causal = pos[None, :] <= pos[:, None]
        wei = jnp.where(causal[None, None], wei, -jnp.inf)
        wei = jax.nn.softmax(wei, axis=-1)
        out = jnp.einsum('bhts,bhsd->bhtd', wei, v)
        out = out.transpose(0, 2, 1, 3).reshape(B, T, H * D)
        return out @ Wo + bo

    def _L0_ffn_ref(x, weight, proj_w, proj_b, scale):
        import jax, jax.numpy as jnp
        import numpy as np
        B, H, E, IN, OUT = (1024, 1, 8, 64, 64)

        @jax.custom_vjp
        def bin_active(x):
            return jnp.sign(x)

        def _ba_fwd(x):
            return (jnp.sign(x), x)

        def _ba_bwd(x, g):
            return (g * (jnp.abs(x) <= 1.0).astype(g.dtype),)
        bin_active.defvjp(_ba_fwd, _ba_bwd)

        @jax.custom_vjp
        def bin_gate(x):
            return (x > 0.5).astype(x.dtype)

        def _bg_fwd(x):
            return ((x > 0.5).astype(x.dtype), None)

        def _bg_bwd(_, g):
            return (g,)
        bin_gate.defvjp(_bg_fwd, _bg_bwd)
        xh = jnp.transpose(x, (1, 0, 2))
        gate = jax.nn.sigmoid(jnp.einsum('hbi,ei->hbe', xh, proj_w) + proj_b)
        gate = bin_gate(gate)
        w = jnp.einsum('hbe,heio->hbio', gate, weight)
        xb = bin_active(xh)
        wb = bin_active(w)
        y = jnp.einsum('hbi,hbio->hbo', xb, wb)
        y = y * scale
        return jnp.transpose(y, (1, 0, 2))

    def _L1_attn_ref(x, Wq, Wk, Wv):
        import jax, jax.numpy as jnp
        import numpy as np
        GAMMA = 0.96875
        B, S, D = (4, 1024, 64)

        def _decay_mask(seq_len: int, gamma: float, dtype=jnp.float32) -> jnp.ndarray:
            i = jnp.arange(seq_len)
            diff = i[:, None] - i[None, :]
            lower = diff >= 0
            vals = jnp.exp(diff.astype(dtype) * jnp.log(jnp.asarray(gamma, dtype)))
            return jnp.where(lower, vals, jnp.zeros((), dtype))
        q = jnp.einsum('bsh,dh->bsd', x, Wq)
        k = jnp.einsum('bsh,dh->bsd', x, Wk)
        v = jnp.einsum('bsh,dh->bsd', x, Wv)
        seq_len = x.shape[1]
        mask = _decay_mask(seq_len, GAMMA, x.dtype)
        scores = jnp.einsum('bsd,btd->bst', q, k) * mask[None, :, :]
        return jnp.einsum('bst,btd->bsd', scores, v)

    def _L1_ffn_ref(x, W_gat, att_src, att_dst, b_gat, ln_gamma, ln_beta, W1, b1, W2, b2, edge_index):
        import jax, jax.numpy as jnp
        import numpy as np
        B, N, D = (16, 1024, 64)
        NUM_EXPERTS, TOP_K, HEADS = (4, 2, 4)
        N_EDGES = 262144
        LN_EPS = 1e-05

        def _layernorm(x, g, b):
            mu = x.mean(-1, keepdims=True)
            var = ((x - mu) ** 2).mean(-1, keepdims=True)
            return (x - mu) * jax.lax.rsqrt(var + LN_EPS) * g + b

        def _forward(x, edge_index, W_gat, att_src, att_dst, b_gat, ln_gamma, ln_beta, W1, b1, W2, b2):
            Bc, Nc, Dc = x.shape
            M = Bc * Nc
            x_flat = x.reshape(M, Dc)
            h = (x_flat @ W_gat).reshape(M, HEADS, NUM_EXPERTS)
            loops = jnp.arange(M, dtype=edge_index.dtype)
            src = jnp.concatenate([edge_index[0], loops])
            dst = jnp.concatenate([edge_index[1], loops])
            a_src = (h * att_src).sum(-1)
            a_dst = (h * att_dst).sum(-1)
            e = jax.nn.leaky_relu(a_src[src] + a_dst[dst], negative_slope=0.2)
            e_max = jax.ops.segment_max(e, dst, num_segments=M)
            ee = jnp.exp(e - e_max[dst])
            denom = jax.ops.segment_sum(ee, dst, num_segments=M)
            alpha = ee / (denom[dst] + 1e-16)
            msg = h[src] * alpha[:, :, None]
            agg = jax.ops.segment_sum(msg, dst, num_segments=M).reshape(M, HEADS * NUM_EXPERTS) + b_gat
            scores = _layernorm(agg, ln_gamma, ln_beta).reshape(M, HEADS, NUM_EXPERTS).mean(1)
            scores = scores.reshape(Bc, Nc, NUM_EXPERTS)
            topk_s, topk_i = jax.lax.top_k(scores, TOP_K)
            w = jax.nn.softmax(topk_s, axis=-1)
            out = jnp.zeros_like(x)
            for ei in range(NUM_EXPERTS):
                g = jnp.where(topk_i == ei, w, 0.0).sum(-1)
                hh = jax.nn.gelu(x @ W1[ei] + b1[ei], approximate=False)
                out = out + g[..., None] * (hh @ W2[ei] + b2[ei])
            return out
        return _forward(x, edge_index, W_gat, att_src, att_dst, b_gat, ln_gamma, ln_beta, W1, b1, W2, b2)
    h = _L0_tok_ref(x, L0_tok_d_gamma_batched, L0_tok_Wq, L0_tok_bq, L0_tok_Wk, L0_tok_bk, L0_tok_Wv, L0_tok_bv, L0_tok_Wo, L0_tok_bo, L0_tok_prelu_a)
    h = jnp.concatenate([h, txt], axis=1)
    h = h + _L0_attn_ref(_layernorm(h, axis=-1), L0_attn_Wq, L0_attn_Wk, L0_attn_Wv, L0_attn_Wo, L0_attn_bo)
    h = h + _L0_ffn_ref(_layernorm(h, axis=-1), L0_ffn_weight, L0_ffn_proj_w, L0_ffn_proj_b, L0_ffn_scale)
    h = h + _L1_attn_ref(_layernorm(h, axis=-1), L1_attn_Wq, L1_attn_Wk, L1_attn_Wv)
    h = h + _L1_ffn_ref(_layernorm(h, axis=-1), L1_ffn_W_gat, L1_ffn_att_src, L1_ffn_att_dst, L1_ffn_b_gat, L1_ffn_ln_gamma, L1_ffn_ln_beta, L1_ffn_W1, L1_ffn_b1, L1_ffn_W2, L1_ffn_b2, L1_ffn_edge_index)
    return h

_drawn_inputs = setup_inputs


def setup_inputs(seed=0):
    import zlib

    import numpy as np

    out = dict(_drawn_inputs(seed))
    spreads = {'L1_ffn_b_gat': (0.0, 2.0),
     'L1_ffn_ln_gamma': (1.0, 0.6),
     'L1_ffn_ln_beta': (0.0, 0.8),
     'L1_ffn_b1': (0.0, 2.0),
     'L1_ffn_b2': (0.0, 2.0)}
    factors = {'L0_tok_bo': 25.226,
     'L0_attn_bo': 64.0,
     'L0_ffn_proj_w': 7.938,
     'L0_ffn_proj_b': 19.958,
     'L1_ffn_W_gat': 8.0,
     'L1_ffn_att_src': 8.0,
     'L1_ffn_att_dst': 25.78,
     'L1_ffn_W1': 8.0,
     'L1_ffn_W2': 8.0}
    for name, (base, spread) in spreads.items():
        noise = np.random.default_rng([zlib.crc32(name.encode()), seed]).standard_normal(out[name].shape)
        drawn = base * np.exp(spread * noise) if base else spread * noise
        out[name] = jnp.asarray(drawn.astype(out[name].dtype))
    for name, factor in factors.items():
        out[name] = (out[name] * factor).astype(out[name].dtype)
    return out
```

```python
from contextlib import ExitStack

import numpy as np

import concourse.bass as bass
from concourse import mybir

F32 = mybir.dt.float32
BF16 = mybir.dt.bfloat16
I32 = mybir.dt.int32
ALU = mybir.AluOpType
ACT = mybir.ActivationFunctionType
X = mybir.AxisListType.X

B, T, TXT, D = 4, 1024, 32, 64
S = T + TXT
N = B * S
P = 128
NT = N // P
CH = 352
NCH = S // CH
HEADS, HD = 8, 32
GH = 4
SB = (S + P - 1) // P
SP_ = SB * P
GAMMA = 0.96875
EPS = 1e-5
MASKED = -1e30


def rows(j):
    return min(P, S - P * j)


TILES = [(c, j, max(CH * c, P * j), CH * (c + 1) - max(CH * c, P * j))
         for c in range(NCH) for j in range(SB) if P * j < CH * (c + 1)]


def settle(eng):
    eng.nop(nofuse=True)


class Arena:

    def __init__(self, tensor):
        self.tensor, self.at = tensor, 0

    def take(self, parts, cols, dtype=F32):
        words = cols if dtype != BF16 else (cols + 1) // 2
        words = (words + 7) // 8 * 8
        ap = self.tensor[0:parts, self.at:self.at + words]
        self.at += words
        assert self.at <= self.tensor.shape[1], self.at
        if dtype != F32:
            ap = ap.bitcast(dtype)
        return ap[:, 0:cols]


def build(nc, a, c):
    ctx = ExitStack()

    def sem(name):
        return ctx.enter_context(nc.semaphore(name))

    def sbuf(name, parts, cols, dtype=F32):
        return ctx.enter_context(nc.sbuf_tensor(name, [parts, cols], dtype))

    ident = sbuf("ident", P, P)
    identb = sbuf("identb", P, P, BF16)
    h = sbuf("h", P, NT * D)
    xhat = sbuf("xhat", P, NT * D)
    xT = sbuf("xT", D + 1, N)
    dT = sbuf("dT", D, N)
    stats = sbuf("stats", P, 4 * NT)
    weights = sbuf("weights", P, 2048)
    arena = sbuf("arena", P, 37800)
    ps = ctx.enter_context(nc.psum_tensor("ps", [P, 8, 512], F32))
    h3 = h[:].rearrange("p (k d) -> p k d", d=D)
    xh3 = xhat[:].rearrange("p (k d) -> p k d", d=D)

    m = dict(nc=nc, a=a, c=c, sem=sem, ident=ident, identb=identb, h3=h3, xh3=xh3, xT=xT, dT=dT,
             stats=stats, weights=weights, arena=arena, ps=ps, ctx=ctx)
    with ctx:
        gated_attention(m)
        norm(m, "n1", first=True)
        softmax_attention(m)
        norm(m, "n2")
        binary_experts(m)
        norm(m, "n3")
        retention(m)
        norm(m, "n4")
        graph_experts(m)


def gated_attention(m):
    nc, a, sem, ps, dT, ident = m["nc"], m["a"], m["sem"], m["ps"], m["dT"], m["ident"]
    ar = Arena(m["arena"])
    NB = T // P
    TH = 512
    gn = ar.take(P, NB * T)
    gT = ar.take(P, NB * T)
    xn = ar.take(P, NB * D)
    xb = ar.take(D + 1, T)
    q = ar.take(D, T)
    k = ar.take(D, T)
    v = ar.take(P, NB * D)
    NP = 4
    p = [ar.take(P, TH) for _ in range(NP)]
    ret = [ar.take(D, TH) for _ in range(2)]
    y = ar.take(D, TH)
    yn = ar.take(D, TH)
    txt = ar.take(P, D)
    w = m["weights"]
    wq, wk, wv, wo = (w[0:D + 1, D * i:D * i + D] for i in range(4))
    bo, pa = w[0:D, 4 * D:4 * D + 1], w[0:D, 4 * D + 1:4 * D + 2]
    ident_in, loaded, gamma_in, x_in = sem("a_ident_in"), sem("a_loaded"), sem("a_gamma_in"), sem("a_x_in")
    ones = sem("a_ones")
    g_turned, g_kept, t_turned, t_kept = sem("a_g_turned"), sem("a_g_kept"), sem("a_t_turned"), sem("a_t_kept")
    prep, prep_slots = sem("a_prep"), sem("a_prep_slots")
    scores, gated, summed = sem("a_scores"), sem("a_gated"), sem("a_summed")
    ret_kept, y_made, y_kept, y_step = sem("a_ret_kept"), sem("a_y_made"), sem("a_y_kept"), sem("a_y_step")
    g3 = gn.rearrange("p (k t) -> p k t", k=NB)
    gT3 = gT.rearrange("p (k t) -> p k t", k=NB)
    v3 = v.rearrange("p (k d) -> p k d", k=NB)

    with nc.Block() as block:
        @block.sync
        def _(sp):
            sp.dma_start(ident[:], m["c"]["ident"]).then_inc(ident_in, 16)
            sp.dma_start(m["identb"][:], m["c"]["identb"]).then_inc(ident_in, 16)
            gsrc = a["L0_tok_d_gamma_batched"].rearrange("(k p) s -> p k s", p=P)
            for n in range(4):
                sp.dma_start(g3[:, 2 * n:2 * n + 2, :], gsrc[:, 2 * n:2 * n + 2, :]).then_inc(gamma_in, 16)
            for dst, name, bias in ((wq, "L0_tok_Wq", "L0_tok_bq"), (wk, "L0_tok_Wk", "L0_tok_bk"),
                                    (wv, "L0_tok_Wv", "L0_tok_bv")):
                sp.dma_start(dst[0:D], a[name]).then_inc(loaded, 16)
                sp.dma_start(dst[D:D + 1], a[bias].rearrange("(o d) -> o d", o=1)).then_inc(loaded, 16)
            sp.dma_start(wo[0:D], a["L0_tok_Wo"]).then_inc(loaded, 16)
            sp.dma_start(bo, a["L0_tok_bo"].rearrange("(d o) -> d o", o=1)).then_inc(loaded, 16)
            sp.dma_start(pa, a["L0_tok_prelu_a"].rearrange("(o d) -> o d", o=1).broadcast_to([D, 1])).then_inc(loaded, 16)
            sp.dma_start(txt, a["txt"].rearrange("b t d -> (b t) d")).then_inc(loaded, 16)
            xsrc = a["x"].rearrange("b o (k p) d -> b p (o k) d", p=P)
            with sp.Fori(0, B) as b:
                sp.wait_ge(prep, 8 * b + 1)
                settle(sp)
                sp.dma_start(xn.rearrange("p (k d) -> p k d", k=NB),
                             xsrc[bass.ds(b, 1)].rearrange("b p k d -> p (b k) d")).then_inc(x_in, 16)

        @block.tensor
        def _(pe):
            pe.sem_inc(prep, 1)
            pe.wait_ge(ident_in, 32)
            pe.wait_ge(loaded, 16 * 10)
            pe.transpose(ps[0:D, 7, 0:P], txt, ident[:]).then_inc(t_turned, 1)
            for n in range(2 * NB):
                j, th = n % NB, n // NB
                pe.wait_ge(gamma_in, 16 * (2 * th + 2))
                if n >= 4:
                    pe.wait_ge(g_kept, n - 3)
                for i in range(4):
                    last = pe.transpose(ps[:, n % 4, P * i:P * i + P], g3[:, 4 * th + i, P * j:P * j + P], ident[:])
                last.then_inc(g_turned, 1)
            pe.wait_ge(g_kept, 2 * NB)
            pe.wait_ge(t_kept, 1)
            pe.wait_ge(ones, 1)
            with pe.Fori(0, B) as b:
                pe.wait_ge(x_in, 16 * b + 16)
                for n in range(2):
                    pe.wait_ge(prep_slots, 8 * b + n + 1)
                    settle(pe)
                    for i in range(4):
                        last = pe.transpose(ps[0:D, 6 + n, P * i:P * i + P], xn[:, D * (4 * n + i):D * (4 * n + i) + D], ident[:])
                    last.then_inc(prep, 1)
                pe.wait_ge(prep_slots, 8 * b + 2 + 2)
                for n in range(2, 6):
                    pe.wait_ge(prep_slots, 8 * b + n + 1)
                    wt, th = (wq, wk)[(n - 2) // 2], n % 2
                    pe.matmul(ps[0:D, 6 + n % 2, :], wt, xb[:, TH * th:TH * th + TH], start=True, stop=True).then_inc(prep, 1)
                for n in range(6, 8):
                    pe.wait_ge(prep_slots, 8 * b + n + 1)
                    for i in range(4):
                        j = 4 * (n - 6) + i
                        last = pe.matmul(ps[:, 6 + n % 2, D * i:D * i + D], xb[:, P * j:P * j + P], wv, start=True, stop=True)
                    last.then_inc(prep, 1)
                pe.wait_ge(prep_slots, 8 * b + 8 + 2)

                def score(n):
                    th, j = n // NB, n % NB
                    pe.wait_ge(gated, 16 * b + n + 1)
                    pe.matmul(ps[:, n % 4, :], k[:, P * j:P * j + P], q[:, TH * th:TH * th + TH],
                              start=True, stop=True).then_inc(scores, 1)

                def weigh(n):
                    th, j = n // NB, n % NB
                    pe.wait_ge(gated, 16 * b + n + 1 + 4)
                    if j == 0:
                        pe.wait_ge(y_kept, 2 * b + th + 1)
                    pe.matmul(ps[0:D, 4 + th, :], v3[:, j, :], p[n % NP], start=(j == 0), stop=(j == NB - 1)).then_inc(summed, 1)

                def project(th):
                    pe.wait_ge(ret_kept, 2 * b + th + 1)
                    settle(pe)
                    pe.matmul(ps[0:D, 4 + th, :], wo[0:D], ret[th], start=True, stop=True).then_inc(y_made, 1)

                score(0)
                score(1)
                for n in range(2 * NB):
                    if n + 2 < 2 * NB:
                        score(n + 2)
                    weigh(n)
                    if n == NB + 1:
                        project(0)
                project(1)

        @block.scalar
        def _(act):
            act.sem_inc(prep_slots, 2)
            with act.Fori(0, B) as b:
                for n in range(8):
                    act.wait_ge(prep, 8 * b + n + 1 + 1)
                    bank = ps[:, 6 + n % 2, :]
                    if n < 2:
                        dst, src = xb[0:D, TH * n:TH * n + TH], bank[0:D]
                    elif n < 6:
                        dst, src = (q, k)[(n - 2) // 2][:, TH * (n % 2):TH * (n % 2) + TH], bank[0:D]
                    else:
                        dst, src = v[:, 4 * D * (n - 6):4 * D * (n - 6) + 4 * D], bank[:, 0:4 * D]
                    act.activation(dst, src, ACT.Copy).then_inc(prep_slots, 1)
                for th in range(2):
                    act.wait_ge(summed, 16 * b + NB * (th + 1) + 4)
                    act.activation(ret[th], ps[0:D, 4 + th, :], ACT.Copy).then_inc(ret_kept, 1)

        @block.vector
        def _(dve):
            dve.memset(xb[D:D + 1, :], 1.0).then_inc(ones, 1)
            dve.sem_inc(gated, 4)
            dve.sem_inc(summed, 4)
            dve.sem_inc(y_kept, 2)
            dve.wait_ge(t_turned, 1)
            for b in range(B):
                last = dve.tensor_copy(dT[:, S * b + T:S * b + S], ps[0:D, 7, TXT * b:TXT * b + TXT])
            last.then_inc(t_kept, 1)
            for n in range(2 * NB):
                j, th = n % NB, n // NB
                dve.wait_ge(g_turned, n + 1)
                dve.tensor_copy(gT3[:, j, TH * th:TH * th + TH], ps[:, n % 4, :]).then_inc(g_kept, 1)
            with dve.Fori(0, B) as b:
                def finish(th):
                    n = 3 * (2 * b + th)
                    dve.wait_ge(y_made, 2 * b + th + 1)
                    dve.tensor_scalar(y, ps[0:D, 4 + th, :], bo, None, ALU.add).then_inc(y_step, 1)
                    dve.wait_ge(y_step, n + 1)
                    dve.tensor_scalar(yn, y, 0.0, pa, ALU.min, ALU.mult).then_inc(y_step, 1)
                    dve.wait_ge(y_step, n + 2)
                    dve.scalar_tensor_tensor(dT[:, bass.ds(b * S + TH * th, TH)], y, 0.0, yn, ALU.max, ALU.add).then_inc(y_step, 1)
                    dve.wait_ge(y_step, n + 3)
                    dve.sem_inc(y_kept, 1)

                for n in range(2 * NB):
                    th, j = n // NB, n % NB
                    dve.wait_ge(scores, 16 * b + n + 1)
                    dve.wait_ge(summed, 16 * b + n + 1)
                    dve.tensor_tensor(p[n % NP], ps[:, n % 4, :], gT3[:, j, TH * th:TH * th + TH], ALU.mult).then_inc(gated, 1)
                    if n == NB + 3:
                        finish(0)
                finish(1)


def norm(m, tag, first=False):
    nc, sem, ps, dT, ident, h3, xh3, xT = (m[k] for k in ("nc", "sem", "ps", "dT", "ident", "h3", "xh3", "xT"))
    sums, var, rstd = (m["stats"][:, NT * i:NT * i + NT] for i in range(3))
    sq = m["arena"][:, 0:NT * D].rearrange("p (k d) -> p k d", d=D)
    turned, step, root, back, kept = (sem(f"{tag}_{s}") for s in ("turned", "step", "root", "back", "kept"))
    groups = [range(8 * g, min(8 * g + 8, NT)) for g in range((NT + 7) // 8)]
    quads = [range(4 * g, min(4 * g + 4, NT)) for g in range((NT + 3) // 4)]
    NG = len(groups)

    with nc.Block() as block:
        @block.tensor
        def _(pe):
            for g, tiles in enumerate(groups):
                for i, t in enumerate(tiles):
                    last = pe.transpose(ps[:, g, D * i:D * i + D], dT[:, P * t:P * t + P], ident[0:D, 0:D])
                last.then_inc(turned, 1)
            for g, tiles in enumerate(quads):
                pe.wait_ge(step, NG + 7)
                if g >= 3:
                    pe.wait_ge(kept, g - 2)
                for i, t in enumerate(tiles):
                    last = pe.transpose(ps[0:D, 5 + g % 3, P * i:P * i + P], xh3[:, t, :], ident[:])
                last.then_inc(back, 1)

        @block.vector
        def _(dve):
            for g, tiles in enumerate(groups):
                lo, hi = tiles[0], tiles[-1] + 1
                dve.wait_ge(turned, g + 1)
                src = ps[:, g, 0:D * (hi - lo)].rearrange("p (k d) -> p k d", d=D)
                if first:
                    dve.tensor_copy(h3[:, lo:hi, :], src).then_inc(step, 1)
                else:
                    dve.tensor_tensor(h3[:, lo:hi, :], h3[:, lo:hi, :], src, ALU.add).then_inc(step, 1)
            if first:
                dve.memset(xT[D:D + 1, :], 1.0)
            dve.wait_ge(step, NG)
            dve.tensor_reduce(sums, h3, X, ALU.add).then_inc(step, 1)
            dve.wait_ge(step, NG + 1)
            dve.tensor_scalar(sums, sums, 1.0 / D, None, ALU.mult).then_inc(step, 1)
            dve.wait_ge(step, NG + 2)
            mean = sums.rearrange("p (k o) -> p k o", o=1).broadcast_to([P, NT, D])
            dve.tensor_tensor(xh3, h3, mean, ALU.subtract).then_inc(step, 1)
            dve.wait_ge(step, NG + 3)
            dve.tensor_tensor(sq, xh3, xh3, ALU.mult).then_inc(step, 1)
            dve.wait_ge(step, NG + 4)
            dve.tensor_reduce(var, sq, X, ALU.add).then_inc(step, 1)
            dve.wait_ge(step, NG + 5)
            dve.tensor_scalar(var, var, 1.0 / D, EPS, ALU.mult, ALU.add).then_inc(step, 1)
            dve.wait_ge(root, 1)
            dve.reciprocal(rstd, rstd).then_inc(root, 1)
            dve.wait_ge(root, 2)
            scale = rstd.rearrange("p (k o) -> p k o", o=1).broadcast_to([P, NT, D])
            dve.tensor_tensor(xh3, xh3, scale, ALU.mult).then_inc(step, 1)

        @block.scalar
        def _(act):
            act.wait_ge(step, NG + 6)
            act.activation(rstd, var, ACT.Sqrt).then_inc(root, 1)
            for g, tiles in enumerate(quads):
                lo, n = P * tiles[0], P * len(tiles)
                act.wait_ge(back, g + 1)
                act.activation(xT[0:D, lo:lo + n], ps[0:D, 5 + g % 3, 0:n], ACT.Copy).then_inc(kept, 1)


def softmax_attention(m):
    nc, a, c, sem, ps, dT, xT = (m[k] for k in ("nc", "a", "c", "sem", "ps", "dT", "xT"))
    ar = Arena(m["arena"])
    identb, ident = m["identb"], m["ident"]
    q1 = [ar.take(102, GH * SP_, BF16).rearrange("p (h t) -> p h t", h=GH) for _ in range(2)]
    k1 = [ar.take(102, GH * SP_, BF16).rearrange("p (h t) -> p h t", h=GH) for _ in range(2)]
    q2 = [ar.take(96, GH * S, BF16).rearrange("p (h t) -> p h t", h=GH) for _ in range(2)]
    k2 = [ar.take(96, GH * S, BF16).rearrange("p (h t) -> p h t", h=GH) for _ in range(2)]
    parts = [[ar.take(P, S, BF16) for _ in range(3)] for _ in range(2)]
    qk = [ar.take(P, S) for _ in range(2)]
    vs = ar.take(P, SB * P)
    v = [ar.take(P, SB * P) for _ in range(2)]
    xb = ar.take(D + 1, S)
    prob = [ar.take(P, GH * CH).rearrange("p (h t) -> p h t", h=GH) for _ in range(2)]
    oT = [ar.take(P, S) for _ in range(2)]
    rec = ar.take(P, CH)
    ones = ar.take(P, HD)
    mask_kq, mask_qk = ar.take(P, P, BF16), ar.take(P, P, BF16)
    mx = ar.take(P, GH * SB * 3)
    mc = ar.take(P, GH * SB)
    mhl = ar.take(GH * SB, 2 * P, BF16)
    w = m["weights"]
    wq, wk, wv = (w[0:D + 1, 256 * i:256 * i + 256] for i in range(3))
    wo = [w[:, 768 + D * g:768 + D * g + D] for g in range(2)]
    bo = w[0:D, 900:901]
    hml = nc.dram_tensor("split_parts", [6, P, S], BF16, kind="Internal").ap()

    loaded, set_up = sem("b_loaded"), sem("b_set_up")
    xb_in, projected, taken_act, taken_dve = sem("b_xb_in"), sem("b_projected"), sem("b_taken_act"), sem("b_taken_dve")
    split, parts_out, first_in, second_in = sem("b_split"), sem("b_parts_out"), sem("b_first_in"), sem("b_second_in")
    maxed, m_split, m_in = sem("b_maxed"), sem("b_m_split"), sem("b_m_in")
    scores, probs, weighed = sem("b_scores"), sem("b_probs"), sem("b_weighed")
    rec_made, normed, out_made, out_kept = sem("b_rec_made"), sem("b_normed"), sem("b_out_made"), sem("b_out_kept")

    UNITS = 2 * B
    PIECES = [(j, i, n, min(512, P * i + rows(i) - 512 * n)) for j in range(GH) for i in range(SB)
              for n in range((P * i + rows(i) + 511) // 512)]
    NM, NPJ = len(PIECES) + 1, 9
    NTL = len(TILES)
    FIRST = 2 * NPJ + NM
    LAST_TILE = [max(n for n in range(NTL) if TILES[n][0] == ch) for ch in range(NCH)]
    PER_SLOT, SLOT0 = 5, 4

    def bank(n):
        return 6 + n % 2

    with nc.Block() as block:
        @block.sync
        def _(sp):
            for dst, name in ((wq, "Wq"), (wk, "Wk"), (wv, "Wv")):
                sp.dma_start(dst[0:D], a["L0_attn_" + name]).then_inc(loaded, 16)
            for g in range(2):
                sp.dma_start(wo[g], a["L0_attn_Wo"][P * g:P * g + P]).then_inc(loaded, 16)
            sp.dma_start(bo, a["L0_attn_bo"].rearrange("(d o) -> d o", o=1)).then_inc(loaded, 16)
            sp.dma_start(mask_kq, c["mask_kq"]).then_inc(loaded, 16)
            sp.dma_start(mask_qk, c["mask_qk"]).then_inc(loaded, 16)
            for g in range(2):
                sp.dma_start(k1[g][96:102], c["bias_k"][:, GH * g:GH * g + GH]).then_inc(loaded, 16)
                sp.dma_start(q1[g][96:100], c["bias_q"][:, GH * g:GH * g + GH]).then_inc(loaded, 16)

            def parts_to_dram(u):
                for n in range(6):
                    sp.wait_ge(split, 8 * u + (1, 3, 4, 5, 7, 8)[n])
                    sp.dma_start(hml[n], parts[n // 3][n % 3]).then_inc(parts_out, 16)

            def stacks_in(u, g):
                sp.wait_ge(parts_out, 96 * u + 96)
                settle(sp)
                if not isinstance(u, int):
                    sp.wait_ge(scores, 2 * NTL * (u - 1))
                for stack, order, done in ((q1, (0, 1, 0), first_in), (k1, (3, 3, 4), first_in),
                                           (q2, (1, 2, 0), second_in), (k2, (4, 3, 5), second_in)):
                    for s, n in enumerate(order):
                        sp.dma_start(stack[g][32 * s:32 * s + 32, :, 0:S],
                                     hml[n].rearrange("(h d) t -> d h t", h=GH)).then_inc(done, 16)
                sp.wait_ge(taken_act, NPJ * u + NPJ)
                if not isinstance(u, int):
                    sp.wait_ge(weighed, NTL * (u - 1) + 2)
                sp.dma_start(v[g], vs).then_inc(second_in, 16)

            def maxima_in(u, g):
                sp.wait_ge(m_split, 2 * u + 2)
                for n in range(2):
                    sp.dma_start(q1[g][100 + n:101 + n, :, :].rearrange("p h t -> p (h t)"),
                                 mhl[:, P * n:P * n + P]).then_inc(m_in, 16)

            parts_to_dram(0)
            stacks_in(0, 0)
            sp.wait_ge(first_in, 96)
            sp.wait_ge(second_in, 112)
            parts_to_dram(1)
            stacks_in(1, 1)
            sp.wait_ge(first_in, 192)
            sp.wait_ge(second_in, 224)
            maxima_in(0, 0)

            def slot(u, g, project, maxima):
                if project:
                    parts_to_dram(u + 2)
                if maxima:
                    maxima_in(u + 1, 1 - g)
                if project:
                    stacks_in(u + 2, g)
                    sp.wait_ge(first_in, 96 * (u + 3))
                    settle(sp)
                    sp.wait_ge(second_in, 112 * (u + 3))
                    settle(sp)

            with sp.Fori(0, B - 1) as b:
                slot(2 * b, 0, True, True)
                slot(2 * b + 1, 1, True, True)
            slot(UNITS - 2, 0, False, True)
            slot(UNITS - 1, 1, False, False)

        @block.gpsimd
        def _(pool):
            pool.memset(ones, 1.0).then_inc(set_up, 1)
            pool.memset(vs[:, P * (SB - 1):], 0.0).then_inc(set_up, 1)

            def split_unit(u, first_of_batch):
                if first_of_batch is not None:
                    if first_of_batch[1] is not None:
                        pool.wait_ge(projected, first_of_batch[1])
                        settle(pool)
                    pool.tensor_copy(xb, xT[:, first_of_batch[0]]).then_inc(xb_in, 1)
                for n in range(2):
                    hi, mid, lo = parts[n]
                    at = 8 * u + 4 * n
                    pool.wait_ge(taken_act, NPJ * u + 3 * n + 3)
                    if not (isinstance(u, int) and u == 0):
                        pool.wait_ge(parts_out, 96 * u)
                    settle(pool)
                    pool.tensor_copy(hi, qk[n]).then_inc(split, 1)
                    pool.wait_ge(split, at + 1)
                    settle(pool)
                    pool.tensor_tensor(qk[n], qk[n], hi, ALU.subtract).then_inc(split, 1)
                    pool.wait_ge(split, at + 2)
                    settle(pool)
                    pool.tensor_copy(mid, qk[n]).then_inc(split, 1)
                    pool.wait_ge(split, at + 3)
                    settle(pool)
                    pool.tensor_tensor(lo, qk[n], mid, ALU.subtract).then_inc(split, 1)

            split_unit(0, (slice(0, S), None))
            split_unit(1, None)
            with pool.Fori(0, B - 1) as b:
                split_unit(2 * b + 2, (bass.ds((b + 1) * S, S), 2 * NPJ + 2 * (NPJ + NM) * b))
                split_unit(2 * b + 3, None)

        @block.tensor
        def _(pe):
            pe.wait_ge(loaded, 16 * 12)
            pe.wait_ge(set_up, 3)

            def project(u, g, n, use):
                pe.wait_ge(xb_in, u // 2 + 1 if isinstance(u, int) else batch_base[0])
                settle(pe)
                if n < 6:
                    wt, ch = (wq, wk)[n // 3], n % 3
                    pe.matmul(ps[:, bank(use), 0:CH], wt[:, P * g:P * g + P], xb[:, CH * ch:CH * ch + CH],
                              start=True, stop=True).then_inc(projected, 1)
                else:
                    for i in range(3):
                        j = 3 * (n - 6) + i
                        last = pe.matmul(ps[0:rows(j), bank(use), P * i:P * i + P], xb[:, P * j:P * j + rows(j)],
                                         wv[:, P * g:P * g + P], start=True, stop=True)
                    last.then_inc(projected, 1)

            def maxima(u, g, n, use):
                if n == NM - 1:
                    pe.wait_ge(maxed, u + 1)
                    settle(pe)
                    pe.transpose(ps[0:GH * SB, bank(use), 0:P], mc, ident[:]).then_inc(projected, 1)
                    return
                j, i, k, width = PIECES[n]
                settle(pe)
                if n == 0:
                    pe.wait_ge(first_in, 96 * (u + 1))
                diag = P * i < 512 * k + width
                last = pe.matmul(ps[0:rows(i), bank(use), 0:width], q1[g][0:100, j, P * i:P * i + rows(i)],
                                 k1[g][0:100, j, 512 * k:512 * k + width], start=True, stop=not diag)
                if diag:
                    o = P * i - 512 * k
                    last = pe.matmul(ps[0:rows(i), bank(use), o:o + rows(i)], identb[:, 0:rows(i)],
                                     mask_qk[:, 0:rows(i)], start=False, stop=True)
                last.then_inc(projected, 1)

            def score(u, g, n):
                ch, j, lo, width = TILES[n]
                if n == 0:
                    pe.wait_ge(m_in, 32 * (u + 1))
                    pe.wait_ge(second_in, 112 * (u + 1))
                for half in range(2):
                    settle(pe)
                    pe.wait_ge(probs, 2 * NTL * u + 2 * n + half + 1)
                    for hd in range(2 * half, 2 * half + 2):
                        r = rows(j)
                        cut = lo < P * j + r
                        pe.matmul(ps[0:r, hd, 0:width], k1[g][0:102, hd, P * j:P * j + r], q1[g][0:102, hd, lo:lo + width],
                                  start=True, stop=False)
                        last = pe.matmul(ps[0:r, hd, 0:width], k2[g][:, hd, P * j:P * j + r], q2[g][:, hd, lo:lo + width],
                                         start=False, stop=not cut)
                        if cut:
                            wd = min(P * j + r, lo + width) - lo
                            last = pe.matmul(ps[0:r, hd, 0:wd], identb[:, 0:r], mask_kq[:, lo - P * j:lo - P * j + wd],
                                             start=False, stop=True)
                    last.then_inc(scores, 1)
                if n == NTL - 1:
                    pass

            def weigh(u, g, n):
                ch, j, lo, width = TILES[n]
                pe.wait_ge(probs, 2 * NTL * u + 2 * n + 2 + 2)
                if j == 0:
                    pe.wait_ge(normed, NCH * u + ch + 1)
                    if g == 0 and ch == 0:
                        pe.wait_ge(out_kept, out_base[0] + 1)
                settle(pe)
                r, o = rows(j), lo - CH * ch
                stop = n in LAST_TILE
                for hd in range(GH):
                    pe.matmul(ps[HD * hd:HD * hd + HD, 4, o:o + width], v[g][0:r, P * j + HD * hd:P * j + HD * hd + HD],
                              prob[n % 2][0:r, hd, 0:width], start=(j == 0), stop=stop, skip_group_check=True)
                for hd in range(GH):
                    last = pe.matmul(ps[HD * hd:HD * hd + HD, 5, o:o + width], ones[0:r, :],
                                     prob[n % 2][0:r, hd, 0:width], start=(j == 0), stop=stop, skip_group_check=True)
                last.then_inc(weighed, 1)

            out_base, batch_base = [None], [None]

            def slot(u, g, b, project_next, maxima_next):
                out_base[0], batch_base[0] = NCH * b, b + 2
                use, acts = 0, NPJ if project_next else 0

                def before():
                    if use >= 2 and use - 2 < acts:
                        pe.wait_ge(taken_act, NPJ * (u + 2) + use - 1)
                    elif use >= 2:
                        pe.wait_ge(taken_dve, NM * (u + 1) + use - 1 - acts)
                    else:
                        pe.wait_ge(taken_dve, NM * (u + 1) + use - 1)

                for n in range(NTL + 1):
                    if n < NTL:
                        score(u, g, n)
                    if project_next and n < 3:
                        for i in range(3):
                            before()
                            project(u + 2, g, 3 * n + i, FIRST + use)
                            use += 1
                    if maxima_next and SLOT0 <= n <= SLOT0 + NM // PER_SLOT:
                        for i in range(PER_SLOT * (n - SLOT0), min(PER_SLOT * (n - SLOT0 + 1), NM)):
                            before()
                            maxima(u + 1, 1 - g, i, FIRST + use)
                            use += 1
                    if n >= 1:
                        weigh(u, g, n - 1)
                if g == 1:
                    for ch in range(NCH):
                        pe.wait_ge(normed, NCH * (u + 1) + 1)
                        if ch == 2:
                            pe.wait_ge(out_kept, NCH * b + 1 + 1)
                        for k in range(2):
                            last = pe.matmul(ps[0:D, 4 + ch % 2, 0:CH], wo[k], oT[k][:, CH * ch:CH * ch + CH],
                                             start=(k == 0), stop=(k == 1))
                        last.then_inc(out_made, 1)

            for n in range(FIRST):
                if n >= 2:
                    if n - 2 < 2 * NPJ:
                        pe.wait_ge(taken_act, n - 1)
                    else:
                        pe.wait_ge(taken_dve, n - 1 - 2 * NPJ)
                if n < 2 * NPJ:
                    project(n // NPJ, n // NPJ, n % NPJ, n)
                else:
                    maxima(0, 0, n - 2 * NPJ, n)
            with pe.Fori(0, B - 1) as b:
                slot(2 * b, 0, b, True, True)
                slot(2 * b + 1, 1, b, True, True)
            slot(UNITS - 2, 0, B - 1, False, True)
            slot(UNITS - 1, 1, B - 1, False, False)

        @block.scalar
        def _(act):
            act.sem_inc(probs, 2)
            act.sem_inc(out_kept, 1)
            act.wait_ge(set_up, 3)
            act.wait_ge(loaded, 16 * 12)

            def take(u, n, use, count):
                act.wait_ge(projected, count + 1)
                if n == 0 or n == 3:
                    if not (isinstance(u, int) and u == 0):
                        act.wait_ge(split, 8 * u - 8 + (4 if n == 0 else 8))
                if n == 6 and not (isinstance(u, int) and u == 0):
                    act.wait_ge(second_in, 112 * u)
                if n < 6:
                    dst = qk[n // 3][:, CH * (n % 3):CH * (n % 3) + CH]
                    act.activation(dst, ps[:, bank(use), 0:CH], ACT.Copy, scale=(HD ** -0.5, 1.0)[n // 3]).then_inc(taken_act, 1)
                elif n < 8:
                    act.activation(vs[:, 3 * P * (n - 6):3 * P * (n - 5)], ps[:, bank(use), 0:3 * P], ACT.Copy).then_inc(taken_act, 1)
                else:
                    act.activation(vs[:, 6 * P:8 * P], ps[:, bank(use), 0:2 * P], ACT.Copy)
                    act.activation(vs[0:rows(8), 8 * P:9 * P], ps[0:rows(8), bank(use), 2 * P:3 * P], ACT.Copy).then_inc(taken_act, 1)

            def slot(u, g, b, project_next):
                for n in range(NTL):
                    ch, j, lo, width = TILES[n]
                    r = rows(j)
                    act.wait_ge(weighed, NTL * u + n + 1)
                    for half in range(2):
                        act.wait_ge(scores, 2 * NTL * u + 2 * n + half + 1)
                        act.activation(prob[n % 2][0:r, 2 * half:2 * half + 2, 0:width], ps[0:r, 2 * half:2 * half + 2, 0:width],
                                       ACT.Exp).then_inc(probs, 1)
                    if project_next and n < 3:
                        for i in range(3):
                            take(u + 2, 3 * n + i, FIRST + 3 * n + i, FIRST + (NPJ + NM) * u + 3 * n + i)
                if g == 1:
                    for ch in range(NCH):
                        act.wait_ge(out_made, NCH * b + ch + 1 + 1)
                        act.activation(dT[:, bass.ds(b * S + CH * ch, CH)] if not isinstance(b, int) else dT[:, b * S + CH * ch:b * S + CH * ch + CH],
                                       ps[0:D, 4 + ch % 2, 0:CH], ACT.Identity, bias=bo).then_inc(out_kept, 1)

            for n in range(2 * NPJ):
                take(n // NPJ, n % NPJ, n, n)
            with act.Fori(0, B - 1) as b:
                slot(2 * b, 0, b, True)
                slot(2 * b + 1, 1, b, True)
            slot(UNITS - 2, 0, B - 1, False)
            slot(UNITS - 1, 1, B - 1, False)

        @block.vector
        def _(dve):
            dve.memset(w[D:D + 1, 0:768], 0.0).then_inc(set_up, 1)
            dve.memset(mx, MASKED).then_inc(rec_made, 1)
            dve.wait_ge(rec_made, 1)
            dve.sem_inc(weighed, 2)
            dve.sem_inc(normed, 1)
            dve.sem_inc(out_made, 1)

            def take_max(u, n, use, count):
                if n == 0:
                    dve.wait_ge(maxed, u if not isinstance(u, int) or u else 0) if not (isinstance(u, int) and u == 0) else None
                if n == NM - 1:
                    dve.wait_ge(taken_dve, NM * u + NM - 1)
                    if not (isinstance(u, int) and u == 0):
                        dve.wait_ge(m_in, 32 * u)
                    dve.tensor_reduce(mc, mx.rearrange("p (b n) -> p b n", n=3), X, ALU.max).then_inc(maxed, 1)
                    dve.wait_ge(projected, count + 1)
                    src = ps[0:GH * SB, bank(use), 0:P]
                    dve.tensor_scalar(mhl[:, 0:P], src, -1.0, None, ALU.mult).then_inc(m_split, 1)
                    dve.wait_ge(m_split, 2 * u + 1)
                    dve.scalar_tensor_tensor(mhl[:, P:2 * P], src, -1.0, mhl[:, 0:P], ALU.mult, ALU.subtract).then_inc(m_split, 1)
                    dve.wait_ge(m_split, 2 * u + 2)
                    dve.sem_inc(taken_dve, 1)
                    return
                j, i, k, width = PIECES[n]
                dve.wait_ge(projected, count + 1)
                at = 3 * (SB * j + i) + k
                dve.reduce_max(mx[0:rows(i), at:at + 1], ps[0:rows(i), bank(use), 0:width], X).then_inc(taken_dve, 1)

            def norm_chunk(u, g, ch, b):
                dve.wait_ge(weighed, NTL * u + LAST_TILE[ch] + 1 + 2)
                dve.wait_ge(normed, NCH * u + ch + 1)
                dve.reciprocal(rec, ps[:, 5, 0:CH]).then_inc(rec_made, 1)
                dve.wait_ge(rec_made, NCH * u + ch + 1 + 1)
                if ch == 0 and g == 0:
                    dve.wait_ge(out_made, NCH * b + 1)
                dve.tensor_tensor(oT[g][:, CH * ch:CH * ch + CH], ps[:, 4, 0:CH], rec, ALU.mult).then_inc(normed, 1)

            def slot(u, g, b, acts, maxima_next):
                use = acts
                for n in range(NTL):
                    if n - 1 in (LAST_TILE[0] , LAST_TILE[1]):
                        pass
                    if n == LAST_TILE[0] + 2:
                        norm_chunk(u, g, 0, b)
                    if n == LAST_TILE[1] + 2:
                        norm_chunk(u, g, 1, b)
                    if maxima_next and SLOT0 <= n <= SLOT0 + NM // PER_SLOT:
                        for i in range(PER_SLOT * (n - SLOT0), min(PER_SLOT * (n - SLOT0 + 1), NM)):
                            take_max(u + 1, i, FIRST + use, FIRST + (NPJ + NM) * u + use)
                            use += 1
                norm_chunk(u, g, 2, b)

            for n in range(NM):
                take_max(0, n, 2 * NPJ + n, 2 * NPJ + n)
            with dve.Fori(0, B - 1) as b:
                slot(2 * b, 0, b, NPJ, True)
                slot(2 * b + 1, 1, b, NPJ, True)
            slot(UNITS - 2, 0, B - 1, 0, True)
            slot(UNITS - 1, 1, B - 1, 0, False)


def binary_experts(m):
    nc, a, c, sem, ps, dT, xT, xh3 = (m[k] for k in ("nc", "a", "c", "sem", "ps", "dT", "xT", "xh3"))
    ar = Arena(m["arena"])
    identb = m["identb"]
    E, IN, OUT = 8, D, D
    NQ, NG = IN * E // P, IN // 4
    NP = NG * 2
    aT = ar.take(P, NQ * N, BF16).rearrange("p (q t) -> p q t", q=NQ)
    an = [ar.take(P, IN * E, BF16) for _ in range(2)]
    sg = ar.take(P, NT * D, BF16)
    gate = ar.take(P, NT * E, BF16)
    stack = [ar.take(96, NG * CH, BF16).rearrange("p (g t) -> p g t", g=NG) for _ in range(3)]
    wf = ar.take(96, NG * OUT)
    wsplit = [ar.take(96, NG * OUT, BF16) for _ in range(3)]
    wl = ar.take(96, NG * 2 * P, BF16)
    NS = 4
    sgn = [ar.take(P, 2 * CH, BF16).rearrange("p (n t) -> p n t", n=2) for _ in range(NS)]
    neg = ar.take(P, 2 * CH, BF16).rearrange("p (n t) -> p n t", n=2)
    pair_sum = ar.take(P, D, BF16)
    pw = ar.take(D + 1, E)
    sc = ar.take(D, 1)
    loaded, w_in, wstep, w_placed, zeroed = sem("c_loaded"), sem("c_w_in"), sem("c_wstep"), sem("c_w_placed"), sem("c_zeroed")
    logits, gates, signs, made, turned, kept = (sem("c_" + s) for s in ("logits", "gates", "signs", "made", "turned", "kept"))
    sg3 = sg.rearrange("p (k d) -> p k d", d=D)
    g3 = gate.rearrange("p (k e) -> p k e", e=E)
    wl4 = wl.rearrange("p (g f i o) -> p g f i o", g=NG, f=2, i=2)

    with nc.Block() as block:
        @block.sync
        def _(sp):
            sp.dma_start(pw[0:D], a["L0_ffn_proj_w"]).then_inc(loaded, 16)
            sp.dma_start(pw[D:D + 1], a["L0_ffn_proj_b"].rearrange("(o e) -> o e", o=1)).then_inc(loaded, 16)
            sp.dma_start(sc, a["L0_ffn_scale"].rearrange("a b o -> o (a b)")).then_inc(loaded, 16)
            sp.dma_start(pair_sum, c["pair_sum"]).then_inc(loaded, 16)
            src = a["L0_ffn_weight"].rearrange("o e (g i) d -> i e (o g) d", i=4)
            for s in range(3):
                for i in range(4):
                    at = 32 * s + E * i
                    sp.dma_start(wf[at:at + E].rearrange("p (g d) -> p g d", g=NG), src[i]).then_inc(w_in, 16)
            sp.wait_ge(wstep, 5)
            sp.wait_ge(zeroed, 1)
            for s in range(3):
                for i in range(4):
                    at = 32 * s + E * i
                    sp.dma_start(wl4[at:at + E, :, i // 2, i % 2, :],
                                 wsplit[s][at:at + E].rearrange("p (g o) -> p g o", g=NG)).then_inc(w_placed, 16)
            sp.wait_ge(w_placed, 192)

        @block.gpsimd
        def _(pool):
            pool.memset(wl, 0.0).then_inc(zeroed, 1)
            hi, mid, lo = wsplit
            pool.wait_ge(w_in, 192)
            pool.tensor_copy(hi, wf).then_inc(wstep, 1)
            pool.wait_ge(wstep, 1)
            pool.tensor_tensor(wf, wf, hi, ALU.subtract).then_inc(wstep, 1)
            pool.wait_ge(wstep, 2)
            pool.tensor_copy(mid, wf).then_inc(wstep, 1)
            pool.wait_ge(wstep, 3)
            pool.tensor_tensor(wf, wf, mid, ALU.subtract).then_inc(wstep, 1)
            pool.wait_ge(wstep, 4)
            pool.tensor_copy(lo, wf).then_inc(wstep, 1)

        @block.tensor
        def _(pe):
            pe.wait_ge(loaded, 64)
            for t in range(NT):
                last = pe.matmul(ps[:, 0, E * t:E * t + E], xT[:, P * t:P * t + P], pw, start=True, stop=True)
            last.then_inc(logits, 1)
            for t in range(NT):
                b = 1 + t % 3
                pe.wait_ge(made, t + 1)
                if t >= 3:
                    pe.wait_ge(kept, t - 2)
                pb = ps[:, b, :].bitcast(BF16)
                for q in range(NQ):
                    last = pe.transpose(pb[:, P * q:P * q + P], an[t % 2][:, P * q:P * q + P], identb[:])
                last.then_inc(turned, 1)

        @block.scalar
        def _(act):
            act.activation(sg3, xh3, ACT.Sign).then_inc(signs, 1)
            for t in range(NT):
                act.wait_ge(turned, t + 1)
                pb = ps[:, 1 + t % 3, :].bitcast(BF16)
                act.activation(aT[:, :, P * t:P * t + P], pb[:, 0:NQ * P].rearrange("p (q t) -> p q t", q=NQ),
                               ACT.Copy).then_inc(kept, 1)

        @block.vector
        def _(dve):
            dve.wait_ge(logits, 1)
            dve.tensor_scalar(gate, ps[:, 0, 0:NT * E], 0.0, None, ALU.is_gt).then_inc(gates, 1)
            dve.wait_ge(gates, 1)
            dve.wait_ge(signs, 1)
            for t in range(NT):
                if t >= 2:
                    dve.wait_ge(turned, t - 1)
                dve.tensor_tensor(an[t % 2].rearrange("p (i e) -> p i e", e=E),
                                  sg3[:, t, :].rearrange("p (i o) -> p i o", o=1).broadcast_to([P, IN, E]),
                                  g3[:, t, :].rearrange("p (o e) -> p o e", o=1).broadcast_to([P, IN, E]),
                                  ALU.mult).then_inc(made, 1)

    stacked, mixed = [sem(f"c_stacked_{q}") for q in range(3)], sem("c_mixed")
    sign_act, sign_dve, neg_made, summed, sum_made, sum_kept = (
        sem("c_" + s) for s in ("sign_act", "sign_dve", "neg_made", "summed", "sum_made", "sum_kept"))
    NCK, PR = N // CH, NP // 2
    Q = 3
    on_dve = [n % 3 == 2 for n in range(PR)]
    ND = sum(on_dve)
    NA = PR - ND
    sum_bank = (6, 7, 6)

    def ahead(n):
        return n - sum(on_dve[:n]), sum(on_dve[:n])

    def wait_signed(eng, ck, n):
        if on_dve[n]:
            eng.wait_ge(sign_dve, ND * ck + ahead(n)[1] + 1 + ND)
        else:
            eng.wait_ge(sign_act, NA * ck + ahead(n)[0] + 1 + NA)

    def wait_free(eng, ck, n):
        eng.wait_ge(summed, PR * ck + n - NS + 1 + PR)

    with nc.Block() as block:
        @block.sync
        def _(sp):
            with sp.Fori(0, NCK // Q) as k:
                for q in range(Q):
                    sp.wait_ge(mixed, PR * (Q * k + q) + PR)
                    settle(sp)
                    for s in range(3):
                        for r in range(4):
                            sp.dma_start(stack[q].rearrange("p (q r) t -> p q r t", r=4)[32 * s:32 * s + 32, :, r, :],
                                         aT[32 * r:32 * r + 32, :, bass.ds((Q * k + q) * CH, CH)]).then_inc(stacked[q], 16)

        @block.tensor
        def _(pe):
            pe.sem_inc(mixed, Q * PR)

            def mix(k, m_):
                q, n = m_ // PR, m_ % PR
                ck = Q * k + q
                if n == 0:
                    pe.wait_ge(stacked[q], 192 * (k + 1))
                wait_signed(pe, ck if n >= 3 else ck - 1, (n - 3) % PR)
                for f in range(2):
                    last = pe.matmul(ps[:, 2 * (m_ % 3) + f, 0:CH], wl[:, P * (2 * n + f):P * (2 * n + f) + P],
                                     stack[q][:, n, :], start=True, stop=True)
                last.then_inc(mixed, 1)

            def add(k, m_):
                q, n = m_ // PR, m_ % PR
                ck = Q * k + q
                if n == 0:
                    pe.wait_ge(sum_kept, ck + (2, 0, 1)[q])
                wait_signed(pe, ck, n)
                settle(pe)
                for f in range(2):
                    last = pe.matmul(ps[0:D, sum_bank[q], 0:CH], pair_sum, sgn[m_ % NS][:, f, :],
                                     start=(n == 0 and f == 0), stop=(n == PR - 1 and f == 1))
                last.then_inc(summed, 1)

            with pe.Fori(0, NCK // Q) as k:
                mix(k, 0)
                mix(k, 1)
                for m_ in range(Q * PR):
                    if m_ + 2 < Q * PR:
                        mix(k, m_ + 2)
                    add(k, m_)

        @block.scalar
        def _(act):
            act.sem_inc(sign_act, NA)
            act.sem_inc(summed, PR)
            act.sem_inc(sum_kept, 2)
            with act.Fori(0, NCK // Q) as k:
                for m_ in range(Q * PR):
                    q, n = m_ // PR, m_ % PR
                    if not on_dve[n]:
                        wait_free(act, Q * k + q, n)
                        act.wait_ge(mixed, PR * (Q * k + q) + n + 1 + Q * PR)
                        b0 = 2 * (m_ % 3)
                        act.activation(sgn[m_ % NS], ps[:, b0:b0 + 2, 0:CH], ACT.Sign).then_inc(sign_act, 1)

        @block.vector
        def _(dve):
            dve.sem_inc(sign_dve, ND)

            def keep(k, q):
                ck = Q * k + q
                dve.wait_ge(summed, PR * ck + PR + PR)
                dve.tensor_scalar(dT[:, bass.ds(ck * CH, CH)], ps[0:D, sum_bank[q], 0:CH], sc, None,
                                  ALU.mult).then_inc(sum_kept, 1)

            with dve.Fori(0, NCK // Q) as k:
                for m_ in range(Q * PR):
                    q, n = m_ // PR, m_ % PR
                    if on_dve[n]:
                        at = ND * (Q * k + q) + ahead(n)[1]
                        b0 = 2 * (m_ % 3)
                        src = ps[:, b0:b0 + 2, 0:CH]
                        dve.wait_ge(sign_dve, at + ND)
                        dve.wait_ge(mixed, PR * (Q * k + q) + n + 1 + Q * PR)
                        dve.tensor_scalar(neg, src, 0.0, None, ALU.is_lt).then_inc(neg_made, 1)
                        wait_free(dve, Q * k + q, n)
                        dve.wait_ge(neg_made, at + 1)
                        dve.scalar_tensor_tensor(sgn[m_ % NS], src, 0.0, neg, ALU.is_gt, ALU.subtract).then_inc(sign_dve, 1)
                    if n == 3 and q >= 1:
                        keep(k, q - 1)
                keep(k, Q - 1)


def retention(m):
    nc, a, c, sem, ps, dT, xT = (m[k] for k in ("nc", "a", "c", "sem", "ps", "dT", "xT"))
    ar = Arena(m["arena"])
    xb = [ar.take(D + 1, S) for _ in range(2)]
    q, k = [ar.take(D + 1, S) for _ in range(2)], [ar.take(D + 1, S) for _ in range(2)]
    v = [ar.take(P, SB * D) for _ in range(2)]
    decay = ar.take(P, S)
    NP = 4
    p = [ar.take(P, CH) for _ in range(NP)]
    w = ar.take(D + 1, 3 * D)
    wq, wk, wv = (w[:, D * i:D * i + D] for i in range(3))
    loaded, set_up, xb_in = sem("d_loaded"), sem("d_set_up"), sem("d_xb_in")
    prep, prep_kept, scores, decayed, summed, kept = (
        sem("d_" + s) for s in ("prep", "prep_kept", "scores", "decayed", "summed", "kept"))
    NTL = len(TILES)
    NPR = 8
    LAST_TILE = [max(n for n in range(NTL) if TILES[n][0] == ch) for ch in range(NCH)]

    with nc.Block() as block:
        @block.sync
        def _(sp):
            for dst, name in ((wq, "Wq"), (wk, "Wk"), (wv, "Wv")):
                sp.dma_start(dst[0:D], a["L1_attn_" + name]).then_inc(loaded, 16)
            sp.dma_start(decay, c["decay"]).then_inc(loaded, 16)

        @block.gpsimd
        def _(pool):
            for n in range(2):
                pool.tensor_copy(xb[n], xT[:, S * n:S * n + S]).then_inc(xb_in, 1)
            with pool.Fori(0, B // 2 - 1) as pair:
                for n in range(2):
                    b = 2 * pair
                    pool.wait_ge(prep, NPR * (b + n + 1))
                    settle(pool)
                    pool.tensor_copy(xb[n], xT[:, bass.ds((b + n + 2) * S, S)]).then_inc(xb_in, 1)

        @block.tensor
        def _(pe):
            pe.wait_ge(loaded, 64)
            pe.wait_ge(set_up, 5)

            def prepare(b, par, n):
                if n == 0:
                    pe.wait_ge(xb_in, b + 1)
                pe.wait_ge(prep_kept, NPR * b + n + 1)
                settle(pe)
                if n < 6:
                    ch = n % 3
                    last = pe.matmul(ps[0:D, 6 + n % 2, 0:CH], (wq, wk)[n // 3], xb[par][:, CH * ch:CH * ch + CH],
                                     start=True, stop=True)
                else:
                    for j in (range(8), range(8, SB))[n - 6]:
                        last = pe.matmul(ps[0:rows(j), 6 + n % 2, D * (j % 8):D * (j % 8) + D],
                                         xb[par][:, P * j:P * j + rows(j)], wv, start=True, stop=True)
                last.then_inc(prep, 1)

            def score(b, par, n):
                ch, j, lo, width = TILES[n]
                if n == 0:
                    pe.wait_ge(prep_kept, NPR * (b + 1) + 2)
                pe.wait_ge(decayed, NTL * b + n + 1)
                r = rows(j)
                pe.matmul(ps[0:r, (NTL * par + n) % 4, 0:width], k[par][:, P * j:P * j + r], q[par][:, lo:lo + width],
                          start=True, stop=True).then_inc(scores, 1)

            def weigh(b, par, n):
                ch, j, lo, width = TILES[n]
                pe.wait_ge(decayed, NTL * b + n + 1 + 4)
                if j == 0:
                    pe.wait_ge(kept, NCH * b + ch + 1)
                settle(pe)
                r, o = rows(j), lo - CH * ch
                pe.matmul(ps[0:D, 4 + (NCH * par + ch) % 2, o:o + width], v[par][0:r, D * j:D * j + D],
                          p[(NTL * par + n) % NP][0:r, 0:width], start=(j == 0), stop=n in LAST_TILE,
                          skip_group_check=True).then_inc(summed, 1)

            for n in range(NPR):
                prepare(0, 0, n)

            def batch(b, par, more):
                score(b, par, 0)
                score(b, par, 1)
                for n in range(NTL):
                    if n + 2 < NTL:
                        score(b, par, n + 2)
                    if more and 4 <= n < 4 + NPR:
                        prepare(b + 1, 1 - par, n - 4)
                    weigh(b, par, n)

            with pe.Fori(0, B // 2 - 1) as pair:
                batch(2 * pair, 0, True)
                batch(2 * pair + 1, 1, True)
            batch(B - 2, 0, True)
            batch(B - 1, 1, False)

        @block.scalar
        def _(act):
            act.sem_inc(prep_kept, 2)
            act.sem_inc(kept, 2)

            def prepare(b, par, n):
                act.wait_ge(prep, NPR * b + n + 1)
                src = ps[:, 6 + n % 2, :]
                if n < 6:
                    ch = n % 3
                    act.activation((q, k)[n // 3][par][0:D, CH * ch:CH * ch + CH], src[0:D, 0:CH], ACT.Copy).then_inc(prep_kept, 1)
                elif n == 6:
                    act.activation(v[par][:, 0:8 * D], src[:, 0:8 * D], ACT.Copy).then_inc(prep_kept, 1)
                else:
                    act.activation(v[par][0:rows(8), 8 * D:9 * D], src[0:rows(8), 0:D], ACT.Copy).then_inc(prep_kept, 1)

            def keep(b, par, ch):
                act.wait_ge(summed, NTL * b + LAST_TILE[ch] + 1 + 4)
                at = b * S + CH * ch
                dst = dT[:, at:at + CH] if isinstance(b, int) else dT[:, bass.ds(at, CH)]
                act.activation(dst, ps[0:D, 4 + (NCH * par + ch) % 2, 0:CH], ACT.Copy).then_inc(kept, 1)

            def batch(b, par, more):
                for n in range(NTL + 2):
                    if more and 4 <= n < 4 + NPR:
                        prepare(b + 1, 1 - par, n - 4)
                    for ch in range(NCH):
                        if n == LAST_TILE[ch] + 2:
                            keep(b, par, ch)

            for n in range(NPR):
                prepare(0, 0, n)
            with act.Fori(0, B // 2 - 1) as pair:
                batch(2 * pair, 0, True)
                batch(2 * pair + 1, 1, True)
            batch(B - 2, 0, True)
            batch(B - 1, 1, False)

        @block.vector
        def _(dve):
            dve.memset(w[D:D + 1, :], 0.0).then_inc(set_up, 1)
            for t in (*q, *k):
                dve.memset(t[D:D + 1, :], 0.0).then_inc(set_up, 1)
            dve.sem_inc(decayed, 4)
            dve.sem_inc(summed, 4)
            dve.wait_ge(loaded, 64)

            def batch(b, par):
                for n in range(NTL):
                    ch, j, lo, width = TILES[n]
                    r = rows(j)
                    i = (NTL * par + n) % 4
                    dve.wait_ge(scores, NTL * b + n + 1)
                    dve.wait_ge(summed, NTL * b + n + 1)
                    dve.tensor_tensor(p[i][0:r, 0:width], ps[0:r, i, 0:width], decay[0:r, lo - P * j:lo - P * j + width],
                                      ALU.mult).then_inc(decayed, 1)

            with dve.Fori(0, B // 2) as pair:
                batch(2 * pair, 0)
                batch(2 * pair + 1, 1)


N_EDGES = 262144
EC = N_EDGES // P
FE = 4
HE = FE * FE
CHN = HE + FE
GC = 16
CAP = 160
LO, HI = 64, N // 64
CB = 128
NONE = -1e9


def load_edges(m):
    nc, a, sem, ps = (m[k] for k in ("nc", "a", "sem", "ps"))
    ar = Arena(m["arena"])
    keys, picked, cnt = m["keys"], m["picked"], m["cnt"]
    src, dst, shi, dhi = (ar.take(P, EC, I32) for _ in range(4))
    near, tmp = ar.take(P, EC), ar.take(P, EC)
    lo, hi = ar.take(P, EC, BF16), ar.take(P, EC, BF16)
    onehot = [ar.take(P, (LO + HI) * CB, BF16).rearrange("p (v e) -> p v e", e=CB) for _ in range(2)]
    cnt64 = ar.take(LO, HI)
    m8 = ar.take(P, 8)
    zero = ar.take(P, LO + HI, BF16)
    zeroed = sem("e_zeroed")
    edges_in, step, made, counted, cnt_kept, cnt_in = (sem("e_" + s) for s in ("edges_in", "step", "made", "counted", "cnt_kept", "cnt_in"))
    NB = EC // CB

    with nc.Block() as block:
        @block.sync
        def _(sp):
            e = a["L1_ffn_edge_index"].rearrange("s (p e) -> s p e", p=P)
            sp.dma_start(src, e[0]).then_inc(edges_in, 16)
            sp.dma_start(dst, e[1]).then_inc(edges_in, 16)
            sp.wait_ge(cnt_kept, 1)
            for half in range(2):
                sp.dma_start(cnt[LO * half:LO * half + LO, :],
                             cnt64[:, NT * half:NT * half + NT]).then_inc(cnt_in, 16)
            sp.wait_ge(cnt_in, 32)

        @block.vector
        def _(dve):
            n = 0

            def chain(instruction):
                nonlocal n
                n += 1
                instruction.then_inc(step, 1)
                dve.wait_ge(step, n)

            dve.memset(zero, 0.0).then_inc(zeroed, 1)
            dve.wait_ge(edges_in, 32)
            chain(dve.tensor_scalar(shi, src, 7, None, ALU.arith_shift_right))
            chain(dve.tensor_scalar(dhi, dst, 7, None, ALU.arith_shift_right))
            chain(dve.tensor_scalar(keys, dhi, float(32 << 14), float(-(544 << 14)), ALU.mult, ALU.add))
            chain(dve.scalar_tensor_tensor(keys, shi, float((1 << 14) - P), keys, ALU.mult, ALU.add))
            chain(dve.scalar_tensor_tensor(keys, dst, float(P), keys, ALU.mult, ALU.add))
            chain(dve.tensor_tensor(keys, src, keys, ALU.add))
            chain(dve.tensor_scalar(tmp, dst, float(N), None, ALU.is_lt))
            chain(dve.scalar_tensor_tensor(near, src, float(N - 1), tmp, ALU.is_lt, ALU.mult))
            chain(dve.tensor_tensor(keys, keys, near, ALU.mult))
            chain(dve.tensor_scalar(tmp, near, -NONE, NONE, ALU.mult, ALU.add))
            chain(dve.tensor_tensor(keys, keys, tmp, ALU.add))
            chain(dve.tensor_scalar(dhi, dst, 6, None, ALU.arith_shift_right))
            chain(dve.tensor_scalar(tmp, src, float(N - 1), 100.0, ALU.is_lt, ALU.mult))
            chain(dve.tensor_tensor(hi, dhi, tmp, ALU.max))
            chain(dve.tensor_scalar(dhi, dst, LO - 1, None, ALU.bitwise_and))
            chain(dve.tensor_copy(lo, dhi))
            for r in range(CAP // 8):
                chain(dve.max(m8, keys))
                chain(dve.tensor_copy(picked[:, 8 * r:8 * r + 8], m8))
                chain(dve.match_replace(out=keys, in_to_replace=m8, in_values=keys, imm_value=NONE))
            dve.sem_inc(counted, 2)
            with dve.Fori(0, NB // 2) as pair:
                for b in range(2):
                    dve.wait_ge(counted, 2 * pair + b + 1)
                    for v in range(LO + HI):
                        part, value = (lo, v) if v < LO else (hi, v - LO)
                        last = dve.tensor_scalar(onehot[b][:, v, :], part[:, bass.ds((2 * pair + b) * CB, CB)],
                                                 float(value), None, ALU.is_equal)
                    last.then_inc(made, 1)
            dve.wait_ge(counted, NB + 2)
            dve.tensor_copy(cnt64.rearrange("p (f k) -> p k f", f=2),
                            ps[0:LO, 7, 0:HI].rearrange("p (k f) -> p k f", f=2)).then_inc(cnt_kept, 1)

        @block.tensor
        def _(pe):
            pe.wait_ge(edges_in, 32)
            pe.wait_ge(zeroed, 1)
            pe.matmul(ps[0:LO, 7, 0:HI], zero[:, 0:LO], zero[:, LO:], start=True, stop=False, skip_group_check=True)
            with pe.Fori(0, NB // 2) as pair:
                for b in range(2):
                    pe.wait_ge(made, 2 * pair + b + 1)
                    settle(pe)
                    for e in range(CB):
                        last = pe.matmul(ps[0:LO, 7, 0:HI], onehot[b][:, 0:LO, e], onehot[b][:, LO:, e],
                                         start=False, stop=False, skip_group_check=True)
                    last.then_inc(counted, 1)


def graph_experts(m):
    nc, a, sem, ps, xT, ident, h3 = (m[k] for k in ("nc", "a", "sem", "ps", "xT", "ident", "h3"))
    ctx = m["ctx"]
    full = Arena(m["arena"])
    m["keys"], m["picked"], m["cnt"] = full.take(P, EC), full.take(P, CAP), full.take(P, NT)
    base = full.at
    m_edges = dict(m, arena=m["arena"][:, base:])
    load_edges(m_edges)
    keys, picked, cnt = m["keys"], m["picked"], m["cnt"]

    def k3(ap, **kw):
        return ap.rearrange("p (k c) -> p k c", **kw)

    ar = full
    outE = ar.take(P, NT * FE * D)
    nodes, dtab = k3(ar.take(P, NT * CHN), k=NT), k3(ar.take(P, NT * FE), k=NT)
    prod = k3(ar.take(P, NT * CHN), k=NT)
    own = k3(ar.take(P, NT * CHN), k=NT)
    bound, t1, t2 = (k3(ar.take(P, NT * FE), k=NT) for _ in range(3))
    lastrow, G4, G4p = ar.take(P, CHN), ar.take(P, FE), ar.take(P, FE)
    att_s, att_d, bg, gamma, beta = (ar.take(P, HE) for _ in range(5))
    b2 = ar.take(P, FE * D)
    wg = ar.take(D + 1, HE)
    w1 = ar.take(D + 1, FE * P)
    w2 = ar.take(P, FE * D)
    loaded, gat, step, tab_out, last_in, gmax, gall, expd = (
        sem("f_" + s) for s in ("loaded", "gat", "step", "tab_out", "last_in", "gmax", "gall", "expd"))
    tab = nc.dram_tensor("node_table", [N, CHN], F32, kind="Internal").ap()
    dtd = nc.dram_tensor("dst_table", [N, FE], F32, kind="Internal").ap()
    bank2 = [(k // 32, k % 32) for k in range(NT)]

    def vec(name, n):
        src = a["L1_ffn_" + name]
        if len(src.shape) == 2:
            src = src.rearrange("h e -> (h e)")
        return src.rearrange("(o d) -> o d", o=1).broadcast_to([P, n])

    with nc.Block() as block:
        @block.sync
        def _(sp):
            sp.dma_start(wg[0:D], a["L1_ffn_W_gat"]).then_inc(loaded, 16)
            for dst, name in ((att_s, "att_src"), (att_d, "att_dst"), (bg, "b_gat"), (gamma, "ln_gamma"), (beta, "ln_beta")):
                sp.dma_start(dst, vec(name, HE)).then_inc(loaded, 16)
            sp.dma_start(b2, vec("b2", FE * D)).then_inc(loaded, 16)
            sp.dma_start(w1[0:D].rearrange("p (e f) -> p e f", e=FE), a["L1_ffn_W1"].rearrange("e d f -> d e f")).then_inc(loaded, 16)
            sp.dma_start(w1[D:D + 1], a["L1_ffn_b1"].rearrange("e f -> (e f)").rearrange("(o d) -> o d", o=1)).then_inc(loaded, 16)
            sp.dma_start(w2.rearrange("p (e d) -> p e d", e=FE), a["L1_ffn_W2"].rearrange("e f d -> f e d")).then_inc(loaded, 16)
            sp.wait_ge(step, 7)
            sp.dma_start(tab.rearrange("(k p) c -> p k c", p=P), nodes).then_inc(tab_out, 16)
            sp.dma_start(dtd.rearrange("(k p) c -> p k c", p=P), dtab).then_inc(tab_out, 16)
            sp.wait_ge(tab_out, 32)
            sp.dma_start(lastrow, tab[N - 1:N, :].broadcast_to([P, CHN])).then_inc(last_in, 16)

        @block.tensor
        def _(pe):
            pe.wait_ge(loaded, 160)
            pe.wait_ge(step, 1)
            for k, (bk, i) in enumerate(bank2):
                last = pe.matmul(ps[:, bk, HE * i:HE * i + HE], xT[:, P * k:P * k + P], wg, start=True, stop=True)
            last.then_inc(gat, 1)

        @block.gpsimd
        def _(pool):
            pool.wait_ge(gmax, 1)
            pool.partition_all_reduce(G4, G4p, P, bass.bass_isa.ReduceOp.max).then_inc(gall, 1)

        @block.scalar
        def _(act):
            act.wait_ge(step, 15)
            act.activation(t1, t1, ACT.Exp).then_inc(expd, 1)
            act.activation(t2, t2, ACT.Exp).then_inc(expd, 1)

        @block.vector
        def _(dve):
            n = 0

            def chain(instruction):
                nonlocal n
                n += 1
                instruction.then_inc(step, 1)
                dve.wait_ge(step, n)

            def leaky(x):
                chain(dve.scalar_tensor_tensor(x, x, 0.2, x, ALU.mult, ALU.max))

            def per_head(ap):
                return ap.rearrange("p (o c) -> p o c", o=1).broadcast_to([P, NT, ap.shape[1]])

            def split(ap):
                return ap.rearrange("p k (h e) -> p k h e", e=FE)

            def spread(w):
                return w.rearrange("p k (h o) -> p k h o", o=1).broadcast_to([P, NT, FE, FE])

            chain(dve.memset(wg[D:D + 1], 0.0))
            dve.wait_ge(loaded, 160)
            dve.wait_ge(gat, 1)
            h16 = nodes[:, :, 0:HE]
            chain(dve.tensor_copy(nodes[:, 32:33, 0:HE], k3(ps[:, 1, 0:HE], k=1)))
            chain(dve.tensor_copy(nodes[:, 0:32, 0:HE], k3(ps[:, 0, :], k=32)))
            pr = prod[:, :, 0:HE]
            chain(dve.tensor_tensor(pr, h16, per_head(att_s), ALU.mult))
            chain(dve.tensor_reduce(nodes[:, :, HE:], split(pr), X, ALU.add))
            chain(dve.tensor_tensor(pr, h16, per_head(att_d), ALU.mult))
            chain(dve.tensor_reduce(dtab, split(pr), X, ALU.add))
            dve.tensor_reduce(G4p, nodes[:, :, HE:].rearrange("p k h -> p h k"), X, ALU.max).then_inc(gmax, 1)
            dve.wait_ge(gall, 1)
            chain(dve.tensor_tensor(bound, dtab, per_head(G4), ALU.add))
            leaky(bound)
            chain(dve.tensor_tensor(t1, nodes[:, :, HE:], dtab, ALU.add))
            leaky(t1)
            chain(dve.tensor_tensor(t1, t1, bound, ALU.subtract))
            dve.wait_ge(last_in, 16)
            chain(dve.tensor_tensor(t2, dtab, per_head(lastrow[:, HE:]), ALU.add))
            leaky(t2)
            chain(dve.tensor_tensor(t2, t2, bound, ALU.subtract))
            dve.wait_ge(expd, 2)
            chain(dve.tensor_tensor(t2, t2, cnt.rearrange("p (k o) -> p k o", o=1).broadcast_to([P, NT, FE]), ALU.mult))
            chain(dve.tensor_tensor(own[:, :, HE:], t1, t2, ALU.add))
            chain(dve.tensor_tensor(split(own[:, :, 0:HE]), split(h16), spread(t1), ALU.mult))
            last4 = per_head(lastrow[:, 0:HE]).rearrange("p k (h e) -> p k h e", e=FE)
            chain(dve.tensor_tensor(split(prod[:, :, 0:HE]), last4, spread(t2), ALU.mult))
            chain(dve.tensor_tensor(own[:, :, 0:HE], own[:, :, 0:HE], prod[:, :, 0:HE], ALU.add))

    gathered_columns(m, ar, tab, dtd, G4, outE, w1, w2)

    pstep, pgate, fin, outd = sem("g_step"), sem("g_gate"), sem("g_fin"), sem("g_outd")
    sc = k3(ar.take(P, NT * FE), k=NT)
    rank = k3(ar.take(P, NT * FE), k=NT)
    one = [k3(ar.take(P, NT), k=NT) for _ in range(2)]
    ex = k3(ar.take(P, NT * FE), k=NT)
    o4 = outE.rearrange("p (k e d) -> p k e d", k=NT, e=FE)
    with nc.Block() as block:
        @block.scalar
        def _(act):
            act.wait_ge(pgate, 1)
            act.activation(one[1], one[1], ACT.Sqrt).then_inc(pgate, 1)
            act.wait_ge(pgate, 3)
            act.activation(ex, sc, ACT.Exp).then_inc(pgate, 1)

        @block.vector
        def _(dve):
            n = 0

            def chain(instruction):
                nonlocal n
                n += 1
                instruction.then_inc(pstep, 1)
                dve.wait_ge(pstep, n)

            def per_row(ap, c):
                return ap.broadcast_to([P, NT, c])

            def vecs(ap):
                return ap.rearrange("p (o c) -> p o c", o=1).broadcast_to([P, NT, ap.shape[1]])

            for b0, lo in ((0, 0), (1, NT // 2 + 1)):
                hi = (NT // 2 + 1, NT)[b0]
                chain(dve.tensor_tensor(own[:, lo:hi, :], own[:, lo:hi, :],
                                        ps[:, b0, 0:(hi - lo) * CHN].rearrange("p (k c) -> p k c", c=CHN), ALU.add))
            chain(dve.reciprocal(t1, own[:, :, HE:]))
            agg = prod[:, :, 0:HE]
            split4 = agg.rearrange("p k (h e) -> p k h e", e=FE)
            chain(dve.tensor_tensor(split4, own[:, :, 0:HE].rearrange("p k (h e) -> p k h e", e=FE),
                                    t1.rearrange("p k (h o) -> p k h o", o=1).broadcast_to([P, NT, FE, FE]), ALU.mult))
            chain(dve.tensor_tensor(agg, agg, vecs(bg), ALU.add))
            chain(dve.tensor_reduce(one[0], agg, X, ALU.add))
            chain(dve.tensor_scalar(one[0], one[0], 1.0 / HE, None, ALU.mult))
            chain(dve.tensor_tensor(agg, agg, per_row(one[0], HE), ALU.subtract))
            sq = own[:, :, 0:HE]
            chain(dve.tensor_tensor(sq, agg, agg, ALU.mult))
            chain(dve.tensor_reduce(one[1], sq, X, ALU.add))
            dve.tensor_scalar(one[1], one[1], 1.0 / HE, EPS, ALU.mult, ALU.add).then_inc(pgate, 1)
            dve.wait_ge(pgate, 2)
            chain(dve.reciprocal(one[0], one[1]))
            chain(dve.tensor_tensor(agg, agg, per_row(one[0], HE), ALU.mult))
            chain(dve.tensor_tensor(agg, agg, vecs(gamma), ALU.mult))
            chain(dve.tensor_tensor(agg, agg, vecs(beta), ALU.add))
            chain(dve.tensor_reduce(sc, agg.rearrange("p k (h e) -> p k e h", e=FE), X, ALU.add))
            chain(dve.tensor_scalar(sc, sc, 1.0 / FE, None, ALU.mult))
            for e in range(FE):
                chain(dve.memset(rank[:, :, e:e + 1], float(FE - 1 - e)))
            for i in range(FE):
                for j in range(i + 1, FE):
                    chain(dve.tensor_tensor(one[0], sc[:, :, i:i + 1], sc[:, :, j:j + 1], ALU.is_ge))
                    chain(dve.tensor_tensor(rank[:, :, j:j + 1], rank[:, :, j:j + 1], one[0], ALU.add))
                    chain(dve.tensor_tensor(rank[:, :, i:i + 1], rank[:, :, i:i + 1], one[0], ALU.subtract))
            chain(dve.tensor_reduce(one[0], sc, X, ALU.max))
            dve.tensor_tensor(sc, sc, per_row(one[0], FE), ALU.subtract).then_inc(pgate, 1)
            dve.wait_ge(pgate, 4)
            chain(dve.scalar_tensor_tensor(ex, rank, 1.5, ex, ALU.is_lt, ALU.mult))
            chain(dve.tensor_reduce(one[0], ex, X, ALU.add))
            chain(dve.reciprocal(one[1], one[0]))
            chain(dve.tensor_tensor(ex, ex, per_row(one[1], FE), ALU.mult))
            flat = outE.rearrange("p (k c) -> p k c", k=NT)
            chain(dve.tensor_tensor(flat, flat, vecs(b2), ALU.add))
            for e in range(FE):
                chain(dve.tensor_tensor(o4[:, :, e, :], o4[:, :, e, :], per_row(ex[:, :, e:e + 1], D), ALU.mult))
                chain(dve.tensor_tensor(h3, h3, o4[:, :, e, :], ALU.add))
            dve.sem_inc(fin, 1)

        @block.sync
        def _(sp):
            sp.wait_ge(fin, 1)
            sp.dma_start(a["out"].rearrange("b s d -> (b s) d").rearrange("(k p) d -> p k d", p=P), h3).then_inc(outd, 16)
            sp.wait_ge(outd, 16)


def gathered_columns(m, ar, tab, dtd, G4, outE, w1, w2):
    nc, a, sem, ps, xT = (m[k] for k in ("nc", "a", "sem", "ps", "xT"))
    picked, keys = m["picked"], m["keys"]

    def k3(ap, **kw):
        return ap.rearrange("p (k c) -> p k c", **kw)

    kint, klo, srci, dsti = (ar.take(P, CAP, I32) for _ in range(4))
    dlo, dhi, ta, tb, kf = (ar.take(P, CAP) for _ in range(5))
    iota = ar.take(P, P)
    iotai = ar.take(P, P, I32)
    idxS, idxD = [ar.take(P, GC, I32) for _ in range(2)], [ar.take(P, GC, I32) for _ in range(2)]
    gS = [k3(ar.take(P, GC * CHN), k=GC) for _ in range(2)]
    gD = [k3(ar.take(P, GC * FE), k=GC) for _ in range(2)]
    ohl = [k3(ar.take(P, GC * P), k=GC) for _ in range(2)]
    ohh = k3(ar.take(P, GC * NT), k=GC)
    za, zb, wt = (k3(ar.take(P, GC * FE), k=GC) for _ in range(3))
    val = k3(ar.take(P, GC * CHN), k=GC)
    NQ = 4
    prod = [ar.take(P, NQ * NT * CHN).rearrange("p (c k f) -> p c k f", c=NQ, k=NT) for _ in range(2)]
    xc = [ar.take(D + 1, 3 * P) for _ in range(2)]
    hh = [ar.take(P, 3 * P) for _ in range(2)]
    zero = ar.take(P, 330)
    QG = GC // NQ
    SPLIT = NT // 2 + 1
    flag = ar.take(P, 1)
    flagi = ar.take(P, 1, I32)
    rest = ar.take(P, 1)

    def decode(chain, dve, width, src):
        w = slice(0, width)
        chain(dve.tensor_scalar(kf[:, w], src, float(-(544 << 14)), None, ALU.max))
        chain(dve.tensor_copy(kint[:, w], kf[:, w]))
        chain(dve.tensor_scalar(klo[:, w], kint[:, w], 7, None, ALU.arith_shift_right))
        chain(dve.tensor_scalar(klo[:, w], klo[:, w], P - 1, None, ALU.bitwise_and))
        chain(dve.tensor_copy(dlo[:, w], klo[:, w]))
        chain(dve.tensor_scalar(klo[:, w], kint[:, w], 14, None, ALU.arith_shift_right))
        chain(dve.tensor_scalar(ta[:, w], klo[:, w], 544.0, None, ALU.add))
        chain(dve.tensor_scalar(dhi[:, w], ta[:, w], float(NT), None, ALU.is_ge))
        for v in range(2, NT):
            chain(dve.scalar_tensor_tensor(dhi[:, w], ta[:, w], float(NT * v), dhi[:, w], ALU.is_ge, ALU.add))
        chain(dve.scalar_tensor_tensor(ta[:, w], dhi[:, w], -float(NT), ta[:, w], ALU.mult, ALU.add))
        chain(dve.tensor_scalar(klo[:, w], kint[:, w], P - 1, None, ALU.bitwise_and))
        chain(dve.scalar_tensor_tensor(tb[:, w], ta[:, w], float(P), klo[:, w], ALU.mult, ALU.add))
        chain(dve.tensor_copy(srci[:, w], tb[:, w]))
        chain(dve.scalar_tensor_tensor(tb[:, w], dhi[:, w], float(P), dlo[:, w], ALU.mult, ALU.add))
        chain(dve.tensor_copy(dsti[:, w], tb[:, w]))
        chain(dve.tensor_scalar(tb[:, w], src, NONE / 2, -1000.0, ALU.is_lt, ALU.mult))
        chain(dve.tensor_tensor(dhi[:, w], dhi[:, w], tb[:, w], ALU.add))

    def signals(tag):
        names = ("decoded", "idx", "consumed", "weighable", "weights", "pair_ready", "quads", "chain")
        s = {n: sem(f"{tag}_{n}") for n in names}
        s["gathered"] = [sem(f"{tag}_gathered_{i}") for i in range(2)]
        return s

    def fetch(pool, s, g, par, j, at):
        pool.wait_ge(s["consumed"], g + 1)
        settle(pool)
        pool.tensor_copy(idxS[par], srci[:, at]).then_inc(s["idx"], 1)
        pool.tensor_copy(idxD[par], dsti[:, at]).then_inc(s["idx"], 1)
        pool.wait_ge(s["idx"], 2 * g + 2)
        settle(pool)
        for c in range(GC):
            pool.indirect_dma_start(gS[par][:, c, :], None, tab, bass.IndirectOffsetOnAxis(ap=idxS[par][:, c:c + 1], axis=0)).then_inc(s["gathered"][par], 16)
            pool.indirect_dma_start(gD[par][:, c, :], None, dtd, bass.IndirectOffsetOnAxis(ap=idxD[par][:, c:c + 1], axis=0)).then_inc(s["gathered"][par], 16)

    STEPS = 14

    def weigh(dve, s, g, par, j, at):
        n = 0

        def chain(instruction):
            nonlocal n
            n += 1
            instruction.then_inc(s["chain"], 1)
            dve.wait_ge(s["chain"], STEPS * g + n)

        def col(ap, c):
            return ap.rearrange("p (c o) -> p c o", o=1).broadcast_to([P, GC, c])

        dve.wait_ge(s["quads"], QG * g + QG)
        chain(dve.tensor_tensor(ohl[par], col(dlo[:, at], P), iota.rearrange("p (o v) -> p o v", o=1).broadcast_to([P, GC, P]), ALU.is_equal))
        chain(dve.tensor_tensor(ohh, col(dhi[:, at], NT), iota[:, 0:NT].rearrange("p (o v) -> p o v", o=1).broadcast_to([P, GC, NT]), ALU.is_equal))
        dve.wait_ge(s["gathered"][par], 32 * GC * (j + 1))
        g4 = G4.rearrange("p (o v) -> p o v", o=1).broadcast_to([P, GC, FE])
        chain(dve.tensor_tensor(za, gS[par][:, :, HE:], gD[par], ALU.add))
        chain(dve.scalar_tensor_tensor(za, za, 0.2, za, ALU.mult, ALU.max))
        chain(dve.tensor_tensor(zb, gD[par], g4, ALU.add))
        chain(dve.scalar_tensor_tensor(zb, zb, 0.2, zb, ALU.mult, ALU.max))
        chain(dve.tensor_tensor(za, za, zb, ALU.subtract))
        dve.sem_inc(s["weighable"], 1)
        dve.wait_ge(s["weights"], g + 1)
        chain(dve.tensor_copy(val[:, :, HE:], wt))
        chain(dve.tensor_tensor(val[:, :, 0:HE].rearrange("p c (h e) -> p c h e", e=FE),
                                gS[par][:, :, 0:HE].rearrange("p c (h e) -> p c h e", e=FE),
                                wt.rearrange("p c (h o) -> p c h o", o=1).broadcast_to([P, GC, FE, FE]), ALU.mult))
        dve.sem_inc(s["consumed"], 1)
        for q in range(QG):
            dve.wait_ge(s["quads"], QG * g + q - 1 + 2 * QG)
            cs = slice(NQ * q, NQ * q + NQ)
            dve.tensor_tensor(prod[q % 2], ohh[:, cs, :].rearrange("p c (k o) -> p c k o", o=1).broadcast_to([P, NQ, NT, CHN]),
                              val[:, cs, :].rearrange("p c (o f) -> p c o f", o=1).broadcast_to([P, NQ, NT, CHN]),
                              ALU.mult).then_inc(s["pair_ready"], 1)
        dve.wait_ge(s["pair_ready"], QG * g + QG)
        for _ in range(STEPS - n):
            dve.sem_inc(s["chain"], 1)

    def exps(act, s, g):
        act.wait_ge(s["weighable"], g + 1)
        act.activation(wt, za, ACT.Exp).then_inc(s["weights"], 1)

    def add(pe, s, g, par):
        for q in range(QG):
            pe.wait_ge(s["pair_ready"], QG * g + q + 1)
            settle(pe)
            for c in range(NQ):
                lhs = ohl[par][:, NQ * q + c, :]
                pe.matmul(ps[:, 0, 0:SPLIT * CHN], lhs, prod[q % 2][:, c, 0:SPLIT, :], start=False, stop=False, skip_group_check=True)
                last = pe.matmul(ps[:, 1, 0:(NT - SPLIT) * CHN], lhs, prod[q % 2][:, c, SPLIT:, :], start=False, stop=False, skip_group_check=True)
            last.then_inc(s["quads"], 1)

    S1 = signals("m")
    step, zeroed, xc_in, hid, hid_kept, gel, outm, outk = (
        sem("h_" + s) for s in ("step", "zeroed", "xc_in", "hid", "hid_kept", "gel", "outm", "outk"))
    NXC = NT // 3
    GROUPS = CAP // GC
    with nc.Block() as block:
        @block.gpsimd
        def _(pool):
            pool.iota(iotai, [[1, P]], base=0, channel_multiplier=0).then_inc(zeroed, 1)
            pool.sem_inc(S1["consumed"], 2)
            for n in range(2):
                pool.tensor_copy(xc[n], xT[:, 3 * P * n:3 * P * n + 3 * P]).then_inc(xc_in, 1)
            pool.wait_ge(S1["decoded"], 1)
            with pool.Fori(0, GROUPS // 2) as pair:
                for par in range(2):
                    g = 2 * pair + par
                    fetch(pool, S1, g, par, pair, bass.ds(g * GC, GC))

        @block.sync
        def _(sp):
            sp.wait_ge(xc_in, 2)

        @block.tensor
        def _(pe):
            pe.wait_ge(zeroed, 2)
            pe.matmul(ps[:, 0, 0:330], zero[:, 0:P], zero, start=True, stop=False, skip_group_check=True)
            pe.matmul(ps[:, 1, 0:330], zero[:, 0:P], zero, start=True, stop=False, skip_group_check=True)
            with pe.Fori(0, GROUPS // 2) as pair:
                for par in range(2):
                    add(pe, S1, 2 * pair + par, par)

        @block.scalar
        def _(act):
            with act.Fori(0, GROUPS // 2) as pair:
                for par in range(2):
                    exps(act, S1, 2 * pair + par)

        @block.vector
        def _(dve):
            n = 0

            def chain(instruction):
                nonlocal n
                n += 1
                instruction.then_inc(step, 1)
                dve.wait_ge(step, n)

            dve.sem_inc(S1["quads"], 2 * QG)
            dve.wait_ge(zeroed, 1)
            chain(dve.tensor_copy(iota, iotai))
            dve.memset(zero, 0.0).then_inc(zeroed, 1)
            dve.tensor_reduce(rest, keys, X, ALU.max).then_inc(step, 1)
            n += 1
            decode(chain, dve, CAP, picked)
            dve.sem_inc(S1["decoded"], 1)
            with dve.Fori(0, GROUPS // 2) as pair:
                for par in range(2):
                    g = 2 * pair + par
                    weigh(dve, S1, g, par, pair, bass.ds(g * GC, GC))

    S2 = signals("r")
    left, all_left, flagged = sem("r_left"), sem("r_all_left"), sem("r_flagged")
    rstep, m8 = sem("r_step"), ar.take(P, 8)
    zero_at = slice(0, GC)
    ROUNDS = (EC - CAP) // GC
    DEC = 13 + NT + 1 + 3 * (GC // 8)

    def any_left(eng):
        eng.wait_ge(flagged, 1)
        return eng.If(eng.value_load(flagi[0:1, 0:1], min_val=0, max_val=1) > 0)

    with nc.Block() as block:
        @block.gpsimd
        def _(pool):
            pool.partition_all_reduce(flag, rest, P, bass.bass_isa.ReduceOp.max).then_inc(all_left, 1)
            pool.sem_inc(S2["consumed"], 1)
            with any_left(pool):
                with pool.Fori(0, ROUNDS) as g:
                    pool.wait_ge(S2["decoded"], g + 1)
                    fetch(pool, S2, g, 0, g, zero_at)

        @block.tensor
        def _(pe):
            with any_left(pe):
                with pe.Fori(0, ROUNDS) as g:
                    add(pe, S2, g, 0)

        @block.scalar
        def _(act):
            with any_left(act):
                with act.Fori(0, ROUNDS) as g:
                    exps(act, S2, g)

        @block.vector
        def _(dve):
            dve.sem_inc(S2["quads"], QG * 2)
            dve.wait_ge(all_left, 1)
            dve.tensor_scalar(flagi, flag, NONE / 2, None, ALU.is_gt).then_inc(flagged, 1)
            with any_left(dve):
                with dve.Fori(0, ROUNDS) as g:
                    k = 0

                    def chain(instruction):
                        nonlocal k
                        k += 1
                        instruction.then_inc(rstep, 1)
                        dve.wait_ge(rstep, DEC * g + k)
                        settle(dve)

                    for q in range(GC // 8):
                        chain(dve.max(m8, keys))
                        chain(dve.tensor_copy(picked[:, 8 * q:8 * q + 8], m8))
                        chain(dve.match_replace(out=keys, in_to_replace=m8, in_values=keys, imm_value=NONE))
                    decode(chain, dve, GC, picked[:, 0:GC])
                    assert k == DEC, k
                    dve.sem_inc(S2["decoded"], 1)
                    weigh(dve, S2, g, 0, g, zero_at)
                    dve.wait_ge(S2["quads"], QG * g + QG + 2 * QG)
                    settle(dve)
    experts(m, xc, hh, outE, w1, w2)


def experts(m, xc, hh, outE, w1, w2):
    nc, sem, ps, xT = (m[k] for k in ("nc", "sem", "ps", "xT"))
    xc_in, hid, gel, outm, outk = (sem("x_" + s) for s in ("xc_in", "hid", "gel", "outm", "outk"))
    m_used = sem("x_used")
    NXC = NT // 3
    with nc.Block() as block:
        @block.gpsimd
        def _(pool):
            pool.sem_inc(outm, 2)
            with pool.Fori(0, NXC) as i:
                pool.wait_ge(outm, i + 2)
                settle(pool)
                pool.tensor_copy(xc[0], xT[:, bass.ds(i * 3 * P, 3 * P)]).then_inc(xc_in, 1)

        @block.tensor
        def _(pe):
            pe.sem_inc(outk, 1)
            with pe.Fori(0, NXC) as i:
                pe.wait_ge(xc_in, i + 1)
                settle(pe)

                def hidden(e):
                    if e >= 2:
                        pe.wait_ge(gel, FE * i + e - 1)
                        settle(pe)
                    pe.matmul(ps[:, 2 + e % 2, 0:3 * P], w1[:, P * e:P * e + P], xc[0], start=True, stop=True).then_inc(hid, 1)

                def project(e):
                    pe.wait_ge(gel, FE * i + e + 1)
                    if e == 0:
                        pe.wait_ge(outk, i + 1)
                    settle(pe)
                    for t in range(3):
                        last = pe.matmul(ps[:, 4 + t // 2, 256 * (t % 2) + D * e:256 * (t % 2) + D * e + D],
                                         hh[e % 2][:, P * t:P * t + P], w2[:, D * e:D * e + D], start=True, stop=True)
                    last.then_inc(outm, 1) if e == FE - 1 else last.then_inc(m_used, 1)

                hidden(0)
                hidden(1)
                for e in range(FE):
                    if e + 2 < FE:
                        hidden(e + 2)
                    project(e)

        @block.scalar
        def _(act):
            with act.Fori(0, NXC) as i:
                for e in range(FE):
                    act.wait_ge(hid, FE * i + e + 1)
                    if e >= 2:
                        act.wait_ge(m_used, 3 * i + e - 1)
                    act.activation(hh[e % 2], ps[:, 2 + e % 2, 0:3 * P], ACT.Gelu).then_inc(gel, 1)
                act.wait_ge(outm, i + 1 + 2)
                act.activation(outE.rearrange("p (k c) -> p k c", k=NT)[:, bass.ds(i * 3, 3), :],
                               ps[:, 4:6, :].rearrange("p b (t c) -> p (b t) c", t=2)[:, 0:3, :], ACT.Copy).then_inc(outk, 1)


_TRANSPOSED = ("L1_attn_Wq", "L1_attn_Wk", "L1_attn_Wv", "L0_ffn_proj_w")


def tables():
    bf = mybir.dt.np(BF16)
    i = np.arange(P)
    out = {"ident": np.eye(P, dtype=np.float32), "identb": np.eye(P, dtype=bf)}
    later = i[None, :] > i[:, None]
    out["mask_kq"] = np.where(later.T, MASKED, 0.0).astype(bf)
    out["mask_qk"] = np.where(later, MASKED, 0.0).astype(bf)
    s = np.arange(SP_)
    slopes = 0.5 ** np.arange(1, HEADS + 1)
    hi, lo = s // 32 * 32, s % 32
    one = np.ones(SP_)
    out["bias_k"] = np.stack([np.stack([f * hi, f * lo, one, one, one, one]) for f in slopes], 1).astype(bf)
    out["bias_q"] = np.stack([np.stack([one, one, -f * hi, -f * lo]) for f in slopes], 1).astype(bf)
    d = np.arange(S)[None, :] - i[:, None]
    decay = np.exp(d.astype(np.float32) * np.log(np.float32(GAMMA)))
    out["decay"] = np.where(d >= 0, decay, 0.0).astype(np.float32)
    pair = np.zeros((P, D), bf)
    pair[i, i % D] = 1
    out["pair_sum"] = pair
    row = np.zeros((P, P), bf)
    row[:] = i.astype(bf)
    out["count_row"] = row
    return out


def kernel(**inputs):
    import concourse.bacc as _bacc
    from concourse.bass_utils import run_bass_kernel_spmd as _run

    nc = _bacc.Bacc("TRN2", target_bir_lowering=False, num_devices=1)
    arrays, a, c = {}, {}, {}

    def give(name, x):
        arrays[name] = x
        return nc.dram_tensor(name, x.shape, mybir.dt.from_np(x.dtype), kind="ExternalInput").ap()

    for name, x in inputs.items():
        x = np.asarray(x)
        if name in _TRANSPOSED:
            x = x.T
        a[name] = give(f"in_{name}", np.ascontiguousarray(x).reshape(x.shape or (1,)))
    for name, x in tables().items():
        c[name] = give(f"table_{name}", x)
    a["out"] = nc.dram_tensor("out_h", (B, S, D), F32, kind="ExternalOutput").ap()
    build(nc, a, c)
    r = _run(nc, [arrays], core_ids=[0])
    return r.results[0]["out_h"]
```

```python
from contextlib import ExitStack

import numpy as np

import concourse.bass as bass
from concourse import mybir

F32 = mybir.dt.float32
BF16 = mybir.dt.bfloat16
I32 = mybir.dt.int32
ALU = mybir.AluOpType
ACT = mybir.ActivationFunctionType
X = mybir.AxisListType.X

B, T, TXT, D = 4, 1024, 32, 64
S = T + TXT
N = B * S
P = 128
NT = N // P
CH = 352
NCH = S // CH
HEADS, HD = 8, 32
GH = 4
SB = (S + P - 1) // P
SP_ = SB * P
GAMMA = 0.96875
EPS = 1e-5
MASKED = -1e30
N_EDGES = 262144
EC = N_EDGES // P
FE = 4
HE = FE * FE
CHN = HE + FE
GC = 16
CAP = 160
LO, HI = 64, N // 64
CB = 128
NONE = -1e9


def rows(j):
    return min(P, S - P * j)


TILES = [(c, j, max(CH * c, P * j), CH * (c + 1) - max(CH * c, P * j))
         for c in range(NCH) for j in range(SB) if P * j < CH * (c + 1)]


def settle(eng):
    eng.nop(nofuse=True)


class Arena:

    def __init__(self, tensor):
        self.tensor, self.at = tensor, 0

    def take(self, parts, cols, dtype=F32):
        words = cols if dtype != BF16 else (cols + 1) // 2
        words = (words + 7) // 8 * 8
        ap = self.tensor[0:parts, self.at:self.at + words]
        self.at += words
        assert self.at <= self.tensor.shape[1], self.at
        if dtype != F32:
            ap = ap.bitcast(dtype)
        return ap[:, 0:cols]


def build(nc, a, c):
    ctx = ExitStack()

    def sem(name):
        return ctx.enter_context(nc.semaphore(name))

    def sbuf(name, parts, cols, dtype=F32):
        return ctx.enter_context(nc.sbuf_tensor(name, [parts, cols], dtype))

    ident = sbuf("ident", P, P)
    identb = sbuf("identb", P, P, BF16)
    h = sbuf("h", P, NT * D)
    xhat = sbuf("xhat", P, NT * D)
    xT = sbuf("xT", D + 1, N)
    dT = sbuf("dT", D, N)
    stats = sbuf("stats", P, 4 * NT)
    weights = sbuf("weights", P, 2048)
    arena = sbuf("arena", P, 37800)
    ps = ctx.enter_context(nc.psum_tensor("ps", [P, 8, 512], F32))
    h3 = h[:].rearrange("p (k d) -> p k d", d=D)
    xh3 = xhat[:].rearrange("p (k d) -> p k d", d=D)

    edge_keys = nc.dram_tensor("edge_keys", [P, EC], F32, kind="Internal").ap()
    edge_picked = nc.dram_tensor("edge_picked", [P, CAP], F32, kind="Internal").ap()
    edge_digits = nc.dram_tensor("edge_digits", [P, 2 * EC], BF16, kind="Internal").ap()
    m = dict(edge_keys=edge_keys, edge_picked=edge_picked, edge_digits=edge_digits, h=h, xhat=xhat, nc=nc, a=a, c=c, sem=sem, ident=ident, identb=identb, h3=h3, xh3=xh3, xT=xT, dT=dT,
             stats=stats, weights=weights, arena=arena, ps=ps, ctx=ctx)
    with ctx:
        gated_attention(m)
        norm(m, "n1", first=True)
        softmax_attention(m)
        norm(m, "n2")
        binary_experts(m)
        norm(m, "n3")
        retention(m)
        norm(m, "n4")
        graph_experts(m)


def gated_attention(m):
    nc, a, sem, ps, dT, ident = m["nc"], m["a"], m["sem"], m["ps"], m["dT"], m["ident"]
    ar = Arena(m["arena"])
    NB = T // P
    TH = 512
    gn = ar.take(P, NB * T)
    gT = ar.take(P, NB * T)
    xn = ar.take(P, NB * D)
    xb = ar.take(D + 1, T)
    q, k = ar.take(D + 1, T), ar.take(D + 1, T)
    v = ar.take(P, NB * D)
    NP = 4
    p = [ar.take(P, TH) for _ in range(NP)]
    ret = [ar.take(D + 1, TH) for _ in range(2)]
    y = ar.take(D, TH)
    yn = ar.take(D, TH)
    txt = ar.take(P, D)
    keys, picked, m8 = ar.take(P, EC), ar.take(P, CAP), ar.take(P, 8)
    src, dst, shi, dhi = (ar.take(P, EC, I32) for _ in range(4))
    digits = ar.take(P, 2 * EC, BF16)
    near, tmp = m["h"][:, 0:EC], m["xhat"][:, 0:EC]
    edges_in, edge_step, sort_step, edges_out = (sem("a_" + s) for s in ("edges_in", "edge_step", "sort_step", "edges_out"))
    RB = CAP // 8 // B
    w = m["weights"]
    wq, wk, wv, wo = (w[0:D + 1, D * i:D * i + D] for i in range(4))
    bo, pa = w[0:D, 4 * D:4 * D + 1], w[0:D, 4 * D + 1:4 * D + 2]
    ident_in, loaded, gamma_in, x_in = sem("a_ident_in"), sem("a_loaded"), sem("a_gamma_in"), sem("a_x_in")
    ones = sem("a_ones")
    g_turned, g_kept, t_turned, t_kept = sem("a_g_turned"), sem("a_g_kept"), sem("a_t_turned"), sem("a_t_kept")
    prep, prep_slots = sem("a_prep"), sem("a_prep_slots")
    scores, gated, summed = sem("a_scores"), sem("a_gated"), sem("a_summed")
    ret_kept, y_made, y_kept, y_step = sem("a_ret_kept"), sem("a_y_made"), sem("a_y_kept"), sem("a_y_step")
    g3 = gn.rearrange("p (k t) -> p k t", k=NB)
    gT3 = gT.rearrange("p (k t) -> p k t", k=NB)
    v3 = v.rearrange("p (k d) -> p k d", k=NB)
    EDGE_STEPS = 16

    with nc.Block() as block:
        @block.sync
        def _(sp):
            sp.dma_start(ident[:], m["c"]["ident"]).then_inc(ident_in, 16)
            sp.dma_start(m["identb"][:], m["c"]["identb"]).then_inc(ident_in, 16)
            e = a["L1_ffn_edge_index"].rearrange("s (p e) -> s p e", p=P)
            sp.dma_start(src, e[0]).then_inc(edges_in, 16)
            sp.dma_start(dst, e[1]).then_inc(edges_in, 16)
            gsrc = a["L0_tok_d_gamma_batched"].rearrange("(k p) s -> p k s", p=P)
            for n in range(4):
                sp.dma_start(g3[:, 2 * n:2 * n + 2, :], gsrc[:, 2 * n:2 * n + 2, :]).then_inc(gamma_in, 16)
            for wt, name, bias in ((wq, "L0_tok_Wq", "L0_tok_bq"), (wk, "L0_tok_Wk", "L0_tok_bk"),
                                    (wv, "L0_tok_Wv", "L0_tok_bv")):
                sp.dma_start(wt[0:D], a[name]).then_inc(loaded, 16)
                sp.dma_start(wt[D:D + 1], a[bias].rearrange("(o d) -> o d", o=1)).then_inc(loaded, 16)
            sp.dma_start(wo[0:D], a["L0_tok_Wo"]).then_inc(loaded, 16)
            sp.dma_start(bo, a["L0_tok_bo"].rearrange("(d o) -> d o", o=1)).then_inc(loaded, 16)
            sp.dma_start(pa, a["L0_tok_prelu_a"].rearrange("(o d) -> o d", o=1).broadcast_to([D, 1])).then_inc(loaded, 16)
            sp.dma_start(txt, a["txt"].rearrange("b t d -> (b t) d")).then_inc(loaded, 16)
            xsrc = a["x"].rearrange("b o (k p) d -> b p (o k) d", p=P)
            with sp.Fori(0, B) as b:
                sp.wait_ge(prep, 8 * b + 1)
                settle(sp)
                sp.dma_start(xn.rearrange("p (k d) -> p k d", k=NB),
                             xsrc[bass.ds(b, 1)].rearrange("b p k d -> p (b k) d")).then_inc(x_in, 16)
            sp.wait_ge(edge_step, EDGE_STEPS)
            sp.wait_ge(sort_step, 3 * RB * B)
            sp.dma_start(m["edge_digits"], digits).then_inc(edges_out, 16)
            sp.dma_start(m["edge_keys"], keys).then_inc(edges_out, 16)
            sp.dma_start(m["edge_picked"], picked).then_inc(edges_out, 16)
            sp.wait_ge(edges_out, 48)

        @block.tensor
        def _(pe):
            pe.sem_inc(prep, 1)
            pe.wait_ge(ident_in, 32)
            pe.wait_ge(loaded, 16 * 10)
            pe.transpose(ps[0:D, 7, 0:P], txt, ident[:]).then_inc(t_turned, 1)
            for n in range(2 * NB):
                j, th = n % NB, n // NB
                pe.wait_ge(gamma_in, 16 * (2 * th + 2))
                if n >= 4:
                    pe.wait_ge(g_kept, n - 3)
                for i in range(4):
                    last = pe.transpose(ps[:, n % 4, P * i:P * i + P], g3[:, 4 * th + i, P * j:P * j + P], ident[:])
                last.then_inc(g_turned, 1)
            pe.wait_ge(g_kept, 2 * NB)
            pe.wait_ge(t_kept, 1)
            pe.wait_ge(ones, 6)
            with pe.Fori(0, B) as b:
                pe.wait_ge(x_in, 16 * b + 16)
                for n in range(2):
                    pe.wait_ge(prep_slots, 8 * b + n + 1)
                    settle(pe)
                    for i in range(4):
                        last = pe.transpose(ps[0:D, 6 + n, P * i:P * i + P], xn[:, D * (4 * n + i):D * (4 * n + i) + D], ident[:])
                    last.then_inc(prep, 1)
                pe.wait_ge(prep_slots, 8 * b + 2 + 2)
                for n in range(2, 6):
                    pe.wait_ge(prep_slots, 8 * b + n + 1)
                    wt, th = (wq, wk)[(n - 2) // 2], n % 2
                    pe.matmul(ps[0:D, 6 + n % 2, :], wt, xb[:, TH * th:TH * th + TH], start=True, stop=True).then_inc(prep, 1)
                for n in range(6, 8):
                    pe.wait_ge(prep_slots, 8 * b + n + 1)
                    for i in range(4):
                        j = 4 * (n - 6) + i
                        last = pe.matmul(ps[:, 6 + n % 2, D * i:D * i + D], xb[:, P * j:P * j + P], wv, start=True, stop=True)
                    last.then_inc(prep, 1)
                pe.wait_ge(prep_slots, 8 * b + 8 + 2)

                def score(n):
                    th, j = n // NB, n % NB
                    pe.wait_ge(gated, 16 * b + n + 1)
                    pe.matmul(ps[:, n % 4, :], k[:, P * j:P * j + P], q[:, TH * th:TH * th + TH],
                              start=True, stop=True).then_inc(scores, 1)

                def weigh(n):
                    th, j = n // NB, n % NB
                    pe.wait_ge(gated, 16 * b + n + 1 + 4)
                    if j == 0:
                        pe.wait_ge(y_kept, 2 * b + th + 1)
                    pe.matmul(ps[0:D, 4 + th, :], v3[:, j, :], p[n % NP], start=(j == 0), stop=(j == NB - 1)).then_inc(summed, 1)

                def project(th):
                    pe.wait_ge(ret_kept, 2 * b + th + 1)
                    settle(pe)
                    pe.matmul(ps[0:D, 4 + th, :], wo, ret[th], start=True, stop=True).then_inc(y_made, 1)

                score(0)
                score(1)
                for n in range(2 * NB):
                    if n + 2 < 2 * NB:
                        score(n + 2)
                    weigh(n)
                    if n == NB + 1:
                        project(0)
                project(1)

        @block.scalar
        def _(act):
            act.wait_ge(t_turned, 1)
            for b in range(B):
                last = act.activation(dT[:, S * b + T:S * b + S], ps[0:D, 7, TXT * b:TXT * b + TXT], ACT.Copy)
            last.then_inc(t_kept, 1)
            for n in range(2 * NB):
                j, th = n % NB, n // NB
                act.wait_ge(g_turned, n + 1)
                act.activation(gT3[:, j, TH * th:TH * th + TH], ps[:, n % 4, :], ACT.Copy).then_inc(g_kept, 1)
            act.sem_inc(prep_slots, 2)
            with act.Fori(0, B) as b:
                for n in range(8):
                    act.wait_ge(prep, 8 * b + n + 1 + 1)
                    bank = ps[:, 6 + n % 2, :]
                    if n < 2:
                        dst, src = xb[0:D, TH * n:TH * n + TH], bank[0:D]
                    elif n < 6:
                        dst, src = (q, k)[(n - 2) // 2][0:D, TH * (n % 2):TH * (n % 2) + TH], bank[0:D]
                    else:
                        dst, src = v[:, 4 * D * (n - 6):4 * D * (n - 6) + 4 * D], bank[:, 0:4 * D]
                    act.activation(dst, src, ACT.Copy).then_inc(prep_slots, 1)
                for th in range(2):
                    act.wait_ge(summed, 16 * b + NB * (th + 1) + 4)
                    act.activation(ret[th][0:D], ps[0:D, 4 + th, :], ACT.Copy).then_inc(ret_kept, 1)

        @block.vector
        def _(dve):
            dve.memset(xb[D:D + 1, :], 1.0).then_inc(ones, 1)
            for t in (q, k, *ret, wo):
                dve.memset(t[D:D + 1, :], 0.0).then_inc(ones, 1)
            dve.sem_inc(gated, 4)
            dve.sem_inc(summed, 4)
            dve.sem_inc(y_kept, 2)
            n = 0

            def chain(instruction):
                nonlocal n
                n += 1
                instruction.then_inc(edge_step, 1)
                dve.wait_ge(edge_step, n)

            dve.wait_ge(edges_in, 32)
            chain(dve.tensor_scalar(shi, src, 7, None, ALU.arith_shift_right))
            chain(dve.tensor_scalar(dhi, dst, 7, None, ALU.arith_shift_right))
            chain(dve.tensor_scalar(keys, dhi, float(32 << 14), float(-(544 << 14)), ALU.mult, ALU.add))
            chain(dve.scalar_tensor_tensor(keys, shi, float((1 << 14) - P), keys, ALU.mult, ALU.add))
            chain(dve.scalar_tensor_tensor(keys, dst, float(P), keys, ALU.mult, ALU.add))
            chain(dve.tensor_tensor(keys, src, keys, ALU.add))
            chain(dve.tensor_scalar(tmp, dst, float(N), None, ALU.is_lt))
            chain(dve.scalar_tensor_tensor(near, src, float(N - 1), tmp, ALU.is_lt, ALU.mult))
            chain(dve.tensor_tensor(keys, keys, near, ALU.mult))
            chain(dve.tensor_scalar(tmp, near, -NONE, NONE, ALU.mult, ALU.add))
            chain(dve.tensor_tensor(keys, keys, tmp, ALU.add))
            chain(dve.tensor_scalar(dhi, dst, 6, None, ALU.arith_shift_right))
            chain(dve.tensor_scalar(tmp, src, float(N - 1), 100.0, ALU.is_lt, ALU.mult))
            chain(dve.tensor_tensor(digits[:, EC:], dhi, tmp, ALU.max))
            chain(dve.tensor_scalar(dhi, dst, LO - 1, None, ALU.bitwise_and))
            chain(dve.tensor_copy(digits[:, 0:EC], dhi))
            assert n == EDGE_STEPS, n
            with dve.Fori(0, B) as b:
                def finish(th):
                    n = 3 * (2 * b + th)
                    dve.wait_ge(y_made, 2 * b + th + 1)
                    dve.tensor_scalar(y, ps[0:D, 4 + th, :], bo, None, ALU.add).then_inc(y_step, 1)
                    dve.wait_ge(y_step, n + 1)
                    dve.tensor_scalar(yn, y, 0.0, pa, ALU.min, ALU.mult).then_inc(y_step, 1)
                    dve.wait_ge(y_step, n + 2)
                    dve.scalar_tensor_tensor(dT[:, bass.ds(b * S + TH * th, TH)], y, 0.0, yn, ALU.max, ALU.add).then_inc(y_step, 1)
                    dve.wait_ge(y_step, n + 3)
                    dve.sem_inc(y_kept, 1)

                def sort(n):
                    r, part = n // 3, n % 3
                    if r >= RB:
                        return
                    done = 3 * RB * b + 3 * r + part
                    if part == 0:
                        if r > 0:
                            dve.wait_ge(sort_step, done)
                            settle(dve)
                        dve.max(m8, keys).then_inc(sort_step, 1)
                    elif part == 1:
                        dve.wait_ge(sort_step, done)
                        dve.tensor_copy(picked[:, bass.ds(8 * RB * b + 8 * r, 8)], m8).then_inc(sort_step, 1)
                    else:
                        dve.wait_ge(sort_step, done)
                        settle(dve)
                        dve.match_replace(out=keys, in_to_replace=m8, in_values=keys, imm_value=NONE).then_inc(sort_step, 1)

                for n in range(2 * NB):
                    th, j = n // NB, n % NB
                    dve.wait_ge(scores, 16 * b + n + 1)
                    dve.wait_ge(summed, 16 * b + n + 1)
                    dve.tensor_tensor(p[n % NP], ps[:, n % 4, :], gT3[:, j, TH * th:TH * th + TH], ALU.mult).then_inc(gated, 1)
                    sort(n)
                    if n == NB + 3:
                        finish(0)
                finish(1)


def norm(m, tag, first=False):
    nc, sem, ps, dT, ident, h3, xh3, xT = (m[k] for k in ("nc", "sem", "ps", "dT", "ident", "h3", "xh3", "xT"))
    sums, var, rstd = (m["stats"][:, NT * i:NT * i + NT] for i in range(3))
    sq = m["arena"][:, 0:NT * D].rearrange("p (k d) -> p k d", d=D)
    turned, step, root, back, kept = (sem(f"{tag}_{s}") for s in ("turned", "step", "root", "back", "kept"))
    groups = [range(8 * g, min(8 * g + 8, NT)) for g in range((NT + 7) // 8)]
    quads = [range(4 * g, min(4 * g + 4, NT)) for g in range((NT + 3) // 4)]
    NG = len(groups)

    with nc.Block() as block:
        @block.tensor
        def _(pe):
            for g, tiles in enumerate(groups):
                for i, t in enumerate(tiles):
                    last = pe.transpose(ps[:, g, D * i:D * i + D], dT[:, P * t:P * t + P], ident[0:D, 0:D])
                last.then_inc(turned, 1)
            for g, tiles in enumerate(quads):
                pe.wait_ge(step, NG + 7)
                if g >= 3:
                    pe.wait_ge(kept, g - 2)
                for i, t in enumerate(tiles):
                    last = pe.transpose(ps[0:D, 5 + g % 3, P * i:P * i + P], xh3[:, t, :], ident[:])
                last.then_inc(back, 1)

        @block.vector
        def _(dve):
            for g, tiles in enumerate(groups):
                lo, hi = tiles[0], tiles[-1] + 1
                dve.wait_ge(turned, g + 1)
                src = ps[:, g, 0:D * (hi - lo)].rearrange("p (k d) -> p k d", d=D)
                if first:
                    dve.tensor_copy(h3[:, lo:hi, :], src).then_inc(step, 1)
                else:
                    dve.tensor_tensor(h3[:, lo:hi, :], h3[:, lo:hi, :], src, ALU.add).then_inc(step, 1)
            if first:
                dve.memset(xT[D:D + 1, :], 1.0)
            dve.wait_ge(step, NG)
            dve.tensor_reduce(sums, h3, X, ALU.add).then_inc(step, 1)
            dve.wait_ge(step, NG + 1)
            dve.tensor_scalar(sums, sums, 1.0 / D, None, ALU.mult).then_inc(step, 1)
            dve.wait_ge(step, NG + 2)
            mean = sums.rearrange("p (k o) -> p k o", o=1).broadcast_to([P, NT, D])
            dve.tensor_tensor(xh3, h3, mean, ALU.subtract).then_inc(step, 1)
            dve.wait_ge(step, NG + 3)
            dve.tensor_tensor(sq, xh3, xh3, ALU.mult).then_inc(step, 1)
            dve.wait_ge(step, NG + 4)
            dve.tensor_reduce(var, sq, X, ALU.add).then_inc(step, 1)
            dve.wait_ge(step, NG + 5)
            dve.tensor_scalar(var, var, 1.0 / D, EPS, ALU.mult, ALU.add).then_inc(step, 1)
            dve.wait_ge(root, 1)
            dve.reciprocal(rstd, rstd).then_inc(root, 1)
            dve.wait_ge(root, 2)
            scale = rstd.rearrange("p (k o) -> p k o", o=1).broadcast_to([P, NT, D])
            dve.tensor_tensor(xh3, xh3, scale, ALU.mult).then_inc(step, 1)

        @block.scalar
        def _(act):
            act.wait_ge(step, NG + 6)
            act.activation(rstd, var, ACT.Sqrt).then_inc(root, 1)
            for g, tiles in enumerate(quads):
                lo, n = P * tiles[0], P * len(tiles)
                act.wait_ge(back, g + 1)
                act.activation(xT[0:D, lo:lo + n], ps[0:D, 5 + g % 3, 0:n], ACT.Copy).then_inc(kept, 1)


def softmax_attention(m):
    nc, a, c, sem, ps, dT, xT = (m[k] for k in ("nc", "a", "c", "sem", "ps", "dT", "xT"))
    ar = Arena(m["arena"])
    identb, ident = m["identb"], m["ident"]
    q1 = [ar.take(102, GH * SP_, BF16).rearrange("p (h t) -> p h t", h=GH) for _ in range(2)]
    k1 = [ar.take(102, GH * SP_, BF16).rearrange("p (h t) -> p h t", h=GH) for _ in range(2)]
    q2 = [ar.take(96, GH * S, BF16).rearrange("p (h t) -> p h t", h=GH) for _ in range(2)]
    k2 = [ar.take(96, GH * S, BF16).rearrange("p (h t) -> p h t", h=GH) for _ in range(2)]
    parts = [[ar.take(P, S, BF16) for _ in range(3)] for _ in range(2)]
    qk = [ar.take(P, S) for _ in range(2)]
    vs = ar.take(P, SB * P)
    v = [ar.take(P, SB * P) for _ in range(2)]
    xb = ar.take(D + 1, S)
    prob = [ar.take(P, GH * CH).rearrange("p (h t) -> p h t", h=GH) for _ in range(2)]
    oT = [ar.take(P, S) for _ in range(2)]
    rec = ar.take(P, CH)
    ones = ar.take(P, HD)
    mask_kq, mask_qk = ar.take(P, P, BF16), ar.take(P, P, BF16)
    mx = ar.take(P, GH * SB * 3)
    mc = ar.take(P, GH * SB)
    mhl = ar.take(GH * SB, 2 * P, BF16)
    w = m["weights"]
    wq, wk, wv = (w[0:D + 1, 256 * i:256 * i + 256] for i in range(3))
    wo = [w[:, 768 + D * g:768 + D * g + D] for g in range(2)]
    bo = w[0:D, 900:901]
    hml = nc.dram_tensor("split_parts", [6, P, S], BF16, kind="Internal").ap()

    loaded, set_up = sem("b_loaded"), sem("b_set_up")
    xb_in, projected, taken_act, taken_dve = sem("b_xb_in"), sem("b_projected"), sem("b_taken_act"), sem("b_taken_dve")
    split, parts_out, first_in, second_in = sem("b_split"), sem("b_parts_out"), sem("b_first_in"), sem("b_second_in")
    maxed, m_split, m_in = sem("b_maxed"), sem("b_m_split"), sem("b_m_in")
    scores, probs, weighed = sem("b_scores"), sem("b_probs"), sem("b_weighed")
    acc_free = sem("b_acc_free")
    rec_made, normed, out_made, out_kept = sem("b_rec_made"), sem("b_normed"), sem("b_out_made"), sem("b_out_kept")

    UNITS = 2 * B
    PIECES = [(j, i, n, min(512, P * i + rows(i) - 512 * n)) for j in range(GH) for i in range(SB)
              for n in range((P * i + rows(i) + 511) // 512)]
    NM, NPJ = len(PIECES) + 1, 9
    NTL = len(TILES)
    FIRST = 2 * NPJ + NM
    LAST_TILE = [max(n for n in range(NTL) if TILES[n][0] == ch) for ch in range(NCH)]
    PER_SLOT, SLOT0 = 5, 2

    def bank(n):
        return 6 + n % 2 if n >= FIRST else n % 8

    def split_unit(eng, u):
        for n in range(2):
            hi, mid, lo = parts[n]
            at = 8 * u + 4 * n
            eng.wait_ge(taken_act, NPJ * u + 3 * n + 3)
            if not (isinstance(u, int) and u == 0):
                eng.wait_ge(parts_out, 96 * u)
            settle(eng)
            eng.tensor_copy(hi, qk[n]).then_inc(split, 1)
            eng.wait_ge(split, at + 1)
            settle(eng)
            eng.tensor_tensor(qk[n], qk[n], hi, ALU.subtract).then_inc(split, 1)
            eng.wait_ge(split, at + 2)
            settle(eng)
            eng.tensor_copy(mid, qk[n]).then_inc(split, 1)
            eng.wait_ge(split, at + 3)
            settle(eng)
            eng.tensor_tensor(lo, qk[n], mid, ALU.subtract).then_inc(split, 1)

    with nc.Block() as block:
        @block.sync
        def _(sp):
            for dst, name in ((wq, "Wq"), (wk, "Wk"), (wv, "Wv")):
                sp.dma_start(dst[0:D], a["L0_attn_" + name]).then_inc(loaded, 16)
            for g in range(2):
                sp.dma_start(wo[g], a["L0_attn_Wo"][P * g:P * g + P]).then_inc(loaded, 16)
            sp.dma_start(bo, a["L0_attn_bo"].rearrange("(d o) -> d o", o=1)).then_inc(loaded, 16)
            sp.dma_start(mask_kq, c["mask_kq"]).then_inc(loaded, 16)
            sp.dma_start(mask_qk, c["mask_qk"]).then_inc(loaded, 16)
            for g in range(2):
                sp.dma_start(k1[g][96:102], c["bias_k"][:, GH * g:GH * g + GH]).then_inc(loaded, 16)
                sp.dma_start(q1[g][96:100], c["bias_q"][:, GH * g:GH * g + GH]).then_inc(loaded, 16)

            def parts_to_dram(u):
                for n in range(6):
                    sp.wait_ge(split, 8 * u + (1, 3, 4, 5, 7, 8)[n])
                    sp.dma_start(hml[n], parts[n // 3][n % 3]).then_inc(parts_out, 16)

            def stacks_in(u, g):
                sp.wait_ge(parts_out, 96 * u + 96)
                settle(sp)
                if not isinstance(u, int):
                    sp.wait_ge(scores, 2 * NTL * (u - 1))
                for stack, order, done in ((q1, (0, 1, 0), first_in), (k1, (3, 3, 4), first_in),
                                           (q2, (1, 2, 0), second_in), (k2, (4, 3, 5), second_in)):
                    for s, n in enumerate(order):
                        sp.dma_start(stack[g][32 * s:32 * s + 32, :, 0:S],
                                     hml[n].rearrange("(h d) t -> d h t", h=GH)).then_inc(done, 16)
                sp.wait_ge(taken_act, NPJ * u + NPJ)
                if not isinstance(u, int):
                    sp.wait_ge(weighed, NTL * (u - 1) + 2)
                sp.dma_start(v[g], vs).then_inc(second_in, 16)

            def maxima_in(u, g):
                sp.wait_ge(m_split, 2 * u + 2)
                for n in range(2):
                    sp.dma_start(q1[g][100 + n:101 + n, :, :].rearrange("p h t -> p (h t)"),
                                 mhl[:, P * n:P * n + P]).then_inc(m_in, 16)

            parts_to_dram(0)
            stacks_in(0, 0)
            sp.wait_ge(first_in, 96)
            sp.wait_ge(second_in, 112)
            parts_to_dram(1)
            stacks_in(1, 1)
            sp.wait_ge(first_in, 192)
            sp.wait_ge(second_in, 224)
            maxima_in(0, 0)

            def slot(u, g, project, maxima):
                if project:
                    parts_to_dram(u + 2)
                if maxima:
                    maxima_in(u + 1, 1 - g)
                if project:
                    stacks_in(u + 2, g)
                    sp.wait_ge(first_in, 96 * (u + 3))
                    settle(sp)
                    sp.wait_ge(second_in, 112 * (u + 3))
                    settle(sp)

            with sp.Fori(0, B - 1) as b:
                slot(2 * b, 0, True, True)
                slot(2 * b + 1, 1, True, True)
            slot(UNITS - 2, 0, False, True)
            slot(UNITS - 1, 1, False, False)

        @block.gpsimd
        def _(pool):
            pool.memset(ones, 1.0).then_inc(set_up, 1)
            pool.memset(vs[:, P * (SB - 1):], 0.0).then_inc(set_up, 1)

            def batch_in(b, earlier):
                if earlier is not None:
                    pool.wait_ge(projected, earlier)
                    settle(pool)
                pool.tensor_copy(xb, xT[:, b]).then_inc(xb_in, 1)

            batch_in(slice(0, S), None)
            with pool.Fori(0, B - 1) as b:
                batch_in(bass.ds((b + 1) * S, S), 2 * NPJ + 2 * (NPJ + NM) * b)
                split_unit(pool, 2 * b + 2)
                split_unit(pool, 2 * b + 3)

        @block.tensor
        def _(pe):
            pe.wait_ge(loaded, 16 * 12)
            pe.wait_ge(set_up, 3)

            def project(u, g, n, use):
                pe.wait_ge(xb_in, u // 2 + 1 if isinstance(u, int) else batch_base[0])
                settle(pe)
                if n < 6:
                    wt, ch = (wq, wk)[n // 3], n % 3
                    pe.matmul(ps[:, bank(use), 0:CH], wt[:, P * g:P * g + P], xb[:, CH * ch:CH * ch + CH],
                              start=True, stop=True).then_inc(projected, 1)
                else:
                    for i in range(3):
                        j = 3 * (n - 6) + i
                        last = pe.matmul(ps[0:rows(j), bank(use), P * i:P * i + P], xb[:, P * j:P * j + rows(j)],
                                         wv[:, P * g:P * g + P], start=True, stop=True)
                    last.then_inc(projected, 1)

            def maxima(u, g, n, use):
                if n == NM - 1:
                    pe.wait_ge(maxed, u + 1)
                    settle(pe)
                    pe.transpose(ps[0:GH * SB, bank(use), 0:P], mc, ident[:]).then_inc(projected, 1)
                    return
                j, i, k, width = PIECES[n]
                settle(pe)
                if n == 0:
                    pe.wait_ge(first_in, 96 * (u + 1))
                diag = P * i < 512 * k + width
                last = pe.matmul(ps[0:rows(i), bank(use), 0:width], q1[g][0:100, j, P * i:P * i + rows(i)],
                                 k1[g][0:100, j, 512 * k:512 * k + width], start=True, stop=not diag)
                if diag:
                    o = P * i - 512 * k
                    last = pe.matmul(ps[0:rows(i), bank(use), o:o + rows(i)], identb[:, 0:rows(i)],
                                     mask_qk[:, 0:rows(i)], start=False, stop=True)
                last.then_inc(projected, 1)

            def score(u, g, n):
                ch, j, lo, width = TILES[n]
                if n == 0:
                    pe.wait_ge(m_in, 32 * (u + 1))
                    pe.wait_ge(second_in, 112 * (u + 1))
                for half in range(2):
                    settle(pe)
                    pe.wait_ge(probs, 2 * NTL * u + 2 * n + half + 1)
                    for hd in range(2 * half, 2 * half + 2):
                        r = rows(j)
                        cut = lo < P * j + r
                        pe.matmul(ps[0:r, hd, 0:width], k1[g][0:102, hd, P * j:P * j + r], q1[g][0:102, hd, lo:lo + width],
                                  start=True, stop=False)
                        last = pe.matmul(ps[0:r, hd, 0:width], k2[g][:, hd, P * j:P * j + r], q2[g][:, hd, lo:lo + width],
                                         start=False, stop=not cut)
                        if cut:
                            wd = min(P * j + r, lo + width) - lo
                            last = pe.matmul(ps[0:r, hd, 0:wd], identb[:, 0:r], mask_kq[:, lo - P * j:lo - P * j + wd],
                                             start=False, stop=True)
                    last.then_inc(scores, 1)
                if n == NTL - 1:
                    pass

            def weigh(u, g, n):
                ch, j, lo, width = TILES[n]
                pe.wait_ge(probs, 2 * NTL * u + 2 * n + 2 + 2)
                if j == 0:
                    pe.wait_ge(acc_free, NCH * u + ch + 1)
                    if g == 0 and ch == 0:
                        pe.wait_ge(out_kept, out_base[0] + 1)
                settle(pe)
                r, o = rows(j), lo - CH * ch
                stop = n in LAST_TILE
                for hd in range(GH):
                    pe.matmul(ps[HD * hd:HD * hd + HD, 4, o:o + width], v[g][0:r, P * j + HD * hd:P * j + HD * hd + HD],
                              prob[n % 2][0:r, hd, 0:width], start=(j == 0), stop=stop, skip_group_check=True)
                for hd in range(GH):
                    last = pe.matmul(ps[HD * hd:HD * hd + HD, 5, o:o + width], ones[0:r, :],
                                     prob[n % 2][0:r, hd, 0:width], start=(j == 0), stop=stop, skip_group_check=True)
                last.then_inc(weighed, 1)

            out_base, batch_base = [None], [None]

            def slot(u, g, b, project_next, maxima_next):
                out_base[0], batch_base[0] = NCH * b, b + 2
                use, acts = 0, NPJ if project_next else 0

                def before():
                    if use >= 2 and use - 2 < acts:
                        pe.wait_ge(taken_act, NPJ * (u + 2) + use - 1)
                    elif use >= 2:
                        pe.wait_ge(taken_dve, NM * (u + 1) + use - 1 - acts)
                    else:
                        pe.wait_ge(taken_dve, NM * (u + 1) + use - 1)

                for n in range(NTL + 1):
                    if n < NTL:
                        score(u, g, n)
                    if project_next and n < 3:
                        for i in range(3):
                            before()
                            project(u + 2, g, 3 * n + i, FIRST + use)
                            use += 1
                    if maxima_next and SLOT0 <= n <= SLOT0 + NM // PER_SLOT:
                        for i in range(PER_SLOT * (n - SLOT0), min(PER_SLOT * (n - SLOT0 + 1), NM)):
                            before()
                            maxima(u + 1, 1 - g, i, FIRST + use)
                            use += 1
                    if n >= 1:
                        weigh(u, g, n - 1)
                if g == 1:
                    for ch in range(NCH):
                        pe.wait_ge(normed, NCH * (u + 1) + 1)
                        if ch == 2:
                            pe.wait_ge(out_kept, NCH * b + 1 + 1)
                        for k in range(2):
                            last = pe.matmul(ps[0:D, 4 + ch % 2, 0:CH], wo[k], oT[k][:, CH * ch:CH * ch + CH],
                                             start=(k == 0), stop=(k == 1))
                        last.then_inc(out_made, 1)

            for n in range(FIRST):
                if n >= 8:
                    if n - 8 < 2 * NPJ:
                        pe.wait_ge(taken_act, n - 7)
                    else:
                        pe.wait_ge(taken_dve, n - 7 - 2 * NPJ)
                if n < 2 * NPJ:
                    project(n // NPJ, n // NPJ, n % NPJ, n)
                else:
                    maxima(0, 0, n - 2 * NPJ, n)
            with pe.Fori(0, B - 1) as b:
                slot(2 * b, 0, b, True, True)
                slot(2 * b + 1, 1, b, True, True)
            slot(UNITS - 2, 0, B - 1, False, True)
            slot(UNITS - 1, 1, B - 1, False, False)

        @block.scalar
        def _(act):
            act.sem_inc(probs, 2)
            act.sem_inc(out_kept, 1)
            act.wait_ge(set_up, 3)
            act.wait_ge(loaded, 16 * 12)

            def take(u, n, use, count):
                act.wait_ge(projected, count + 1)
                if n == 0 or n == 3:
                    if not (isinstance(u, int) and u == 0):
                        act.wait_ge(split, 8 * u - 8 + (4 if n == 0 else 8))
                if n == 6 and not (isinstance(u, int) and u == 0):
                    act.wait_ge(second_in, 112 * u)
                if n < 6:
                    dst = qk[n // 3][:, CH * (n % 3):CH * (n % 3) + CH]
                    act.activation(dst, ps[:, bank(use), 0:CH], ACT.Copy, scale=(HD ** -0.5, 1.0)[n // 3]).then_inc(taken_act, 1)
                elif n < 8:
                    act.activation(vs[:, 3 * P * (n - 6):3 * P * (n - 5)], ps[:, bank(use), 0:3 * P], ACT.Copy).then_inc(taken_act, 1)
                else:
                    act.activation(vs[:, 6 * P:8 * P], ps[:, bank(use), 0:2 * P], ACT.Copy)
                    act.activation(vs[0:rows(8), 8 * P:9 * P], ps[0:rows(8), bank(use), 2 * P:3 * P], ACT.Copy).then_inc(taken_act, 1)

            def slot(u, g, b, project_next):
                for n in range(NTL):
                    ch, j, lo, width = TILES[n]
                    r = rows(j)
                    act.wait_ge(weighed, NTL * u + n + 1)
                    for half in range(2):
                        act.wait_ge(scores, 2 * NTL * u + 2 * n + half + 1)
                        act.activation(prob[n % 2][0:r, 2 * half:2 * half + 2, 0:width], ps[0:r, 2 * half:2 * half + 2, 0:width],
                                       ACT.Exp).then_inc(probs, 1)
                    if project_next and n < 3:
                        for i in range(3):
                            take(u + 2, 3 * n + i, FIRST + 3 * n + i, FIRST + (NPJ + NM) * u + 3 * n + i)
                if g == 1:
                    for ch in range(NCH):
                        act.wait_ge(out_made, NCH * b + ch + 1 + 1)
                        act.activation(dT[:, bass.ds(b * S + CH * ch, CH)] if not isinstance(b, int) else dT[:, b * S + CH * ch:b * S + CH * ch + CH],
                                       ps[0:D, 4 + ch % 2, 0:CH], ACT.Identity, bias=bo).then_inc(out_kept, 1)

            for n in range(2 * NPJ):
                take(n // NPJ, n % NPJ, n, n)
            with act.Fori(0, B - 1) as b:
                slot(2 * b, 0, b, True)
                slot(2 * b + 1, 1, b, True)
            slot(UNITS - 2, 0, B - 1, False)
            slot(UNITS - 1, 1, B - 1, False)

        @block.vector
        def _(dve):
            dve.memset(w[D:D + 1, 0:768], 0.0).then_inc(set_up, 1)
            dve.memset(mx, MASKED).then_inc(rec_made, 1)
            dve.wait_ge(rec_made, 1)
            dve.sem_inc(weighed, 2)
            dve.sem_inc(normed, 1)
            dve.sem_inc(acc_free, 1)
            dve.sem_inc(out_made, 1)
            split_unit(dve, 0)
            split_unit(dve, 1)

            def take_max(u, n, use, count):
                if n == 0:
                    dve.wait_ge(maxed, u if not isinstance(u, int) or u else 0) if not (isinstance(u, int) and u == 0) else None
                if n == NM - 1:
                    dve.wait_ge(taken_dve, NM * u + NM - 1)
                    if not (isinstance(u, int) and u == 0):
                        dve.wait_ge(m_in, 32 * u)
                    dve.tensor_reduce(mc, mx.rearrange("p (b n) -> p b n", n=3), X, ALU.max).then_inc(maxed, 1)
                    dve.wait_ge(projected, count + 1)
                    src = ps[0:GH * SB, bank(use), 0:P]
                    dve.tensor_scalar(mhl[:, 0:P], src, -1.0, None, ALU.mult).then_inc(m_split, 1)
                    dve.wait_ge(m_split, 2 * u + 1)
                    dve.scalar_tensor_tensor(mhl[:, P:2 * P], src, -1.0, mhl[:, 0:P], ALU.mult, ALU.subtract).then_inc(m_split, 1)
                    dve.wait_ge(m_split, 2 * u + 2)
                    dve.sem_inc(taken_dve, 1)
                    return
                j, i, k, width = PIECES[n]
                dve.wait_ge(projected, count + 1)
                at = 3 * (SB * j + i) + k
                dve.reduce_max(mx[0:rows(i), at:at + 1], ps[0:rows(i), bank(use), 0:width], X).then_inc(taken_dve, 1)

            def empty_banks(u, g, ch, b):
                dve.wait_ge(weighed, NTL * u + LAST_TILE[ch] + 1 + 2)
                dve.wait_ge(normed, NCH * u + ch + 1)
                if ch == 0 and g == 0:
                    dve.wait_ge(out_made, NCH * b + 1)
                at = 3 * (NCH * u + ch) + 1
                out = oT[g][:, CH * ch:CH * ch + CH]
                dve.tensor_copy(rec, ps[:, 5, 0:CH]).then_inc(rec_made, 1)
                dve.tensor_copy(out, ps[:, 4, 0:CH]).then_inc(rec_made, 1)
                dve.wait_ge(rec_made, at + 2)
                dve.sem_inc(acc_free, 1)

            def norm_chunk(u, g, ch):
                at = 3 * (NCH * u + ch) + 1
                out = oT[g][:, CH * ch:CH * ch + CH]
                dve.reciprocal(rec, rec).then_inc(rec_made, 1)
                dve.wait_ge(rec_made, at + 3)
                settle(dve)
                dve.tensor_tensor(out, out, rec, ALU.mult).then_inc(normed, 1)

            def slot(u, g, b, acts, maxima_next):
                use = acts
                for n in range(NTL):
                    for ch in range(NCH - 1):
                        if n == LAST_TILE[ch] + 2:
                            empty_banks(u, g, ch, b)
                    if maxima_next and SLOT0 <= n <= SLOT0 + NM // PER_SLOT:
                        for i in range(PER_SLOT * (n - SLOT0), min(PER_SLOT * (n - SLOT0 + 1), NM)):
                            take_max(u + 1, i, FIRST + use, FIRST + (NPJ + NM) * u + use)
                            use += 1
                    for ch in range(NCH - 1):
                        if n == LAST_TILE[ch] + 2:
                            norm_chunk(u, g, ch)
                empty_banks(u, g, NCH - 1, b)
                norm_chunk(u, g, NCH - 1)

            for n in range(NM):
                take_max(0, n, 2 * NPJ + n, 2 * NPJ + n)
            with dve.Fori(0, B - 1) as b:
                slot(2 * b, 0, b, NPJ, True)
                slot(2 * b + 1, 1, b, NPJ, True)
            slot(UNITS - 2, 0, B - 1, 0, True)
            slot(UNITS - 1, 1, B - 1, 0, False)


def binary_experts(m):
    nc, a, c, sem, ps, dT, xT, xh3 = (m[k] for k in ("nc", "a", "c", "sem", "ps", "dT", "xT", "xh3"))
    ar = Arena(m["arena"])
    identb = m["identb"]
    E, IN, OUT = 8, D, D
    NQ, NG = IN * E // P, IN // 4
    NP = NG * 2
    aT = ar.take(P, NQ * N, BF16).rearrange("p (q t) -> p q t", q=NQ)
    an = [ar.take(P, IN * E, BF16) for _ in range(2)]
    sg = ar.take(P, NT * D, BF16)
    gate = ar.take(P, NT * E, BF16)
    stack = [ar.take(96, NG * CH, BF16).rearrange("p (g t) -> p g t", g=NG) for _ in range(3)]
    wf = ar.take(96, NG * OUT)
    wsplit = [ar.take(96, NG * OUT, BF16) for _ in range(3)]
    wl = ar.take(96, NG * 2 * P, BF16)
    NS = 4
    sgn = [ar.take(P, 2 * CH, BF16).rearrange("p (n t) -> p n t", n=2) for _ in range(NS)]
    neg = ar.take(P, 2 * CH, BF16).rearrange("p (n t) -> p n t", n=2)
    pair_sum = ar.take(P, D, BF16)
    pw = ar.take(D + 1, E)
    sc = ar.take(D, 1)
    loaded, w_in, wstep, w_placed, zeroed = sem("c_loaded"), sem("c_w_in"), sem("c_wstep"), sem("c_w_placed"), sem("c_zeroed")
    logits, gates, signs, made, turned, kept = (sem("c_" + s) for s in ("logits", "gates", "signs", "made", "turned", "kept"))
    sg3 = sg.rearrange("p (k d) -> p k d", d=D)
    g3 = gate.rearrange("p (k e) -> p k e", e=E)
    wl4 = wl.rearrange("p (g f i o) -> p g f i o", g=NG, f=2, i=2)

    with nc.Block() as block:
        @block.sync
        def _(sp):
            sp.dma_start(pw[0:D], a["L0_ffn_proj_w"]).then_inc(loaded, 16)
            sp.dma_start(pw[D:D + 1], a["L0_ffn_proj_b"].rearrange("(o e) -> o e", o=1)).then_inc(loaded, 16)
            sp.dma_start(sc, a["L0_ffn_scale"].rearrange("a b o -> o (a b)")).then_inc(loaded, 16)
            sp.dma_start(pair_sum, c["pair_sum"]).then_inc(loaded, 16)
            src = a["L0_ffn_weight"].rearrange("o e (g i) d -> i e (o g) d", i=4)
            for s in range(3):
                for i in range(4):
                    at = 32 * s + E * i
                    sp.dma_start(wf[at:at + E].rearrange("p (g d) -> p g d", g=NG), src[i]).then_inc(w_in, 16)
            sp.wait_ge(wstep, 5)
            sp.wait_ge(zeroed, 1)
            for s in range(3):
                for i in range(4):
                    at = 32 * s + E * i
                    sp.dma_start(wl4[at:at + E, :, i // 2, i % 2, :],
                                 wsplit[s][at:at + E].rearrange("p (g o) -> p g o", g=NG)).then_inc(w_placed, 16)
            sp.wait_ge(w_placed, 192)

        @block.gpsimd
        def _(pool):
            pool.memset(wl, 0.0).then_inc(zeroed, 1)
            hi, mid, lo = wsplit
            pool.wait_ge(w_in, 192)
            pool.tensor_copy(hi, wf).then_inc(wstep, 1)
            pool.wait_ge(wstep, 1)
            pool.tensor_tensor(wf, wf, hi, ALU.subtract).then_inc(wstep, 1)
            pool.wait_ge(wstep, 2)
            pool.tensor_copy(mid, wf).then_inc(wstep, 1)
            pool.wait_ge(wstep, 3)
            pool.tensor_tensor(wf, wf, mid, ALU.subtract).then_inc(wstep, 1)
            pool.wait_ge(wstep, 4)
            pool.tensor_copy(lo, wf).then_inc(wstep, 1)

        @block.tensor
        def _(pe):
            pe.wait_ge(loaded, 64)
            for t in range(NT):
                last = pe.matmul(ps[:, 0, E * t:E * t + E], xT[:, P * t:P * t + P], pw, start=True, stop=True)
            last.then_inc(logits, 1)
            for t in range(NT):
                b = 1 + t % 3
                pe.wait_ge(made, t + 1)
                if t >= 3:
                    pe.wait_ge(kept, t - 2)
                pb = ps[:, b, :].bitcast(BF16)
                for q in range(NQ):
                    last = pe.transpose(pb[:, P * q:P * q + P], an[t % 2][:, P * q:P * q + P], identb[:])
                last.then_inc(turned, 1)

        @block.scalar
        def _(act):
            act.activation(sg3, xh3, ACT.Sign).then_inc(signs, 1)
            for t in range(NT):
                act.wait_ge(turned, t + 1)
                pb = ps[:, 1 + t % 3, :].bitcast(BF16)
                act.activation(aT[:, :, P * t:P * t + P], pb[:, 0:NQ * P].rearrange("p (q t) -> p q t", q=NQ),
                               ACT.Copy).then_inc(kept, 1)

        @block.vector
        def _(dve):
            dve.wait_ge(logits, 1)
            dve.tensor_scalar(gate, ps[:, 0, 0:NT * E], 0.0, None, ALU.is_gt).then_inc(gates, 1)
            dve.wait_ge(gates, 1)
            dve.wait_ge(signs, 1)
            for t in range(NT):
                if t >= 2:
                    dve.wait_ge(turned, t - 1)
                dve.tensor_tensor(an[t % 2].rearrange("p (i e) -> p i e", e=E),
                                  sg3[:, t, :].rearrange("p (i o) -> p i o", o=1).broadcast_to([P, IN, E]),
                                  g3[:, t, :].rearrange("p (o e) -> p o e", o=1).broadcast_to([P, IN, E]),
                                  ALU.mult).then_inc(made, 1)

    stacked, mixed = [sem(f"c_stacked_{q}") for q in range(3)], sem("c_mixed")
    sign_act, sign_dve, neg_made, summed, sum_made, sum_kept = (
        sem("c_" + s) for s in ("sign_act", "sign_dve", "neg_made", "summed", "sum_made", "sum_kept"))
    NCK, PR = N // CH, NP // 2
    Q = 3
    on_dve = [n % 3 == 2 for n in range(PR)]
    ND = sum(on_dve)
    NA = PR - ND
    sum_bank = (6, 7, 6)

    def ahead(n):
        return n - sum(on_dve[:n]), sum(on_dve[:n])

    def wait_signed(eng, ck, n):
        if on_dve[n]:
            eng.wait_ge(sign_dve, ND * ck + ahead(n)[1] + 1 + ND)
        else:
            eng.wait_ge(sign_act, NA * ck + ahead(n)[0] + 1 + NA)

    def wait_free(eng, ck, n):
        eng.wait_ge(summed, PR * ck + n - NS + 1 + PR)

    with nc.Block() as block:
        @block.sync
        def _(sp):
            with sp.Fori(0, NCK // Q) as k:
                for q in range(Q):
                    sp.wait_ge(mixed, PR * (Q * k + q) + PR)
                    settle(sp)
                    for s in range(3):
                        for r in range(4):
                            sp.dma_start(stack[q].rearrange("p (q r) t -> p q r t", r=4)[32 * s:32 * s + 32, :, r, :],
                                         aT[32 * r:32 * r + 32, :, bass.ds((Q * k + q) * CH, CH)]).then_inc(stacked[q], 16)

        @block.tensor
        def _(pe):
            pe.sem_inc(mixed, Q * PR)

            def mix(k, m_):
                q, n = m_ // PR, m_ % PR
                ck = Q * k + q
                if n == 0:
                    pe.wait_ge(stacked[q], 192 * (k + 1))
                wait_signed(pe, ck if n >= 3 else ck - 1, (n - 3) % PR)
                for f in range(2):
                    last = pe.matmul(ps[:, 2 * (m_ % 3) + f, 0:CH], wl[:, P * (2 * n + f):P * (2 * n + f) + P],
                                     stack[q][:, n, :], start=True, stop=True)
                last.then_inc(mixed, 1)

            def add(k, m_):
                q, n = m_ // PR, m_ % PR
                ck = Q * k + q
                if n == 0:
                    pe.wait_ge(sum_kept, ck + (2, 0, 1)[q])
                wait_signed(pe, ck, n)
                settle(pe)
                for f in range(2):
                    last = pe.matmul(ps[0:D, sum_bank[q], 0:CH], pair_sum, sgn[m_ % NS][:, f, :],
                                     start=(n == 0 and f == 0), stop=(n == PR - 1 and f == 1))
                last.then_inc(summed, 1)

            with pe.Fori(0, NCK // Q) as k:
                mix(k, 0)
                mix(k, 1)
                for m_ in range(Q * PR):
                    if m_ + 2 < Q * PR:
                        mix(k, m_ + 2)
                    add(k, m_)

        @block.scalar
        def _(act):
            act.sem_inc(sign_act, NA)
            act.sem_inc(summed, PR)
            act.sem_inc(sum_kept, 2)
            with act.Fori(0, NCK // Q) as k:
                for m_ in range(Q * PR):
                    q, n = m_ // PR, m_ % PR
                    if not on_dve[n]:
                        wait_free(act, Q * k + q, n)
                        act.wait_ge(mixed, PR * (Q * k + q) + n + 1 + Q * PR)
                        b0 = 2 * (m_ % 3)
                        act.activation(sgn[m_ % NS], ps[:, b0:b0 + 2, 0:CH], ACT.Sign).then_inc(sign_act, 1)

        @block.vector
        def _(dve):
            dve.sem_inc(sign_dve, ND)

            def keep(k, q):
                ck = Q * k + q
                dve.wait_ge(summed, PR * ck + PR + PR)
                dve.tensor_scalar(dT[:, bass.ds(ck * CH, CH)], ps[0:D, sum_bank[q], 0:CH], sc, None,
                                  ALU.mult).then_inc(sum_kept, 1)

            with dve.Fori(0, NCK // Q) as k:
                for m_ in range(Q * PR):
                    q, n = m_ // PR, m_ % PR
                    if on_dve[n]:
                        at = ND * (Q * k + q) + ahead(n)[1]
                        b0 = 2 * (m_ % 3)
                        src = ps[:, b0:b0 + 2, 0:CH]
                        dve.wait_ge(sign_dve, at + ND)
                        dve.wait_ge(mixed, PR * (Q * k + q) + n + 1 + Q * PR)
                        dve.tensor_scalar(neg, src, 0.0, None, ALU.is_lt).then_inc(neg_made, 1)
                        wait_free(dve, Q * k + q, n)
                        dve.wait_ge(neg_made, at + 1)
                        dve.scalar_tensor_tensor(sgn[m_ % NS], src, 0.0, neg, ALU.is_gt, ALU.subtract).then_inc(sign_dve, 1)
                    if n == 3 and q >= 1:
                        keep(k, q - 1)
                keep(k, Q - 1)


def retention(m):
    nc, a, c, sem, ps, dT, xT = (m[k] for k in ("nc", "a", "c", "sem", "ps", "dT", "xT"))
    ar = Arena(m["arena"])
    xb = [ar.take(D + 1, S) for _ in range(2)]
    q, k = [ar.take(D + 1, S) for _ in range(2)], [ar.take(D + 1, S) for _ in range(2)]
    v = [ar.take(P, SB * D) for _ in range(2)]
    decay = ar.take(P, S)
    NP = 4
    p = [ar.take(P, CH) for _ in range(NP)]
    w = ar.take(D + 1, 3 * D)
    wq, wk, wv = (w[:, D * i:D * i + D] for i in range(3))
    loaded, set_up, xb_in = sem("d_loaded"), sem("d_set_up"), sem("d_xb_in")
    prep, prep_kept, scores, decayed, summed, kept = (
        sem("d_" + s) for s in ("prep", "prep_kept", "scores", "decayed", "summed", "kept"))
    NTL = len(TILES)
    NPR = 8
    LAST_TILE = [max(n for n in range(NTL) if TILES[n][0] == ch) for ch in range(NCH)]

    with nc.Block() as block:
        @block.sync
        def _(sp):
            for dst, name in ((wq, "Wq"), (wk, "Wk"), (wv, "Wv")):
                sp.dma_start(dst[0:D], a["L1_attn_" + name]).then_inc(loaded, 16)
            sp.dma_start(decay, c["decay"]).then_inc(loaded, 16)

        @block.gpsimd
        def _(pool):
            for n in range(2):
                pool.tensor_copy(xb[n], xT[:, S * n:S * n + S]).then_inc(xb_in, 1)
            with pool.Fori(0, B // 2 - 1) as pair:
                for n in range(2):
                    b = 2 * pair
                    pool.wait_ge(prep, NPR * (b + n + 1))
                    settle(pool)
                    pool.tensor_copy(xb[n], xT[:, bass.ds((b + n + 2) * S, S)]).then_inc(xb_in, 1)

        @block.tensor
        def _(pe):
            pe.wait_ge(loaded, 64)
            pe.wait_ge(set_up, 5)

            def prepare(b, par, n):
                if n == 0:
                    pe.wait_ge(xb_in, b + 1)
                pe.wait_ge(prep_kept, NPR * b + n + 1)
                settle(pe)
                if n < 6:
                    ch = n % 3
                    last = pe.matmul(ps[0:D, 6 + n % 2, 0:CH], (wq, wk)[n // 3], xb[par][:, CH * ch:CH * ch + CH],
                                     start=True, stop=True)
                else:
                    for j in (range(8), range(8, SB))[n - 6]:
                        last = pe.matmul(ps[0:rows(j), 6 + n % 2, D * (j % 8):D * (j % 8) + D],
                                         xb[par][:, P * j:P * j + rows(j)], wv, start=True, stop=True)
                last.then_inc(prep, 1)

            def score(b, par, n):
                ch, j, lo, width = TILES[n]
                if n == 0:
                    pe.wait_ge(prep_kept, NPR * (b + 1) + 2)
                pe.wait_ge(decayed, NTL * b + n + 1)
                r = rows(j)
                pe.matmul(ps[0:r, (NTL * par + n) % 4, 0:width], k[par][:, P * j:P * j + r], q[par][:, lo:lo + width],
                          start=True, stop=True).then_inc(scores, 1)

            def weigh(b, par, n):
                ch, j, lo, width = TILES[n]
                pe.wait_ge(decayed, NTL * b + n + 1 + 4)
                if j == 0:
                    pe.wait_ge(kept, NCH * b + ch + 1)
                settle(pe)
                r, o = rows(j), lo - CH * ch
                pe.matmul(ps[0:D, 4 + (NCH * par + ch) % 2, o:o + width], v[par][0:r, D * j:D * j + D],
                          p[(NTL * par + n) % NP][0:r, 0:width], start=(j == 0), stop=n in LAST_TILE,
                          skip_group_check=True).then_inc(summed, 1)

            for n in range(NPR):
                prepare(0, 0, n)

            def batch(b, par, more):
                score(b, par, 0)
                score(b, par, 1)
                for n in range(NTL):
                    if n + 2 < NTL:
                        score(b, par, n + 2)
                    if more and 4 <= n < 4 + NPR:
                        prepare(b + 1, 1 - par, n - 4)
                    weigh(b, par, n)

            with pe.Fori(0, B // 2 - 1) as pair:
                batch(2 * pair, 0, True)
                batch(2 * pair + 1, 1, True)
            batch(B - 2, 0, True)
            batch(B - 1, 1, False)

        @block.scalar
        def _(act):
            act.sem_inc(prep_kept, 2)
            act.sem_inc(kept, 2)

            def prepare(b, par, n):
                act.wait_ge(prep, NPR * b + n + 1)
                src = ps[:, 6 + n % 2, :]
                if n < 6:
                    ch = n % 3
                    act.activation((q, k)[n // 3][par][0:D, CH * ch:CH * ch + CH], src[0:D, 0:CH], ACT.Copy).then_inc(prep_kept, 1)
                elif n == 6:
                    act.activation(v[par][:, 0:8 * D], src[:, 0:8 * D], ACT.Copy).then_inc(prep_kept, 1)
                else:
                    act.activation(v[par][0:rows(8), 8 * D:9 * D], src[0:rows(8), 0:D], ACT.Copy).then_inc(prep_kept, 1)

            def keep(b, par, ch):
                act.wait_ge(summed, NTL * b + LAST_TILE[ch] + 1 + 4)
                at = b * S + CH * ch
                dst = dT[:, at:at + CH] if isinstance(b, int) else dT[:, bass.ds(at, CH)]
                act.activation(dst, ps[0:D, 4 + (NCH * par + ch) % 2, 0:CH], ACT.Copy).then_inc(kept, 1)

            def batch(b, par, more):
                for n in range(NTL + 2):
                    if more and 4 <= n < 4 + NPR:
                        prepare(b + 1, 1 - par, n - 4)
                    for ch in range(NCH):
                        if n == LAST_TILE[ch] + 2:
                            keep(b, par, ch)

            for n in range(NPR):
                prepare(0, 0, n)
            with act.Fori(0, B // 2 - 1) as pair:
                batch(2 * pair, 0, True)
                batch(2 * pair + 1, 1, True)
            batch(B - 2, 0, True)
            batch(B - 1, 1, False)

        @block.vector
        def _(dve):
            dve.memset(w[D:D + 1, :], 0.0).then_inc(set_up, 1)
            for t in (*q, *k):
                dve.memset(t[D:D + 1, :], 0.0).then_inc(set_up, 1)
            dve.sem_inc(decayed, 4)
            dve.sem_inc(summed, 4)
            dve.wait_ge(loaded, 64)

            def batch(b, par):
                for n in range(NTL):
                    ch, j, lo, width = TILES[n]
                    r = rows(j)
                    i = (NTL * par + n) % 4
                    dve.wait_ge(scores, NTL * b + n + 1)
                    dve.wait_ge(summed, NTL * b + n + 1)
                    dve.tensor_tensor(p[i][0:r, 0:width], ps[0:r, i, 0:width], decay[0:r, lo - P * j:lo - P * j + width],
                                      ALU.mult).then_inc(decayed, 1)

            with dve.Fori(0, B // 2) as pair:
                batch(2 * pair, 0)
                batch(2 * pair + 1, 1)


def count_clamped(m):
    nc, a, sem, ps = (m[k] for k in ("nc", "a", "sem", "ps"))
    ar = Arena(m["arena"])
    keys, picked, cnt = m["keys"], m["picked"], m["cnt"]
    load, copy_in, products, gelus, credits = expert_chunks(m, m["outE"])
    NXC = NT // 3
    onehot = [ar.take(P, (LO + HI) * CB, BF16).rearrange("p (v e) -> p v e", e=CB) for _ in range(2)]
    digits = ar.take(P, 2 * EC, BF16)
    cnt64 = ar.take(LO, HI)
    zero = ar.take(P, LO + HI, BF16)
    zeroed = sem("e_zeroed")
    edges_in, made, counted, cnt_kept, cnt_in = (sem("e_" + s) for s in ("edges_in", "made", "counted", "cnt_kept", "cnt_in"))
    NB = EC // CB

    with nc.Block() as block:
        @block.sync
        def _(sp):
            sp.dma_start(digits, m["edge_digits"]).then_inc(edges_in, 16)
            sp.dma_start(picked, m["edge_picked"]).then_inc(edges_in, 16)
            sp.dma_start(keys, m["edge_keys"]).then_inc(edges_in, 16)
            load(sp)
            sp.wait_ge(cnt_kept, 1)
            for half in range(2):
                sp.dma_start(cnt[LO * half:LO * half + LO, :],
                             cnt64[:, NT * half:NT * half + NT]).then_inc(cnt_in, 16)
            sp.wait_ge(cnt_in, 32)
            sp.wait_ge(edges_in, 48)

        @block.vector
        def _(dve):
            dve.memset(zero, 0.0).then_inc(zeroed, 1)
            dve.wait_ge(edges_in, 48)
            dve.sem_inc(counted, 2)
            with dve.Fori(0, NB // 2) as pair:
                for b in range(2):
                    dve.wait_ge(counted, 2 * pair + b + 1)
                    for v in range(LO + HI):
                        which = v // LO if v < 2 * LO else 1
                        last = dve.tensor_scalar(onehot[b][:, v, :], digits[:, bass.ds((2 * pair + b) * CB + EC * which, CB)],
                                                 float(v - LO * which), None, ALU.is_equal)
                    last.then_inc(made, 1)
            dve.wait_ge(counted, NB + 2)
            dve.tensor_copy(cnt64.rearrange("p (f k) -> p k f", f=2),
                            ps[0:LO, 7, 0:HI].rearrange("p (k f) -> p k f", f=2)).then_inc(cnt_kept, 1)

        @block.tensor
        def _(pe):
            pe.wait_ge(zeroed, 1)
            pe.matmul(ps[0:LO, 7, 0:HI], zero[:, 0:LO], zero[:, LO:], start=True, stop=False, skip_group_check=True)
            with pe.Fori(0, NB // 2) as pair:
                products(pe, pair)
                for b in range(2):
                    pe.wait_ge(made, 2 * pair + b + 1)
                    settle(pe)
                    for e in range(CB):
                        last = pe.matmul(ps[0:LO, 7, 0:HI], onehot[b][:, 0:LO, e], onehot[b][:, LO:, e],
                                         start=False, stop=False, skip_group_check=True)
                    last.then_inc(counted, 1)
            with pe.Fori(NB // 2, NXC) as i:
                products(pe, i)

        @block.gpsimd
        def _(pool):
            with pool.Fori(0, NXC) as i:
                copy_in(pool, i)

        @block.scalar
        def _(act):
            credits(act)
            with act.Fori(0, NXC) as i:
                gelus(act, i)


def graph_experts(m):
    nc, a, sem, ps, xT, ident, h3 = (m[k] for k in ("nc", "a", "sem", "ps", "xT", "ident", "h3"))
    ctx = m["ctx"]
    full = Arena(m["arena"])
    m["outE"] = outE = full.take(P, NT * FE * D)
    m["keys"], m["picked"], m["cnt"] = full.take(P, EC), full.take(P, CAP), full.take(P, NT)
    base = full.at
    m_edges = dict(m, arena=m["arena"][:, base:])
    count_clamped(m_edges)
    keys, picked, cnt = m["keys"], m["picked"], m["cnt"]

    def k3(ap, **kw):
        return ap.rearrange("p (k c) -> p k c", **kw)

    ar = full
    nodes, dtab = k3(ar.take(P, NT * CHN), k=NT), k3(ar.take(P, NT * FE), k=NT)
    prod = k3(ar.take(P, NT * CHN), k=NT)
    own = k3(ar.take(P, NT * CHN), k=NT)
    bound, t1, t2 = (k3(ar.take(P, NT * FE), k=NT) for _ in range(3))
    lastrow, G4, G4p = ar.take(P, CHN), ar.take(P, FE), ar.take(P, FE)
    att_s, att_d, bg, gamma, beta = (ar.take(P, HE) for _ in range(5))
    b2 = ar.take(P, FE * D)
    wg = ar.take(D + 1, HE)
    loaded, gat, step, tab_out, last_in, gmax, gall, expd = (
        sem("f_" + s) for s in ("loaded", "gat", "step", "tab_out", "last_in", "gmax", "gall", "expd"))
    tab = nc.dram_tensor("node_table", [N, CHN], F32, kind="Internal").ap()
    bank2 = [(k // 32, k % 32) for k in range(NT)]

    def vec(name, n):
        src = a["L1_ffn_" + name]
        if len(src.shape) == 2:
            src = src.rearrange("h e -> (h e)")
        return src.rearrange("(o d) -> o d", o=1).broadcast_to([P, n])

    with nc.Block() as block:
        @block.sync
        def _(sp):
            sp.dma_start(wg[0:D], a["L1_ffn_W_gat"]).then_inc(loaded, 16)
            for dst, name in ((att_s, "att_src"), (att_d, "att_dst"), (bg, "b_gat"), (gamma, "ln_gamma"), (beta, "ln_beta")):
                sp.dma_start(dst, vec(name, HE)).then_inc(loaded, 16)
            sp.dma_start(b2, vec("b2", FE * D)).then_inc(loaded, 16)
            sp.wait_ge(step, 7)
            sp.dma_start(tab.rearrange("(k p) c -> p k c", p=P), nodes).then_inc(tab_out, 16)
            sp.wait_ge(tab_out, 16)
            sp.dma_start(lastrow, tab[N - 1:N, :].broadcast_to([P, CHN])).then_inc(last_in, 16)

        @block.tensor
        def _(pe):
            pe.wait_ge(loaded, 112)
            pe.wait_ge(step, 1)
            for k, (bk, i) in enumerate(bank2):
                last = pe.matmul(ps[:, bk, HE * i:HE * i + HE], xT[:, P * k:P * k + P], wg, start=True, stop=True)
            last.then_inc(gat, 1)

        @block.gpsimd
        def _(pool):
            pool.wait_ge(gmax, 1)
            pool.partition_all_reduce(G4, G4p, P, bass.bass_isa.ReduceOp.max).then_inc(gall, 1)

        @block.scalar
        def _(act):
            act.wait_ge(step, 15)
            act.activation(t1, t1, ACT.Exp).then_inc(expd, 1)
            act.activation(t2, t2, ACT.Exp).then_inc(expd, 1)

        @block.vector
        def _(dve):
            n = 0

            def chain(instruction):
                nonlocal n
                n += 1
                instruction.then_inc(step, 1)
                dve.wait_ge(step, n)

            def leaky(x):
                chain(dve.scalar_tensor_tensor(x, x, 0.2, x, ALU.mult, ALU.max))

            def per_head(ap):
                return ap.rearrange("p (o c) -> p o c", o=1).broadcast_to([P, NT, ap.shape[1]])

            def split(ap):
                return ap.rearrange("p k (h e) -> p k h e", e=FE)

            def spread(w):
                return w.rearrange("p k (h o) -> p k h o", o=1).broadcast_to([P, NT, FE, FE])

            chain(dve.memset(wg[D:D + 1], 0.0))
            dve.wait_ge(loaded, 112)
            dve.wait_ge(gat, 1)
            h16 = nodes[:, :, 0:HE]
            chain(dve.tensor_copy(nodes[:, 32:33, 0:HE], k3(ps[:, 1, 0:HE], k=1)))
            chain(dve.tensor_copy(nodes[:, 0:32, 0:HE], k3(ps[:, 0, :], k=32)))
            pr = prod[:, :, 0:HE]
            chain(dve.tensor_tensor(pr, h16, per_head(att_s), ALU.mult))
            chain(dve.tensor_reduce(nodes[:, :, HE:], split(pr), X, ALU.add))
            chain(dve.tensor_tensor(pr, h16, per_head(att_d), ALU.mult))
            chain(dve.tensor_reduce(dtab, split(pr), X, ALU.add))
            dve.tensor_reduce(G4p, nodes[:, :, HE:].rearrange("p k h -> p h k"), X, ALU.max).then_inc(gmax, 1)
            dve.wait_ge(gall, 1)
            chain(dve.tensor_tensor(bound, dtab, per_head(G4), ALU.add))
            leaky(bound)
            chain(dve.tensor_tensor(t1, nodes[:, :, HE:], dtab, ALU.add))
            leaky(t1)
            chain(dve.tensor_tensor(t1, t1, bound, ALU.subtract))
            dve.wait_ge(last_in, 16)
            chain(dve.tensor_tensor(t2, dtab, per_head(lastrow[:, HE:]), ALU.add))
            leaky(t2)
            chain(dve.tensor_tensor(t2, t2, bound, ALU.subtract))
            dve.wait_ge(expd, 2)
            chain(dve.tensor_tensor(t2, t2, cnt.rearrange("p (k o) -> p k o", o=1).broadcast_to([P, NT, FE]), ALU.mult))
            chain(dve.tensor_tensor(own[:, :, HE:], t1, t2, ALU.add))
            chain(dve.tensor_tensor(split(own[:, :, 0:HE]), split(h16), spread(t1), ALU.mult))
            last4 = per_head(lastrow[:, 0:HE]).rearrange("p k (h e) -> p k h e", e=FE)
            chain(dve.tensor_tensor(split(prod[:, :, 0:HE]), last4, spread(t2), ALU.mult))
            chain(dve.tensor_tensor(own[:, :, 0:HE], own[:, :, 0:HE], prod[:, :, 0:HE], ALU.add))

    gathered_columns(m, ar, tab, dtab, G4)

    pstep, pgate, fin, outd = sem("g_step"), sem("g_gate"), sem("g_fin"), sem("g_outd")
    sc = k3(ar.take(P, NT * FE), k=NT)
    rank = k3(ar.take(P, NT * FE), k=NT)
    one = [k3(ar.take(P, NT), k=NT) for _ in range(2)]
    ex = k3(ar.take(P, NT * FE), k=NT)
    o4 = outE.rearrange("p (k e d) -> p k e d", k=NT, e=FE)
    with nc.Block() as block:
        @block.scalar
        def _(act):
            act.wait_ge(pgate, 1)
            act.activation(one[1], one[1], ACT.Sqrt).then_inc(pgate, 1)
            act.wait_ge(pgate, 3)
            act.activation(ex, sc, ACT.Exp).then_inc(pgate, 1)

        @block.vector
        def _(dve):
            n = 0

            def chain(instruction):
                nonlocal n
                n += 1
                instruction.then_inc(pstep, 1)
                dve.wait_ge(pstep, n)

            def per_row(ap, c):
                return ap.broadcast_to([P, NT, c])

            def vecs(ap):
                return ap.rearrange("p (o c) -> p o c", o=1).broadcast_to([P, NT, ap.shape[1]])

            for b0, lo in ((0, 0), (1, NT // 2 + 1)):
                hi = (NT // 2 + 1, NT)[b0]
                chain(dve.tensor_tensor(own[:, lo:hi, :], own[:, lo:hi, :],
                                        ps[:, b0, 0:(hi - lo) * CHN].rearrange("p (k c) -> p k c", c=CHN), ALU.add))
            chain(dve.reciprocal(t1, own[:, :, HE:]))
            agg = prod[:, :, 0:HE]
            split4 = agg.rearrange("p k (h e) -> p k h e", e=FE)
            chain(dve.tensor_tensor(split4, own[:, :, 0:HE].rearrange("p k (h e) -> p k h e", e=FE),
                                    t1.rearrange("p k (h o) -> p k h o", o=1).broadcast_to([P, NT, FE, FE]), ALU.mult))
            chain(dve.tensor_tensor(agg, agg, vecs(bg), ALU.add))
            chain(dve.tensor_reduce(one[0], agg, X, ALU.add))
            chain(dve.tensor_scalar(one[0], one[0], 1.0 / HE, None, ALU.mult))
            chain(dve.tensor_tensor(agg, agg, per_row(one[0], HE), ALU.subtract))
            sq = own[:, :, 0:HE]
            chain(dve.tensor_tensor(sq, agg, agg, ALU.mult))
            chain(dve.tensor_reduce(one[1], sq, X, ALU.add))
            dve.tensor_scalar(one[1], one[1], 1.0 / HE, EPS, ALU.mult, ALU.add).then_inc(pgate, 1)
            dve.wait_ge(pgate, 2)
            chain(dve.reciprocal(one[0], one[1]))
            chain(dve.tensor_tensor(agg, agg, per_row(one[0], HE), ALU.mult))
            chain(dve.tensor_tensor(agg, agg, vecs(gamma), ALU.mult))
            chain(dve.tensor_tensor(agg, agg, vecs(beta), ALU.add))
            chain(dve.tensor_reduce(sc, agg.rearrange("p k (h e) -> p k e h", e=FE), X, ALU.add))
            chain(dve.tensor_scalar(sc, sc, 1.0 / FE, None, ALU.mult))
            for e in range(FE):
                chain(dve.memset(rank[:, :, e:e + 1], float(FE - 1 - e)))
            for i in range(FE):
                for j in range(i + 1, FE):
                    chain(dve.tensor_tensor(one[0], sc[:, :, i:i + 1], sc[:, :, j:j + 1], ALU.is_ge))
                    chain(dve.tensor_tensor(rank[:, :, j:j + 1], rank[:, :, j:j + 1], one[0], ALU.add))
                    chain(dve.tensor_tensor(rank[:, :, i:i + 1], rank[:, :, i:i + 1], one[0], ALU.subtract))
            chain(dve.tensor_reduce(one[0], sc, X, ALU.max))
            dve.tensor_tensor(sc, sc, per_row(one[0], FE), ALU.subtract).then_inc(pgate, 1)
            dve.wait_ge(pgate, 4)
            chain(dve.scalar_tensor_tensor(ex, rank, 1.5, ex, ALU.is_lt, ALU.mult))
            chain(dve.tensor_reduce(one[0], ex, X, ALU.add))
            chain(dve.reciprocal(one[1], one[0]))
            chain(dve.tensor_tensor(ex, ex, per_row(one[1], FE), ALU.mult))
            flat = outE.rearrange("p (k c) -> p k c", k=NT)
            chain(dve.tensor_tensor(flat, flat, vecs(b2), ALU.add))
            for e in range(FE):
                chain(dve.tensor_tensor(o4[:, :, e, :], o4[:, :, e, :], per_row(ex[:, :, e:e + 1], D), ALU.mult))
                chain(dve.tensor_tensor(h3, h3, o4[:, :, e, :], ALU.add))
            dve.sem_inc(fin, 1)

        @block.sync
        def _(sp):
            sp.wait_ge(fin, 1)
            sp.dma_start(a["out"].rearrange("b s d -> (b s) d").rearrange("(k p) d -> p k d", p=P), h3).then_inc(outd, 16)
            sp.wait_ge(outd, 16)


def gathered_columns(m, ar, tab, dtab, G4):
    nc, sem, ps, identb = (m[k] for k in ("nc", "sem", "ps", "identb"))
    picked, keys = m["picked"], m["keys"]

    def k3(ap, **kw):
        return ap.rearrange("p (k c) -> p k c", **kw)

    kint, klo, srci = (ar.take(P, CAP, I32) for _ in range(3))
    dlo, dhi, ta, tb, kf = (ar.take(P, CAP) for _ in range(5))
    dlob = ar.take(P, CAP, BF16)
    iota, iotab = ar.take(P, P), ar.take(P, P, BF16)
    iotai = ar.take(P, P, I32)
    idx = [ar.take(P, GC, I32) for _ in range(2)]
    rows_ = [k3(ar.take(P, GC * CHN), k=GC) for _ in range(2)]
    hot = k3(ar.take(P, GC * P, BF16), k=GC)
    hot32 = [k3(ar.take(P, GC * P), k=GC) for _ in range(2)]
    hotT = ar.take(P, GC * P, BF16)
    high = [k3(ar.take(P, GC * NT), k=GC) for _ in range(2)]
    dparts = [ar.take(P, NT * FE, BF16) for _ in range(3)]
    drest = ar.take(P, NT * FE)
    looked_up = ar.take(P, 4 * NT * FE).rearrange("p (c k f) -> p c k f", c=4, k=NT)
    dval, za, zb, wt = (k3(ar.take(P, GC * FE), k=GC) for _ in range(4))
    val = k3(ar.take(P, GC * CHN), k=GC)
    NQ = 4
    prod = [ar.take(P, NQ * NT * CHN).rearrange("p (c k f) -> p c k f", c=NQ, k=NT) for _ in range(2)]
    zero = ar.take(P, 330)
    QG = GC // NQ
    SPLIT = NT // 2 + 1
    flag = ar.take(P, 1)
    flagi = ar.take(P, 1, I32)
    rest = ar.take(P, 1)

    def chained(dve, s, base):
        n = 0

        def chain(instruction):
            nonlocal n
            n += 1
            instruction.then_inc(s, 1)
            dve.wait_ge(s, base + n)
        return chain

    DEC = 12 + NT

    def decode(chain, width, src):
        w = slice(0, width)
        chain(nc.vector.tensor_scalar(kf[:, w], src, float(-(544 << 14)), None, ALU.max))
        chain(nc.vector.tensor_copy(kint[:, w], kf[:, w]))
        chain(nc.vector.tensor_scalar(klo[:, w], kint[:, w], 7, None, ALU.arith_shift_right))
        chain(nc.vector.tensor_scalar(klo[:, w], klo[:, w], P - 1, None, ALU.bitwise_and))
        chain(nc.vector.tensor_copy(dlob[:, w], klo[:, w]))
        chain(nc.vector.tensor_scalar(klo[:, w], kint[:, w], 14, None, ALU.arith_shift_right))
        chain(nc.vector.tensor_scalar(ta[:, w], klo[:, w], 544.0, None, ALU.add))
        chain(nc.vector.tensor_scalar(dhi[:, w], ta[:, w], float(NT), None, ALU.is_ge))
        for v in range(2, NT):
            chain(nc.vector.scalar_tensor_tensor(dhi[:, w], ta[:, w], float(NT * v), dhi[:, w], ALU.is_ge, ALU.add))
        chain(nc.vector.scalar_tensor_tensor(ta[:, w], dhi[:, w], -float(NT), ta[:, w], ALU.mult, ALU.add))
        chain(nc.vector.tensor_scalar(klo[:, w], kint[:, w], P - 1, None, ALU.bitwise_and))
        chain(nc.vector.scalar_tensor_tensor(tb[:, w], ta[:, w], float(P), klo[:, w], ALU.mult, ALU.add))
        chain(nc.vector.tensor_copy(srci[:, w], tb[:, w]))
        chain(nc.vector.tensor_scalar(tb[:, w], src, NONE / 2, -1000.0, ALU.is_lt, ALU.mult))
        chain(nc.vector.tensor_tensor(dhi[:, w], dhi[:, w], tb[:, w], ALU.add))

    def signals(tag):
        names = ("decoded", "idx", "consumed", "hot", "step", "turned", "hotT_kept", "hot32_made", "looked",
                 "selected", "weighable", "weights", "products", "quads")
        s = {n: sem(f"{tag}_{n}") for n in names}
        s["gathered"] = [sem(f"{tag}_gathered_{i}") for i in range(2)]
        return s

    SELECT_AT = 1
    WEIGH_AT = SELECT_AT + 2 * QG
    STEPS = WEIGH_AT + 7


    def fetch(pool, s, g, par, j, at):
        pool.wait_ge(s["consumed"], g + 1)
        settle(pool)
        pool.tensor_copy(idx[par], srci[:, at]).then_inc(s["idx"], 1)
        pool.wait_ge(s["idx"], g + 1)
        settle(pool)
        for c in range(GC):
            pool.indirect_dma_start(rows_[par][:, c, :], None, tab, bass.IndirectOffsetOnAxis(ap=idx[par][:, c:c + 1], axis=0)).then_inc(s["gathered"][par], 16)

    def onehots(dve, s, g, par, at):
        def col(ap, c):
            return ap.rearrange("p (c o) -> p c o", o=1).broadcast_to([P, GC, c])

        dve.wait_ge(s["turned"], 2 * g + 2)
        dve.wait_ge(s["hot32_made"], g + 1)
        dve.tensor_tensor(hot, col(dlob[:, at], P), iotab.rearrange("p (o v) -> p o v", o=1).broadcast_to([P, GC, P]),
                          ALU.is_equal).then_inc(s["hot"], 1)
        dve.tensor_tensor(high[par], col(dhi[:, at], NT), iota[:, 0:NT].rearrange("p (o v) -> p o v", o=1).broadcast_to([P, GC, NT]),
                          ALU.is_equal).then_inc(s["step"], 1)
        dve.wait_ge(s["step"], STEPS * g + 1)

    def turn(pe, s, g):
        pe.wait_ge(s["hot"], g + 1)
        for i in range(2):
            pe.wait_ge(s["hotT_kept"], 2 * g + i + 1)
            settle(pe)
            pb = ps[:, 2 + i, :].bitcast(BF16)
            for c in range(8):
                last = pe.transpose(pb[:, P * c:P * c + P], hot[:, 8 * i + c, :], identb[:])
            last.then_inc(s["turned"], 1)

    def keep(act, s, g, par):
        for i in range(2):
            act.wait_ge(s["turned"], 2 * g + i + 1 + 2)
            act.wait_ge(s["looked"], QG * g + 2 * i + 2)
            act.activation(hotT[:, 8 * P * i:8 * P * i + 8 * P], ps[:, 2 + i, :].bitcast(BF16), ACT.Copy).then_inc(s["hotT_kept"], 1)
        act.wait_ge(s["hot"], g + 1)
        act.wait_ge(s["quads"], QG * g + QG)
        act.activation(hot32[par], hot, ACT.Copy).then_inc(s["hot32_made"], 1)

    def look(pe, s, g, q):
        pe.wait_ge(s["hotT_kept"], 2 * g + q // 2 + 1 + 2)
        pe.wait_ge(s["selected"], QG * g + q + 1)
        settle(pe)
        for c in range(NQ):
            for n, part in enumerate(dparts):
                last = pe.matmul(ps[:, 4 + 2 * (q % 2) + c // 2, 256 * (c % 2):256 * (c % 2) + NT * FE],
                                 hotT[:, P * (NQ * q + c):P * (NQ * q + c) + P], part, start=(n == 0), stop=(n == 2))
        last.then_inc(s["looked"], 1)

    def select(dve, s, g, par, q):
        b = 4 + 2 * (q % 2)
        cs = slice(NQ * q, NQ * q + NQ)
        chain = chained(dve, s["step"], STEPS * g + SELECT_AT + 2 * q)
        dve.wait_ge(s["looked"], QG * g + q + 1 + 4)
        src = ps[:, b:b + 2, :].rearrange("p b (c x) -> p (b c) x", c=2)[:, :, 0:NT * FE].rearrange("p c (k f) -> p c k f", f=FE)
        chain(dve.tensor_tensor(looked_up, src, high[par][:, cs, :].rearrange("p c (k o) -> p c k o", o=1).broadcast_to([P, NQ, NT, FE]), ALU.mult))
        dve.sem_inc(s["selected"], 1)
        chain(dve.tensor_reduce(dval[:, cs, :], looked_up.rearrange("p c k f -> p c f k"), X, ALU.add))

    def weigh(dve, s, g, par, j):
        chain = chained(dve, s["step"], STEPS * g + WEIGH_AT)
        dve.wait_ge(s["gathered"][par], 16 * GC * (j + 1))
        g4 = G4.rearrange("p (o v) -> p o v", o=1).broadcast_to([P, GC, FE])
        chain(dve.tensor_tensor(za, rows_[par][:, :, HE:], dval, ALU.add))
        chain(dve.scalar_tensor_tensor(za, za, 0.2, za, ALU.mult, ALU.max))
        chain(dve.tensor_tensor(zb, dval, g4, ALU.add))
        chain(dve.scalar_tensor_tensor(zb, zb, 0.2, zb, ALU.mult, ALU.max))
        chain(dve.tensor_tensor(za, za, zb, ALU.subtract))
        dve.sem_inc(s["weighable"], 1)
        dve.wait_ge(s["weights"], g + 1)
        dve.wait_ge(s["products"], QG * g + QG)
        chain(dve.tensor_copy(val[:, :, HE:], wt))
        chain(dve.tensor_tensor(val[:, :, 0:HE].rearrange("p c (h e) -> p c h e", e=FE),
                                rows_[par][:, :, 0:HE].rearrange("p c (h e) -> p c h e", e=FE),
                                wt.rearrange("p c (h o) -> p c h o", o=1).broadcast_to([P, GC, FE, FE]), ALU.mult))
        dve.sem_inc(s["consumed"], 1)

    def spread(dve, s, g, par, q):
        cs = slice(NQ * q, NQ * q + NQ)
        dve.wait_ge(s["quads"], QG * g + q - 1 + 2 * QG)
        dve.tensor_tensor(prod[q % 2], high[par][:, cs, :].rearrange("p c (k o) -> p c k o", o=1).broadcast_to([P, NQ, NT, CHN]),
                          val[:, cs, :].rearrange("p c (o f) -> p c o f", o=1).broadcast_to([P, NQ, NT, CHN]),
                          ALU.mult).then_inc(s["products"], 1)

    def exps(act, s, g):
        act.wait_ge(s["weighable"], g + 1)
        act.activation(wt, za, ACT.Exp).then_inc(s["weights"], 1)

    def add(pe, s, g, par, q):
        if q == 0:
            pe.wait_ge(s["hot32_made"], g + 1 + 1)
        pe.wait_ge(s["products"], QG * g + q + 1 + QG)
        settle(pe)
        for c in range(NQ):
            lhs = hot32[par][:, NQ * q + c, :]
            pe.matmul(ps[:, 0, 0:SPLIT * CHN], lhs, prod[q % 2][:, c, 0:SPLIT, :], start=False, stop=False, skip_group_check=True)
            last = pe.matmul(ps[:, 1, 0:(NT - SPLIT) * CHN], lhs, prod[q % 2][:, c, SPLIT:, :], start=False, stop=False, skip_group_check=True)
        last.then_inc(s["quads"], 1)

    def dve_credits(dve, s):
        dve.sem_inc(s["quads"], 2 * QG)
        dve.sem_inc(s["products"], QG)
        dve.sem_inc(s["selected"], 2)

    def act_credits(act, s):
        act.sem_inc(s["hot32_made"], 1)
        act.sem_inc(s["hotT_kept"], 2)
        act.sem_inc(s["turned"], 2)
        act.sem_inc(s["looked"], QG)

    S1 = signals("m")
    step, zeroed = sem("h_step"), sem("h_zeroed")
    GROUPS = CAP // GC

    def at(g):
        return slice(g * GC, g * GC + GC) if isinstance(g, int) else bass.ds(g * GC, GC)

    with nc.Block() as block:
        @block.gpsimd
        def _(pool):
            pool.iota(iotai, [[1, P]], base=0, channel_multiplier=0).then_inc(zeroed, 1)
            pool.sem_inc(S1["consumed"], 2)
            pool.wait_ge(S1["decoded"], 1)
            with pool.Fori(0, GROUPS // 2) as pair:
                for par in range(2):
                    g = 2 * pair + par
                    fetch(pool, S1, g, par, pair, at(g))

        @block.tensor
        def _(pe):
            pe.wait_ge(zeroed, 2)
            pe.matmul(ps[:, 0, 0:330], zero[:, 0:P], zero, start=True, stop=False, skip_group_check=True)
            pe.matmul(ps[:, 1, 0:330], zero[:, 0:P], zero, start=True, stop=False, skip_group_check=True)
            turn(pe, S1, 0)
            for q in range(QG):
                look(pe, S1, 0, q)

            def group(g, par, more):
                add(pe, S1, g, par, 0)
                if more:
                    turn(pe, S1, g + 1)
                add(pe, S1, g, par, 1)
                if more:
                    look(pe, S1, g + 1, 0)
                    look(pe, S1, g + 1, 1)
                add(pe, S1, g, par, 2)
                if more:
                    look(pe, S1, g + 1, 2)
                    look(pe, S1, g + 1, 3)
                add(pe, S1, g, par, 3)

            with pe.Fori(0, GROUPS // 2 - 1) as pair:
                group(2 * pair, 0, True)
                group(2 * pair + 1, 1, True)
            group(GROUPS - 2, 0, True)
            group(GROUPS - 1, 1, False)

        @block.scalar
        def _(act):
            act_credits(act, S1)
            keep(act, S1, 0, 0)
            exps(act, S1, 0)
            with act.Fori(0, GROUPS // 2 - 1) as pair:
                for par in range(2):
                    g = 2 * pair + par + 1
                    keep(act, S1, g, 1 - par)
                    exps(act, S1, g)
            keep(act, S1, GROUPS - 1, 1)
            exps(act, S1, GROUPS - 1)

        @block.vector
        def _(dve):
            dve_credits(dve, S1)
            dve.memset(zero, 0.0).then_inc(zeroed, 1)
            chain = chained(dve, step, 0)
            dve.wait_ge(zeroed, 2)
            chain(dve.tensor_copy(iota, iotai))
            chain(dve.tensor_copy(iotab, iotai))
            chain(dve.tensor_reduce(rest, keys, X, ALU.max))
            flat = dtab.rearrange("p k f -> p (k f)")
            chain(dve.tensor_copy(dparts[0], flat))
            chain(dve.tensor_tensor(drest, flat, dparts[0], ALU.subtract))
            chain(dve.tensor_copy(dparts[1], drest))
            chain(dve.tensor_tensor(drest, drest, dparts[1], ALU.subtract))
            chain(dve.tensor_copy(dparts[2], drest))
            decode(chain, CAP, picked)
            dve.sem_inc(S1["decoded"], 1)
            onehots(dve, S1, 0, 0, at(0))
            for q in range(QG):
                select(dve, S1, 0, 0, q)
            weigh(dve, S1, 0, 0, 0)

            def group(g, par, j, more):
                spread(dve, S1, g, par, 0)
                spread(dve, S1, g, par, 1)
                if more:
                    onehots(dve, S1, g + 1, 1 - par, at(g + 1))
                spread(dve, S1, g, par, 2)
                spread(dve, S1, g, par, 3)
                if more:
                    for q in range(QG):
                        select(dve, S1, g + 1, 1 - par, q)
                    weigh(dve, S1, g + 1, 1 - par, j + par)

            with dve.Fori(0, GROUPS // 2 - 1) as pair:
                group(2 * pair, 0, pair, True)
                group(2 * pair + 1, 1, pair, True)
            group(GROUPS - 2, 0, GROUPS // 2 - 1, True)
            group(GROUPS - 1, 1, GROUPS // 2 - 1, False)

    S2 = signals("r")
    all_left, flagged = sem("r_all_left"), sem("r_flagged")
    rstep, m8 = sem("r_keys"), ar.take(P, 8)
    ROUNDS = (EC - CAP) // GC
    ROUND_STEPS = DEC + 3 * (GC // 8)

    def any_left(eng):
        eng.wait_ge(flagged, 1)
        return eng.If(eng.value_load(flagi[0:1, 0:1], min_val=0, max_val=1) > 0)

    with nc.Block() as block:
        @block.gpsimd
        def _(pool):
            pool.partition_all_reduce(flag, rest, P, bass.bass_isa.ReduceOp.max).then_inc(all_left, 1)
            pool.sem_inc(S2["consumed"], 1)
            with any_left(pool):
                with pool.Fori(0, ROUNDS) as g:
                    pool.wait_ge(S2["decoded"], g + 1)
                    fetch(pool, S2, g, 0, g, at(0))

        @block.tensor
        def _(pe):
            with any_left(pe):
                with pe.Fori(0, ROUNDS) as g:
                    turn(pe, S2, g)
                    for q in range(QG):
                        look(pe, S2, g, q)
                    for q in range(QG):
                        add(pe, S2, g, 0, q)

        @block.scalar
        def _(act):
            act_credits(act, S2)
            with any_left(act):
                with act.Fori(0, ROUNDS) as g:
                    keep(act, S2, g, 0)
                    exps(act, S2, g)

        @block.vector
        def _(dve):
            dve_credits(dve, S2)
            dve.wait_ge(all_left, 1)
            dve.tensor_scalar(flagi, flag, NONE / 2, None, ALU.is_gt).then_inc(flagged, 1)
            with any_left(dve):
                with dve.Fori(0, ROUNDS) as g:
                    once = chained(dve, rstep, ROUND_STEPS * g)

                    def chain(instruction):
                        once(instruction)
                        settle(dve)

                    for q in range(GC // 8):
                        chain(dve.max(m8, keys))
                        chain(dve.tensor_copy(picked[:, 8 * q:8 * q + 8], m8))
                        chain(dve.match_replace(out=keys, in_to_replace=m8, in_values=keys, imm_value=NONE))
                    decode(chain, GC, picked[:, 0:GC])
                    dve.sem_inc(S2["decoded"], 1)
                    onehots(dve, S2, g, 0, at(0))
                    for q in range(QG):
                        select(dve, S2, g, 0, q)
                    weigh(dve, S2, g, 0, g)
                    for q in range(QG):
                        spread(dve, S2, g, 0, q)
                    dve.wait_ge(S2["quads"], QG * g + QG + 2 * QG)
                    settle(dve)


def expert_chunks(m, outE):
    a, sem, ps, xT = (m[k] for k in ("a", "sem", "ps", "xT"))
    wa = Arena(m["weights"])
    w1, w2 = wa.take(D + 1, FE * P), wa.take(P, FE * D)
    hh = [wa.take(P, 3 * P) for _ in range(2)]
    xc = m["xhat"][0:D + 1, 0:3 * P]
    w_in, xc_in, hid, gel, used, outm, outk = (sem("x_" + s) for s in ("w_in", "xc_in", "hid", "gel", "used", "outm", "outk"))
    out3 = outE.rearrange("p (k c) -> p k c", k=NT)

    def load(sp):
        sp.dma_start(w1[0:D].rearrange("p (e f) -> p e f", e=FE), a["L1_ffn_W1"].rearrange("e d f -> d e f")).then_inc(w_in, 16)
        sp.dma_start(w1[D:D + 1], a["L1_ffn_b1"].rearrange("e f -> (e f)").rearrange("(o d) -> o d", o=1)).then_inc(w_in, 16)
        sp.dma_start(w2.rearrange("p (e d) -> p e d", e=FE), a["L1_ffn_W2"].rearrange("e f d -> f e d")).then_inc(w_in, 16)

    def copy_in(pool, i):
        pool.wait_ge(outm, i + 1)
        settle(pool)
        pool.tensor_copy(xc, xT[:, bass.ds(i * 3 * P, 3 * P)]).then_inc(xc_in, 1)

    def products(pe, i):
        pe.wait_ge(w_in, 48)
        pe.wait_ge(xc_in, i + 1)
        settle(pe)

        def hidden(e):
            if e >= 2:
                pe.wait_ge(gel, FE * i + e - 1)
                settle(pe)
            pe.matmul(ps[:, 2 + e % 2, 0:3 * P], w1[:, P * e:P * e + P], xc, start=True, stop=True).then_inc(hid, 1)

        def project(e):
            pe.wait_ge(gel, FE * i + e + 1)
            if e == 0:
                pe.wait_ge(outk, i + 1)
            settle(pe)
            for t in range(3):
                last = pe.matmul(ps[:, 4 + t // 2, 256 * (t % 2) + D * e:256 * (t % 2) + D * e + D],
                                 hh[e % 2][:, P * t:P * t + P], w2[:, D * e:D * e + D], start=True, stop=True)
            last.then_inc(outm if e == FE - 1 else used, 1)

        hidden(0)
        hidden(1)
        for e in range(FE):
            if e + 2 < FE:
                hidden(e + 2)
            project(e)

    def gelus(act, i):
        for e in range(FE):
            act.wait_ge(hid, FE * i + e + 1)
            if e >= 2:
                act.wait_ge(used, (FE - 1) * i + e - 1)
            act.activation(hh[e % 2], ps[:, 2 + e % 2, 0:3 * P], ACT.Gelu).then_inc(gel, 1)
        act.wait_ge(outm, i + 2)
        act.activation(out3[:, bass.ds(i * 3, 3), :],
                       ps[:, 4:6, :].rearrange("p b (t c) -> p (b t) c", t=2)[:, 0:3, :], ACT.Copy).then_inc(outk, 1)

    def credits(act):
        act.sem_inc(outm, 1)
        act.sem_inc(outk, 1)

    return load, copy_in, products, gelus, credits


_TRANSPOSED = ("L1_attn_Wq", "L1_attn_Wk", "L1_attn_Wv", "L0_ffn_proj_w")


def tables():
    bf = mybir.dt.np(BF16)
    i = np.arange(P)
    out = {"ident": np.eye(P, dtype=np.float32), "identb": np.eye(P, dtype=bf)}
    later = i[None, :] > i[:, None]
    out["mask_kq"] = np.where(later.T, MASKED, 0.0).astype(bf)
    out["mask_qk"] = np.where(later, MASKED, 0.0).astype(bf)
    s = np.arange(SP_)
    slopes = 0.5 ** np.arange(1, HEADS + 1)
    hi, lo = s // 32 * 32, s % 32
    one = np.ones(SP_)
    out["bias_k"] = np.stack([np.stack([f * hi, f * lo, one, one, one, one]) for f in slopes], 1).astype(bf)
    out["bias_q"] = np.stack([np.stack([one, one, -f * hi, -f * lo]) for f in slopes], 1).astype(bf)
    d = np.arange(S)[None, :] - i[:, None]
    decay = np.exp(d.astype(np.float32) * np.log(np.float32(GAMMA)))
    out["decay"] = np.where(d >= 0, decay, 0.0).astype(np.float32)
    pair = np.zeros((P, D), bf)
    pair[i, i % D] = 1
    out["pair_sum"] = pair
    row = np.zeros((P, P), bf)
    row[:] = i.astype(bf)
    out["count_row"] = row
    return out


def kernel(**inputs):
    import concourse.bacc as _bacc
    from concourse.bass_utils import run_bass_kernel_spmd as _run

    nc = _bacc.Bacc("TRN2", target_bir_lowering=False, num_devices=1)
    arrays, a, c = {}, {}, {}

    def give(name, x):
        arrays[name] = x
        return nc.dram_tensor(name, x.shape, mybir.dt.from_np(x.dtype), kind="ExternalInput").ap()

    for name, x in inputs.items():
        x = np.asarray(x)
        if name in _TRANSPOSED:
            x = x.T
        a[name] = give(f"in_{name}", np.ascontiguousarray(x).reshape(x.shape or (1,)))
    for name, x in tables().items():
        c[name] = give(f"table_{name}", x)
    a["out"] = nc.dram_tensor("out_h", (B, S, D), F32, kind="ExternalOutput").ap()
    build(nc, a, c)
    r = _run(nc, [arrays], core_ids=[0])
    return r.results[0]["out_h"]
```

```python
from contextlib import ExitStack

import numpy as np

import concourse.bass as bass
from concourse import mybir

F32 = mybir.dt.float32
BF16 = mybir.dt.bfloat16
I32 = mybir.dt.int32
ALU = mybir.AluOpType
ACT = mybir.ActivationFunctionType
X = mybir.AxisListType.X

B, T, TXT, D = 4, 1024, 32, 64
S = T + TXT
N = B * S
P = 128
NT = N // P
CH = 352
NCH = S // CH
HEADS, HD = 8, 32
GH = 4
SB = (S + P - 1) // P
SP_ = SB * P
GAMMA = 0.96875
EPS = 1e-5
MASKED = -1e30
N_EDGES = 262144
EC = N_EDGES // P
FE = 4
HE = FE * FE
CHN = HE + FE
GC = 16
CAP = 160
LO, HI = 64, N // 64
CB = 128
NONE = -1e9
NXC = NT // 3


def rows(j):
    return min(P, S - P * j)


TILES = [(c, j, max(CH * c, P * j), CH * (c + 1) - max(CH * c, P * j))
         for c in range(NCH) for j in range(SB) if P * j < CH * (c + 1)]


def settle(eng):
    eng.nop(nofuse=True)


class Arena:

    def __init__(self, tensor):
        self.tensor, self.at = tensor, 0

    def take(self, parts, cols, dtype=F32):
        words = cols if dtype != BF16 else (cols + 1) // 2
        words = (words + 7) // 8 * 8
        ap = self.tensor[0:parts, self.at:self.at + words]
        self.at += words
        assert self.at <= self.tensor.shape[1], self.at
        if dtype != F32:
            ap = ap.bitcast(dtype)
        return ap[:, 0:cols]


def build(nc, a, c):
    ctx = ExitStack()

    def sem(name):
        return ctx.enter_context(nc.semaphore(name))

    def sbuf(name, parts, cols, dtype=F32):
        return ctx.enter_context(nc.sbuf_tensor(name, [parts, cols], dtype))

    ident = sbuf("ident", P, P)
    identb = sbuf("identb", P, P, BF16)
    h = sbuf("h", P, NT * D)
    xhat = sbuf("xhat", P, NT * D)
    xT = sbuf("xT", D + 1, N)
    dT = sbuf("dT", D, N)
    stats = sbuf("stats", P, 4 * NT)
    weights = sbuf("weights", P, 2048)
    arena = sbuf("arena", P, 37800)
    ps = ctx.enter_context(nc.psum_tensor("ps", [P, 8, 512], F32))
    h3 = h[:].rearrange("p (k d) -> p k d", d=D)
    xh3 = xhat[:].rearrange("p (k d) -> p k d", d=D)

    edge_keys = nc.dram_tensor("edge_keys", [P, EC], F32, kind="Internal").ap()
    edge_picked = nc.dram_tensor("edge_picked", [P, CAP], F32, kind="Internal").ap()
    edge_digits = nc.dram_tensor("edge_digits", [P, 2 * EC], BF16, kind="Internal").ap()
    m = dict(edge_keys=edge_keys, edge_picked=edge_picked, edge_digits=edge_digits, h=h, xhat=xhat, nc=nc, a=a, c=c, sem=sem, ident=ident, identb=identb, h3=h3, xh3=xh3, xT=xT, dT=dT,
             stats=stats, weights=weights, arena=arena, ps=ps, ctx=ctx)
    with ctx:
        gated_attention(m)
        softmax_attention(m)
        binary_experts(m)
        retention(m)
        graph_experts(m)


def gated_attention(m):
    nc, a, sem, ps, dT, ident = m["nc"], m["a"], m["sem"], m["ps"], m["dT"], m["ident"]
    ar = Arena(m["arena"])
    NB = T // P
    TH = 512
    gn = ar.take(P, NB * T)
    gT = ar.take(P, NB * T)
    xn = ar.take(P, NB * D)
    xb = ar.take(D + 1, T)
    q, k = ar.take(D + 1, T), ar.take(D + 1, T)
    v = ar.take(P, NB * D)
    NP = 4
    p = [ar.take(P, TH) for _ in range(NP)]
    ret = [ar.take(D + 1, TH) for _ in range(2)]
    y = ar.take(D, TH)
    yn = ar.take(D, TH)
    txt = ar.take(P, D)
    keys, picked, m8 = ar.take(P, EC), ar.take(P, CAP), ar.take(P, 8)
    src, dst, shi, dhi = (ar.take(P, EC, I32) for _ in range(4))
    digits = ar.take(P, 2 * EC, BF16)
    near, tmp = m["h"][:, 0:EC], m["xhat"][:, 0:EC]
    edges_in, edge_step, sort_step, edges_out = (sem("a_" + s) for s in ("edges_in", "edge_step", "sort_step", "edges_out"))
    RB = CAP // 8 // B
    w = m["weights"]
    wq, wk, wv, wo = (w[0:D + 1, D * i:D * i + D] for i in range(4))
    bo, pa = w[0:D, 4 * D:4 * D + 1], w[0:D, 4 * D + 1:4 * D + 2]
    ident_in, loaded, gamma_in, x_in = sem("a_ident_in"), sem("a_loaded"), [sem(f"a_gamma_in_{i}") for i in range(2)], sem("a_x_in")
    ones = sem("a_ones")
    g_turned, g_kept, t_turned, t_kept = sem("a_g_turned"), sem("a_g_kept"), sem("a_t_turned"), sem("a_t_kept")
    prep, prep_slots = sem("a_prep"), sem("a_prep_slots")
    scores, gated, summed = sem("a_scores"), sem("a_gated"), sem("a_summed")
    ret_kept, y_made, y_kept, y_step = sem("a_ret_kept"), sem("a_y_made"), sem("a_y_kept"), sem("a_y_step")
    g3 = gn.rearrange("p (k t) -> p k t", k=NB)
    gT3 = gT.rearrange("p (k t) -> p k t", k=NB)
    v3 = v.rearrange("p (k d) -> p k d", k=NB)
    EDGE_STEPS = 16

    with nc.Block() as block:
        @block.sync
        def _(sp):
            sp.dma_start(ident[:], m["c"]["ident"]).then_inc(ident_in, 16)
            sp.dma_start(m["identb"][:], m["c"]["identb"]).then_inc(ident_in, 16)
            e = a["L1_ffn_edge_index"].rearrange("s (p e) -> s p e", p=P)
            sp.dma_start(src, e[0]).then_inc(edges_in, 16)
            sp.dma_start(dst, e[1]).then_inc(edges_in, 16)
            gsrc = a["L0_tok_d_gamma_batched"].rearrange("(k p) s -> p k s", p=P)
            for n in range(4):
                sp.dma_start(g3[:, 2 * n:2 * n + 2, :], gsrc[:, 2 * n:2 * n + 2, :]).then_inc(gamma_in[n // 2], 16)
            for wt, name, bias in ((wq, "L0_tok_Wq", "L0_tok_bq"), (wk, "L0_tok_Wk", "L0_tok_bk"),
                                    (wv, "L0_tok_Wv", "L0_tok_bv")):
                sp.dma_start(wt[0:D], a[name]).then_inc(loaded, 16)
                sp.dma_start(wt[D:D + 1], a[bias].rearrange("(o d) -> o d", o=1)).then_inc(loaded, 16)
            sp.dma_start(wo[0:D], a["L0_tok_Wo"]).then_inc(loaded, 16)
            sp.dma_start(bo, a["L0_tok_bo"].rearrange("(d o) -> d o", o=1)).then_inc(loaded, 16)
            sp.dma_start(pa, a["L0_tok_prelu_a"].rearrange("(o d) -> o d", o=1).broadcast_to([D, 1])).then_inc(loaded, 16)
            sp.dma_start(txt, a["txt"].rearrange("b t d -> (b t) d")).then_inc(loaded, 16)
            xsrc = a["x"].rearrange("b o (k p) d -> b p (o k) d", p=P)
            with sp.Fori(0, B) as b:
                sp.wait_ge(prep, 8 * b + 1)
                settle(sp)
                sp.dma_start(xn.rearrange("p (k d) -> p k d", k=NB),
                             xsrc[bass.ds(b, 1)].rearrange("b p k d -> p (b k) d")).then_inc(x_in, 16)
            sp.wait_ge(edge_step, EDGE_STEPS)
            sp.wait_ge(sort_step, 3 * RB * B)
            sp.dma_start(m["edge_digits"], digits).then_inc(edges_out, 16)
            sp.dma_start(m["edge_keys"], keys).then_inc(edges_out, 16)
            sp.dma_start(m["edge_picked"], picked).then_inc(edges_out, 16)
            sp.wait_ge(edges_out, 48)

        @block.tensor
        def _(pe):
            pe.sem_inc(prep, 1)
            pe.wait_ge(ident_in, 32)
            for n in range(2 * NB):
                j, th = n % NB, n // NB
                pe.wait_ge(gamma_in[th], 32)
                if n >= 4:
                    pe.wait_ge(g_kept, n - 3)
                for i in range(4):
                    last = pe.transpose(ps[:, n % 4, P * i:P * i + P], g3[:, 4 * th + i, P * j:P * j + P], ident[:])
                last.then_inc(g_turned, 1)
            pe.wait_ge(loaded, 16 * 10)
            pe.transpose(ps[0:D, 7, 0:P], txt, ident[:]).then_inc(t_turned, 1)
            pe.wait_ge(g_kept, 2 * NB)
            pe.wait_ge(t_kept, 1)
            pe.wait_ge(ones, 6)
            with pe.Fori(0, B) as b:
                pe.wait_ge(x_in, 16 * b + 16)
                for n in range(2):
                    pe.wait_ge(prep_slots, 8 * b + n + 1)
                    settle(pe)
                    for i in range(4):
                        last = pe.transpose(ps[0:D, 6 + n, P * i:P * i + P], xn[:, D * (4 * n + i):D * (4 * n + i) + D], ident[:])
                    last.then_inc(prep, 1)
                pe.wait_ge(prep_slots, 8 * b + 2 + 2)
                for n in range(2, 6):
                    pe.wait_ge(prep_slots, 8 * b + n + 1)
                    wt, th = (wq, wk)[(n - 2) // 2], n % 2
                    pe.matmul(ps[0:D, 6 + n % 2, :], wt, xb[:, TH * th:TH * th + TH], start=True, stop=True).then_inc(prep, 1)
                for n in range(6, 8):
                    pe.wait_ge(prep_slots, 8 * b + n + 1)
                    for i in range(4):
                        j = 4 * (n - 6) + i
                        last = pe.matmul(ps[:, 6 + n % 2, D * i:D * i + D], xb[:, P * j:P * j + P], wv, start=True, stop=True)
                    last.then_inc(prep, 1)
                pe.wait_ge(prep_slots, 8 * b + 8 + 2)

                def score(n):
                    th, j = n // NB, n % NB
                    pe.wait_ge(gated, 16 * b + n + 1)
                    pe.matmul(ps[:, n % 4, :], k[:, P * j:P * j + P], q[:, TH * th:TH * th + TH],
                              start=True, stop=True).then_inc(scores, 1)

                def weigh(n):
                    th, j = n // NB, n % NB
                    pe.wait_ge(gated, 16 * b + n + 1 + 4)
                    if j == 0:
                        pe.wait_ge(y_kept, 2 * b + th + 1)
                    pe.matmul(ps[0:D, 4 + th, :], v3[:, j, :], p[n % NP], start=(j == 0), stop=(j == NB - 1)).then_inc(summed, 1)

                def project(th):
                    pe.wait_ge(ret_kept, 2 * b + th + 1)
                    settle(pe)
                    pe.matmul(ps[0:D, 4 + th, :], wo, ret[th], start=True, stop=True).then_inc(y_made, 1)

                score(0)
                score(1)
                for n in range(2 * NB):
                    if n + 2 < 2 * NB:
                        score(n + 2)
                    weigh(n)
                    if n == NB + 1:
                        project(0)
                project(1)

        @block.scalar
        def _(act):
            for n in range(2 * NB):
                j, th = n % NB, n // NB
                act.wait_ge(g_turned, n + 1)
                act.activation(gT3[:, j, TH * th:TH * th + TH], ps[:, n % 4, :], ACT.Copy).then_inc(g_kept, 1)
            act.wait_ge(t_turned, 1)
            for b in range(B):
                last = act.activation(dT[:, S * b + T:S * b + S], ps[0:D, 7, TXT * b:TXT * b + TXT], ACT.Copy)
            last.then_inc(t_kept, 1)
            act.sem_inc(prep_slots, 2)
            with act.Fori(0, B) as b:
                for n in range(8):
                    act.wait_ge(prep, 8 * b + n + 1 + 1)
                    bank = ps[:, 6 + n % 2, :]
                    if n < 2:
                        dst, src = xb[0:D, TH * n:TH * n + TH], bank[0:D]
                    elif n < 6:
                        dst, src = (q, k)[(n - 2) // 2][0:D, TH * (n % 2):TH * (n % 2) + TH], bank[0:D]
                    else:
                        dst, src = v[:, 4 * D * (n - 6):4 * D * (n - 6) + 4 * D], bank[:, 0:4 * D]
                    act.activation(dst, src, ACT.Copy).then_inc(prep_slots, 1)
                for th in range(2):
                    act.wait_ge(summed, 16 * b + NB * (th + 1) + 4)
                    act.activation(ret[th][0:D], ps[0:D, 4 + th, :], ACT.Copy).then_inc(ret_kept, 1)

        @block.vector
        def _(dve):
            dve.memset(xb[D:D + 1, :], 1.0).then_inc(ones, 1)
            for t in (q, k, *ret, wo):
                dve.memset(t[D:D + 1, :], 0.0).then_inc(ones, 1)
            dve.sem_inc(gated, 4)
            dve.sem_inc(summed, 4)
            dve.sem_inc(y_kept, 2)
            n = 0

            def chain(instruction):
                nonlocal n
                n += 1
                instruction.then_inc(edge_step, 1)
                dve.wait_ge(edge_step, n)

            dve.wait_ge(edges_in, 32)
            chain(dve.tensor_scalar(shi, src, 7, None, ALU.arith_shift_right))
            chain(dve.tensor_scalar(dhi, dst, 7, None, ALU.arith_shift_right))
            chain(dve.tensor_scalar(keys, dhi, float(32 << 14), float(-(544 << 14)), ALU.mult, ALU.add))
            chain(dve.scalar_tensor_tensor(keys, shi, float((1 << 14) - P), keys, ALU.mult, ALU.add))
            chain(dve.scalar_tensor_tensor(keys, dst, float(P), keys, ALU.mult, ALU.add))
            chain(dve.tensor_tensor(keys, src, keys, ALU.add))
            chain(dve.tensor_scalar(tmp, dst, float(N), None, ALU.is_lt))
            chain(dve.scalar_tensor_tensor(near, src, float(N - 1), tmp, ALU.is_lt, ALU.mult))
            chain(dve.tensor_tensor(keys, keys, near, ALU.mult))
            chain(dve.tensor_scalar(tmp, near, -NONE, NONE, ALU.mult, ALU.add))
            chain(dve.tensor_tensor(keys, keys, tmp, ALU.add))
            chain(dve.tensor_scalar(dhi, dst, 6, None, ALU.arith_shift_right))
            chain(dve.tensor_scalar(tmp, src, float(N - 1), 100.0, ALU.is_lt, ALU.mult))
            chain(dve.tensor_tensor(digits[:, EC:], dhi, tmp, ALU.max))
            chain(dve.tensor_scalar(dhi, dst, LO - 1, None, ALU.bitwise_and))
            chain(dve.tensor_copy(digits[:, 0:EC], dhi))
            assert n == EDGE_STEPS, n
            with dve.Fori(0, B) as b:
                def finish(th):
                    n = 3 * (2 * b + th)
                    dve.wait_ge(y_made, 2 * b + th + 1)
                    dve.tensor_scalar(y, ps[0:D, 4 + th, :], bo, None, ALU.add).then_inc(y_step, 1)
                    dve.wait_ge(y_step, n + 1)
                    dve.tensor_scalar(yn, y, 0.0, pa, ALU.min, ALU.mult).then_inc(y_step, 1)
                    dve.wait_ge(y_step, n + 2)
                    dve.scalar_tensor_tensor(dT[:, bass.ds(b * S + TH * th, TH)], y, 0.0, yn, ALU.max, ALU.add).then_inc(y_step, 1)
                    dve.wait_ge(y_step, n + 3)
                    dve.sem_inc(y_kept, 1)

                def sort(n):
                    r, part = n // 3, n % 3
                    if r >= RB:
                        return
                    done = 3 * RB * b + 3 * r + part
                    if part == 0:
                        if r > 0:
                            dve.wait_ge(sort_step, done)
                            settle(dve)
                        dve.max(m8, keys).then_inc(sort_step, 1)
                    elif part == 1:
                        dve.wait_ge(sort_step, done)
                        dve.tensor_copy(picked[:, bass.ds(8 * RB * b + 8 * r, 8)], m8).then_inc(sort_step, 1)
                    else:
                        dve.wait_ge(sort_step, done)
                        settle(dve)
                        dve.match_replace(out=keys, in_to_replace=m8, in_values=keys, imm_value=NONE).then_inc(sort_step, 1)

                for n in range(2 * NB):
                    th, j = n // NB, n % NB
                    dve.wait_ge(scores, 16 * b + n + 1)
                    dve.wait_ge(summed, 16 * b + n + 1)
                    dve.tensor_tensor(p[n % NP], ps[:, n % 4, :], gT3[:, j, TH * th:TH * th + TH], ALU.mult).then_inc(gated, 1)
                    sort(n)
                    if n == NB + 3:
                        finish(0)
                finish(1)


def norm(m, r, loads):
    nc, sem, ps, dT, ident, h3, xh3, xT = (m[k] for k in ("nc", "sem", "ps", "dT", "ident", "h3", "xh3", "xT"))
    sums, var, rstd = (m["stats"][:, NT * i:NT * i + NT] for i in range(3))
    sq = m["arena"][:, 0:NT * D].rearrange("p (k d) -> p k d", d=D)
    if "norm_sems" not in m:
        m["norm_sems"] = [sem(f"n_{s}") for s in ("turned", "step", "squared", "root", "back", "kept")]
    turned, step, squared, root, back, kept = m["norm_sems"]
    groups = [range(8 * g, min(8 * g + 8, NT)) for g in range((NT + 7) // 8)]
    quads = [range(4 * g, min(4 * g + 4, NT)) for g in range((NT + 3) // 4)]
    NG, NQ = len(groups), len(quads)
    MID = 16
    halves = [slice(0, MID), slice(MID, NT)]
    STEPS = NG + 14
    s0 = STEPS * r

    with nc.Block() as block:
        @block.sync
        def _(sp):
            loads(sp)

        @block.tensor
        def _(pe):
            for g, tiles in enumerate(groups):
                for i, t in enumerate(tiles):
                    last = pe.transpose(ps[:, g, D * i:D * i + D], dT[:, P * t:P * t + P], ident[0:D, 0:D])
                last.then_inc(turned, 1)
            for g, tiles in enumerate(quads):
                pe.wait_ge(step, s0 + STEPS - (2 if tiles[-1] < MID else 0))
                if g >= 3:
                    pe.wait_ge(kept, NQ * r + g - 2)
                for i, t in enumerate(tiles):
                    last = pe.transpose(ps[0:D, 5 + g % 3, P * i:P * i + P], xh3[:, t, :], ident[:])
                last.then_inc(back, 1)

        @block.vector
        def _(dve):
            for g, tiles in enumerate(groups):
                lo, hi = tiles[0], tiles[-1] + 1
                dve.wait_ge(turned, NG * r + g + 1)
                src = ps[:, g, 0:D * (hi - lo)].rearrange("p (k d) -> p k d", d=D)
                if r == 0:
                    dve.tensor_copy(h3[:, lo:hi, :], src).then_inc(step, 1)
                else:
                    dve.tensor_tensor(h3[:, lo:hi, :], h3[:, lo:hi, :], src, ALU.add).then_inc(step, 1)
            if r == 0:
                dve.memset(xT[D:D + 1, :], 1.0)
            n = s0 + NG
            dve.wait_ge(step, n)

            def chain(instruction):
                nonlocal n
                n += 1
                instruction.then_inc(step, 1)
                dve.wait_ge(step, n)

            def wide(ap, k):
                return ap[:, k].rearrange("p (k o) -> p k o", o=1).broadcast_to([P, k.stop - k.start, D])

            for k in halves:
                chain(dve.tensor_reduce(sums[:, k], h3[:, k, :], X, ALU.add))
                chain(dve.tensor_scalar(sums[:, k], sums[:, k], 1.0 / D, None, ALU.mult))
                chain(dve.tensor_tensor(xh3[:, k, :], h3[:, k, :], wide(sums, k), ALU.subtract))
            for i, k in enumerate(halves):
                dve.wait_ge(squared, 2 * r + i + 1)
                chain(dve.tensor_reduce(var[:, k], sq[:, k, :], X, ALU.add))
                chain(dve.tensor_scalar(var[:, k], var[:, k], 1.0 / D, EPS, ALU.mult, ALU.add))
            for i, k in enumerate(halves):
                dve.wait_ge(root, 2 * r + i + 1)
                chain(dve.reciprocal(rstd[:, k], rstd[:, k]))
                chain(dve.tensor_tensor(xh3[:, k, :], xh3[:, k, :], wide(rstd, k), ALU.mult))
            assert n == s0 + STEPS, n

        @block.scalar
        def _(act):
            for i, k in enumerate(halves):
                act.wait_ge(step, s0 + NG + 3 * (i + 1))
                act.activation(sq[:, k, :], xh3[:, k, :], ACT.Square).then_inc(squared, 1)
            for i, k in enumerate(halves):
                act.wait_ge(step, s0 + NG + 6 + 2 * (i + 1))
                act.activation(rstd[:, k], var[:, k], ACT.Sqrt).then_inc(root, 1)
            for g, tiles in enumerate(quads):
                lo, n = P * tiles[0], P * len(tiles)
                act.wait_ge(back, NQ * r + g + 1)
                act.activation(xT[0:D, lo:lo + n], ps[0:D, 5 + g % 3, 0:n], ACT.Copy).then_inc(kept, 1)


def softmax_attention(m):
    nc, a, c, sem, ps, dT, xT = (m[k] for k in ("nc", "a", "c", "sem", "ps", "dT", "xT"))
    ar = Arena(m["arena"])
    identb, ident = m["identb"], m["ident"]
    q1 = [ar.take(102, GH * SP_, BF16).rearrange("p (h t) -> p h t", h=GH) for _ in range(2)]
    k1 = [ar.take(102, GH * SP_, BF16).rearrange("p (h t) -> p h t", h=GH) for _ in range(2)]
    q2 = [ar.take(96, GH * S, BF16).rearrange("p (h t) -> p h t", h=GH) for _ in range(2)]
    k2 = [ar.take(96, GH * S, BF16).rearrange("p (h t) -> p h t", h=GH) for _ in range(2)]
    parts = [[ar.take(P, S, BF16) for _ in range(3)] for _ in range(2)]
    qk = [ar.take(P, S) for _ in range(2)]
    vs = ar.take(P, SB * P)
    v = [ar.take(P, SB * P) for _ in range(2)]
    xb = ar.take(D + 1, S)
    prob = [ar.take(P, GH * CH).rearrange("p (h t) -> p h t", h=GH) for _ in range(2)]
    oT = [ar.take(P, S) for _ in range(2)]
    rec = ar.take(P, CH)
    ones = ar.take(P, HD)
    mask_kq, mask_qk = ar.take(P, P, BF16), ar.take(P, P, BF16)
    mx = ar.take(P, GH * SB * 3)
    mc = ar.take(P, GH * SB)
    mhl = ar.take(GH * SB, 2 * P, BF16)
    w = m["weights"]
    wq, wk, wv = (w[0:D + 1, 256 * i:256 * i + 256] for i in range(3))
    wo = [w[:, 768 + D * g:768 + D * g + D] for g in range(2)]
    bo = w[0:D, 900:901]
    hml = nc.dram_tensor("split_parts", [6, P, S], BF16, kind="Internal").ap()

    loaded, set_up = sem("b_loaded"), sem("b_set_up")
    xb_in, projected, taken_act, taken_dve = sem("b_xb_in"), sem("b_projected"), sem("b_taken_act"), sem("b_taken_dve")
    split, parts_out, first_in, second_in = sem("b_split"), sem("b_parts_out"), sem("b_first_in"), sem("b_second_in")
    maxed, m_split, m_in = sem("b_maxed"), sem("b_m_split"), sem("b_m_in")
    scores, probs, weighed = sem("b_scores"), sem("b_probs"), sem("b_weighed")
    acc_free = sem("b_acc_free")
    rec_made, normed, out_made, out_kept = sem("b_rec_made"), sem("b_normed"), sem("b_out_made"), sem("b_out_kept")

    UNITS = 2 * B
    PIECES = [(j, i, n, min(512, P * i + rows(i) - 512 * n)) for j in range(GH) for i in range(SB)
              for n in range((P * i + rows(i) + 511) // 512)]
    NM, NPJ = len(PIECES) + 1, 9
    NTL = len(TILES)
    FIRST = 2 * NPJ + NM
    LAST_TILE = [max(n for n in range(NTL) if TILES[n][0] == ch) for ch in range(NCH)]
    PER_SLOT, SLOT0 = 5, 2

    def bank(n):
        return 6 + n % 2 if n >= FIRST else n % 8

    def split_unit(eng, u):
        for n in range(2):
            hi, mid, lo = parts[n]
            at = 8 * u + 4 * n
            eng.wait_ge(taken_act, NPJ * u + 3 * n + 3)
            if not (isinstance(u, int) and u == 0):
                eng.wait_ge(parts_out, 96 * u)
            settle(eng)
            eng.tensor_copy(hi, qk[n]).then_inc(split, 1)
            eng.wait_ge(split, at + 1)
            settle(eng)
            eng.tensor_tensor(qk[n], qk[n], hi, ALU.subtract).then_inc(split, 1)
            eng.wait_ge(split, at + 2)
            settle(eng)
            eng.tensor_copy(mid, qk[n]).then_inc(split, 1)
            eng.wait_ge(split, at + 3)
            settle(eng)
            eng.tensor_tensor(lo, qk[n], mid, ALU.subtract).then_inc(split, 1)

    weights_in = sem("b_weights_in")

    def loads(sp):
        for dst, name in ((wq, "Wq"), (wk, "Wk"), (wv, "Wv")):
            sp.dma_start(dst[0:D], a["L0_attn_" + name]).then_inc(weights_in, 16)
        for g in range(2):
            sp.dma_start(wo[g], a["L0_attn_Wo"][P * g:P * g + P]).then_inc(weights_in, 16)
        sp.dma_start(bo, a["L0_attn_bo"].rearrange("(d o) -> d o", o=1)).then_inc(weights_in, 16)

    norm(m, 0, loads)
    with nc.Block() as block:
        @block.sync
        def _(sp):
            sp.dma_start(mask_kq, c["mask_kq"]).then_inc(loaded, 16)
            sp.dma_start(mask_qk, c["mask_qk"]).then_inc(loaded, 16)
            for g in range(2):
                sp.dma_start(k1[g][96:102], c["bias_k"][:, GH * g:GH * g + GH]).then_inc(loaded, 16)
                sp.dma_start(q1[g][96:100], c["bias_q"][:, GH * g:GH * g + GH]).then_inc(loaded, 16)

            def parts_to_dram(u):
                for n in range(6):
                    sp.wait_ge(split, 8 * u + (1, 3, 4, 5, 7, 8)[n])
                    sp.dma_start(hml[n], parts[n // 3][n % 3]).then_inc(parts_out, 16)

            def stacks_in(u, g):
                sp.wait_ge(parts_out, 96 * u + 96)
                settle(sp)
                if not isinstance(u, int):
                    sp.wait_ge(scores, 2 * NTL * (u - 1))
                for stack, order, done in ((q1, (0, 1, 0), first_in), (k1, (3, 3, 4), first_in),
                                           (q2, (1, 2, 0), second_in), (k2, (4, 3, 5), second_in)):
                    for s, n in enumerate(order):
                        sp.dma_start(stack[g][32 * s:32 * s + 32, :, 0:S],
                                     hml[n].rearrange("(h d) t -> d h t", h=GH)).then_inc(done, 16)
                sp.wait_ge(taken_act, NPJ * u + NPJ)
                if not isinstance(u, int):
                    sp.wait_ge(weighed, NTL * (u - 1) + 2)
                sp.dma_start(v[g], vs).then_inc(second_in, 16)

            def maxima_in(u, g):
                sp.wait_ge(m_split, 2 * u + 2)
                for n in range(2):
                    sp.dma_start(q1[g][100 + n:101 + n, :, :].rearrange("p h t -> p (h t)"),
                                 mhl[:, P * n:P * n + P]).then_inc(m_in, 16)

            parts_to_dram(0)
            stacks_in(0, 0)
            sp.wait_ge(first_in, 96)
            sp.wait_ge(second_in, 112)
            parts_to_dram(1)
            stacks_in(1, 1)
            sp.wait_ge(first_in, 192)
            sp.wait_ge(second_in, 224)
            maxima_in(0, 0)

            def slot(u, g, project, maxima):
                if project:
                    parts_to_dram(u + 2)
                if maxima:
                    maxima_in(u + 1, 1 - g)
                if project:
                    stacks_in(u + 2, g)
                    sp.wait_ge(first_in, 96 * (u + 3))
                    settle(sp)
                    sp.wait_ge(second_in, 112 * (u + 3))
                    settle(sp)

            with sp.Fori(0, B - 1) as b:
                slot(2 * b, 0, True, True)
                slot(2 * b + 1, 1, True, True)
            slot(UNITS - 2, 0, False, True)
            slot(UNITS - 1, 1, False, False)

        @block.gpsimd
        def _(pool):
            pool.memset(ones, 1.0).then_inc(set_up, 1)
            pool.memset(vs[:, P * (SB - 1):], 0.0).then_inc(set_up, 1)

            def batch_in(b, earlier):
                if earlier is not None:
                    pool.wait_ge(projected, earlier)
                    settle(pool)
                pool.tensor_copy(xb, xT[:, b]).then_inc(xb_in, 1)

            batch_in(slice(0, S), None)
            with pool.Fori(0, B - 1) as b:
                batch_in(bass.ds((b + 1) * S, S), 2 * NPJ + 2 * (NPJ + NM) * b)
                split_unit(pool, 2 * b + 2)
                split_unit(pool, 2 * b + 3)

        @block.tensor
        def _(pe):
            pe.wait_ge(weights_in, 16 * 6)
            pe.wait_ge(set_up, 3)

            def project(u, g, n, use):
                pe.wait_ge(xb_in, u // 2 + 1 if isinstance(u, int) else batch_base[0])
                settle(pe)
                if n < 6:
                    wt, ch = (wq, wk)[n // 3], n % 3
                    pe.matmul(ps[:, bank(use), 0:CH], wt[:, P * g:P * g + P], xb[:, CH * ch:CH * ch + CH],
                              start=True, stop=True).then_inc(projected, 1)
                else:
                    for i in range(3):
                        j = 3 * (n - 6) + i
                        last = pe.matmul(ps[0:rows(j), bank(use), P * i:P * i + P], xb[:, P * j:P * j + rows(j)],
                                         wv[:, P * g:P * g + P], start=True, stop=True)
                    last.then_inc(projected, 1)

            def maxima(u, g, n, use):
                if n == NM - 1:
                    pe.wait_ge(maxed, u + 1)
                    settle(pe)
                    pe.transpose(ps[0:GH * SB, bank(use), 0:P], mc, ident[:]).then_inc(projected, 1)
                    return
                j, i, k, width = PIECES[n]
                settle(pe)
                if n == 0:
                    pe.wait_ge(first_in, 96 * (u + 1))
                diag = P * i < 512 * k + width
                last = pe.matmul(ps[0:rows(i), bank(use), 0:width], q1[g][0:100, j, P * i:P * i + rows(i)],
                                 k1[g][0:100, j, 512 * k:512 * k + width], start=True, stop=not diag)
                if diag:
                    o = P * i - 512 * k
                    last = pe.matmul(ps[0:rows(i), bank(use), o:o + rows(i)], identb[:, 0:rows(i)],
                                     mask_qk[:, 0:rows(i)], start=False, stop=True)
                last.then_inc(projected, 1)

            def score(u, g, n):
                ch, j, lo, width = TILES[n]
                if n == 0:
                    pe.wait_ge(m_in, 32 * (u + 1))
                    pe.wait_ge(second_in, 112 * (u + 1))
                for half in range(2):
                    settle(pe)
                    pe.wait_ge(probs, 2 * NTL * u + 2 * n + half + 1)
                    for hd in range(2 * half, 2 * half + 2):
                        r = rows(j)
                        cut = lo < P * j + r
                        pe.matmul(ps[0:r, hd, 0:width], k1[g][0:102, hd, P * j:P * j + r], q1[g][0:102, hd, lo:lo + width],
                                  start=True, stop=False)
                        last = pe.matmul(ps[0:r, hd, 0:width], k2[g][:, hd, P * j:P * j + r], q2[g][:, hd, lo:lo + width],
                                         start=False, stop=not cut)
                        if cut:
                            wd = min(P * j + r, lo + width) - lo
                            last = pe.matmul(ps[0:r, hd, 0:wd], identb[:, 0:r], mask_kq[:, lo - P * j:lo - P * j + wd],
                                             start=False, stop=True)
                    last.then_inc(scores, 1)

            def weigh(u, g, n):
                ch, j, lo, width = TILES[n]
                pe.wait_ge(probs, 2 * NTL * u + 2 * n + 2 + 2)
                if j == 0:
                    pe.wait_ge(acc_free, NCH * u + ch + 1)
                    if g == 0 and ch == 0:
                        pe.wait_ge(out_kept, out_base[0] + 1)
                settle(pe)
                r, o = rows(j), lo - CH * ch
                stop = n in LAST_TILE
                for hd in range(GH):
                    pe.matmul(ps[HD * hd:HD * hd + HD, 4, o:o + width], v[g][0:r, P * j + HD * hd:P * j + HD * hd + HD],
                              prob[n % 2][0:r, hd, 0:width], start=(j == 0), stop=stop, skip_group_check=True)
                for hd in range(GH):
                    last = pe.matmul(ps[HD * hd:HD * hd + HD, 5, o:o + width], ones[0:r, :],
                                     prob[n % 2][0:r, hd, 0:width], start=(j == 0), stop=stop, skip_group_check=True)
                last.then_inc(weighed, 1)

            out_base, batch_base = [None], [None]

            def slot(u, g, b, project_next, maxima_next):
                out_base[0], batch_base[0] = NCH * b, b + 2
                use, acts = 0, NPJ if project_next else 0

                def before():
                    if use >= 2 and use - 2 < acts:
                        pe.wait_ge(taken_act, NPJ * (u + 2) + use - 1)
                    elif use >= 2:
                        pe.wait_ge(taken_dve, NM * (u + 1) + use - 1 - acts)
                    else:
                        pe.wait_ge(taken_dve, NM * (u + 1) + use - 1)

                for n in range(NTL + 1):
                    if n < NTL:
                        score(u, g, n)
                    if project_next and n < 3:
                        for i in range(3):
                            before()
                            project(u + 2, g, 3 * n + i, FIRST + use)
                            use += 1
                    if maxima_next and SLOT0 <= n <= SLOT0 + NM // PER_SLOT:
                        for i in range(PER_SLOT * (n - SLOT0), min(PER_SLOT * (n - SLOT0 + 1), NM)):
                            before()
                            maxima(u + 1, 1 - g, i, FIRST + use)
                            use += 1
                    if n >= 1:
                        weigh(u, g, n - 1)
                if g == 1:
                    for ch in range(NCH):
                        pe.wait_ge(normed, NCH * (u + 1) + 1)
                        if ch == 2:
                            pe.wait_ge(out_kept, NCH * b + 1 + 1)
                        for k in range(2):
                            last = pe.matmul(ps[0:D, 4 + ch % 2, 0:CH], wo[k], oT[k][:, CH * ch:CH * ch + CH],
                                             start=(k == 0), stop=(k == 1))
                        last.then_inc(out_made, 1)

            for n in range(FIRST):
                if n >= 8:
                    if n - 8 < 2 * NPJ:
                        pe.wait_ge(taken_act, n - 7)
                    else:
                        pe.wait_ge(taken_dve, n - 7 - 2 * NPJ)
                if n == 2 * NPJ:
                    pe.wait_ge(loaded, 16 * 6)
                if n < 2 * NPJ:
                    project(n // NPJ, n // NPJ, n % NPJ, n)
                else:
                    maxima(0, 0, n - 2 * NPJ, n)
            with pe.Fori(0, B - 1) as b:
                slot(2 * b, 0, b, True, True)
                slot(2 * b + 1, 1, b, True, True)
            slot(UNITS - 2, 0, B - 1, False, True)
            slot(UNITS - 1, 1, B - 1, False, False)

        @block.scalar
        def _(act):
            act.sem_inc(probs, 2)
            act.sem_inc(out_kept, 1)
            act.wait_ge(set_up, 3)
            act.wait_ge(weights_in, 16 * 6)

            def take(u, n, use, count):
                act.wait_ge(projected, count + 1)
                if n == 0 or n == 3:
                    if not (isinstance(u, int) and u == 0):
                        act.wait_ge(split, 8 * u - 8 + (4 if n == 0 else 8))
                if n == 6 and not (isinstance(u, int) and u == 0):
                    act.wait_ge(second_in, 112 * u)
                if n < 6:
                    dst = qk[n // 3][:, CH * (n % 3):CH * (n % 3) + CH]
                    act.activation(dst, ps[:, bank(use), 0:CH], ACT.Copy, scale=(HD ** -0.5, 1.0)[n // 3]).then_inc(taken_act, 1)
                elif n < 8:
                    act.activation(vs[:, 3 * P * (n - 6):3 * P * (n - 5)], ps[:, bank(use), 0:3 * P], ACT.Copy).then_inc(taken_act, 1)
                else:
                    act.activation(vs[:, 6 * P:8 * P], ps[:, bank(use), 0:2 * P], ACT.Copy)
                    act.activation(vs[0:rows(8), 8 * P:9 * P], ps[0:rows(8), bank(use), 2 * P:3 * P], ACT.Copy).then_inc(taken_act, 1)

            def slot(u, g, b, project_next):
                for n in range(NTL):
                    ch, j, lo, width = TILES[n]
                    r = rows(j)
                    act.wait_ge(weighed, NTL * u + n + 1)
                    for half in range(2):
                        act.wait_ge(scores, 2 * NTL * u + 2 * n + half + 1)
                        act.activation(prob[n % 2][0:r, 2 * half:2 * half + 2, 0:width], ps[0:r, 2 * half:2 * half + 2, 0:width],
                                       ACT.Exp).then_inc(probs, 1)
                    if project_next and n < 3:
                        for i in range(3):
                            take(u + 2, 3 * n + i, FIRST + 3 * n + i, FIRST + (NPJ + NM) * u + 3 * n + i)
                if g == 1:
                    for ch in range(NCH):
                        act.wait_ge(out_made, NCH * b + ch + 1 + 1)
                        act.activation(dT[:, bass.ds(b * S + CH * ch, CH)] if not isinstance(b, int) else dT[:, b * S + CH * ch:b * S + CH * ch + CH],
                                       ps[0:D, 4 + ch % 2, 0:CH], ACT.Identity, bias=bo).then_inc(out_kept, 1)

            for n in range(2 * NPJ):
                take(n // NPJ, n % NPJ, n, n)
            with act.Fori(0, B - 1) as b:
                slot(2 * b, 0, b, True)
                slot(2 * b + 1, 1, b, True)
            slot(UNITS - 2, 0, B - 1, False)
            slot(UNITS - 1, 1, B - 1, False)

        @block.vector
        def _(dve):
            dve.memset(w[D:D + 1, 0:768], 0.0).then_inc(set_up, 1)
            dve.memset(mx, MASKED).then_inc(rec_made, 1)
            dve.wait_ge(rec_made, 1)
            dve.sem_inc(weighed, 2)
            dve.sem_inc(normed, 1)
            dve.sem_inc(acc_free, 1)
            dve.sem_inc(out_made, 1)
            split_unit(dve, 0)
            split_unit(dve, 1)

            def take_max(u, n, use, count):
                if n == 0 and not (isinstance(u, int) and u == 0):
                    dve.wait_ge(maxed, u)
                if n == NM - 1:
                    dve.wait_ge(taken_dve, NM * u + NM - 1)
                    if not (isinstance(u, int) and u == 0):
                        dve.wait_ge(m_in, 32 * u)
                    dve.tensor_reduce(mc, mx.rearrange("p (b n) -> p b n", n=3), X, ALU.max).then_inc(maxed, 1)
                    dve.wait_ge(projected, count + 1)
                    src = ps[0:GH * SB, bank(use), 0:P]
                    dve.tensor_scalar(mhl[:, 0:P], src, -1.0, None, ALU.mult).then_inc(m_split, 1)
                    dve.wait_ge(m_split, 2 * u + 1)
                    dve.scalar_tensor_tensor(mhl[:, P:2 * P], src, -1.0, mhl[:, 0:P], ALU.mult, ALU.subtract).then_inc(m_split, 1)
                    dve.wait_ge(m_split, 2 * u + 2)
                    dve.sem_inc(taken_dve, 1)
                    return
                j, i, k, width = PIECES[n]
                dve.wait_ge(projected, count + 1)
                at = 3 * (SB * j + i) + k
                dve.reduce_max(mx[0:rows(i), at:at + 1], ps[0:rows(i), bank(use), 0:width], X).then_inc(taken_dve, 1)

            def empty_banks(u, g, ch, b):
                dve.wait_ge(weighed, NTL * u + LAST_TILE[ch] + 1 + 2)
                dve.wait_ge(normed, NCH * u + ch + 1)
                if ch == 0 and g == 0:
                    dve.wait_ge(out_made, NCH * b + 1)
                at = 3 * (NCH * u + ch) + 1
                out = oT[g][:, CH * ch:CH * ch + CH]
                dve.tensor_copy(rec, ps[:, 5, 0:CH]).then_inc(rec_made, 1)
                dve.tensor_copy(out, ps[:, 4, 0:CH]).then_inc(rec_made, 1)
                dve.wait_ge(rec_made, at + 2)
                dve.sem_inc(acc_free, 1)

            def norm_chunk(u, g, ch):
                at = 3 * (NCH * u + ch) + 1
                out = oT[g][:, CH * ch:CH * ch + CH]
                dve.reciprocal(rec, rec).then_inc(rec_made, 1)
                dve.wait_ge(rec_made, at + 3)
                settle(dve)
                dve.tensor_tensor(out, out, rec, ALU.mult).then_inc(normed, 1)

            def slot(u, g, b, acts, maxima_next):
                use = acts
                for n in range(NTL):
                    for ch in range(NCH - 1):
                        if n == LAST_TILE[ch] + 2:
                            empty_banks(u, g, ch, b)
                    if maxima_next and SLOT0 <= n <= SLOT0 + NM // PER_SLOT:
                        for i in range(PER_SLOT * (n - SLOT0), min(PER_SLOT * (n - SLOT0 + 1), NM)):
                            take_max(u + 1, i, FIRST + use, FIRST + (NPJ + NM) * u + use)
                            use += 1
                    for ch in range(NCH - 1):
                        if n == LAST_TILE[ch] + 2:
                            norm_chunk(u, g, ch)
                empty_banks(u, g, NCH - 1, b)
                norm_chunk(u, g, NCH - 1)

            for n in range(NM):
                take_max(0, n, 2 * NPJ + n, 2 * NPJ + n)
            with dve.Fori(0, B - 1) as b:
                slot(2 * b, 0, b, NPJ, True)
                slot(2 * b + 1, 1, b, NPJ, True)
            slot(UNITS - 2, 0, B - 1, 0, True)
            slot(UNITS - 1, 1, B - 1, 0, False)


def binary_experts(m):
    nc, a, c, sem, ps, dT, xT, xh3 = (m[k] for k in ("nc", "a", "c", "sem", "ps", "dT", "xT", "xh3"))
    ar = Arena(m["arena"])
    identb = m["identb"]
    E, IN, OUT = 8, D, D
    NQ, NG = IN * E // P, IN // 4
    NP = NG * 2
    aT = ar.take(P, NQ * N, BF16).rearrange("p (q t) -> p q t", q=NQ)
    an = [ar.take(P, IN * E, BF16) for _ in range(2)]
    sg = ar.take(P, NT * D, BF16)
    gate = ar.take(P, NT * E, BF16)
    stack = [ar.take(96, NG * CH, BF16).rearrange("p (g t) -> p g t", g=NG) for _ in range(3)]
    wf = ar.take(96, NG * OUT)
    wsplit = [ar.take(96, NG * OUT, BF16) for _ in range(3)]
    wl = ar.take(96, NG * 2 * P, BF16)
    NS = 4
    sgn = [ar.take(P, 2 * CH, BF16).rearrange("p (n t) -> p n t", n=2) for _ in range(NS)]
    pair_sum, pair_sum_big = ar.take(P, D, BF16), ar.take(P, D, BF16)
    TINY = 2.0 ** -120
    pw = ar.take(D + 1, E)
    sc = ar.take(D, 1)
    loaded, w_in, wstep, w_placed, zeroed = sem("c_loaded"), sem("c_w_in"), sem("c_wstep"), sem("c_w_placed"), sem("c_zeroed")
    logits, gates, signs, made, turned, kept = (sem("c_" + s) for s in ("logits", "gates", "signs", "made", "turned", "kept"))
    sg3 = sg.rearrange("p (k d) -> p k d", d=D)
    g3 = gate.rearrange("p (k e) -> p k e", e=E)
    wl4 = wl.rearrange("p (g f i o) -> p g f i o", g=NG, f=2, i=2)

    def loads(sp):
        sp.dma_start(pw[0:D], a["L0_ffn_proj_w"]).then_inc(loaded, 16)
        sp.dma_start(pw[D:D + 1], a["L0_ffn_proj_b"].rearrange("(o e) -> o e", o=1)).then_inc(loaded, 16)
        sp.dma_start(sc, a["L0_ffn_scale"].rearrange("a b o -> o (a b)")).then_inc(loaded, 16)
        sp.dma_start(pair_sum, c["pair_sum"]).then_inc(loaded, 16)
        src = a["L0_ffn_weight"].rearrange("o e (g i) d -> i e (o g) d", i=4)
        for s in range(3):
            for i in range(4):
                at = 32 * s + E * i
                sp.dma_start(wf[at:at + E].rearrange("p (g d) -> p g d", g=NG), src[i]).then_inc(w_in, 16)

    norm(m, 1, loads)
    with nc.Block() as block:
        @block.sync
        def _(sp):
            sp.wait_ge(wstep, 5)
            sp.wait_ge(zeroed, 1)
            for s in range(3):
                for i in range(4):
                    at = 32 * s + E * i
                    sp.dma_start(wl4[at:at + E, :, i // 2, i % 2, :],
                                 wsplit[s][at:at + E].rearrange("p (g o) -> p g o", g=NG)).then_inc(w_placed, 16)
            sp.wait_ge(w_placed, 192)

        @block.gpsimd
        def _(pool):
            pool.memset(wl, 0.0).then_inc(zeroed, 1)
            hi, mid, lo = wsplit
            pool.wait_ge(w_in, 192)
            pool.tensor_copy(hi, wf).then_inc(wstep, 1)
            pool.wait_ge(wstep, 1)
            pool.tensor_tensor(wf, wf, hi, ALU.subtract).then_inc(wstep, 1)
            pool.wait_ge(wstep, 2)
            pool.tensor_copy(mid, wf).then_inc(wstep, 1)
            pool.wait_ge(wstep, 3)
            pool.tensor_tensor(wf, wf, mid, ALU.subtract).then_inc(wstep, 1)
            pool.wait_ge(wstep, 4)
            pool.tensor_copy(lo, wf).then_inc(wstep, 1)

        @block.tensor
        def _(pe):
            pe.wait_ge(loaded, 64)
            for t in range(NT):
                last = pe.matmul(ps[:, 0, E * t:E * t + E], xT[:, P * t:P * t + P], pw, start=True, stop=True)
            last.then_inc(logits, 1)
            for t in range(NT):
                b = 1 + t % 3
                pe.wait_ge(made, t + 1)
                if t >= 3:
                    pe.wait_ge(kept, t - 2)
                pb = ps[:, b, :].bitcast(BF16)
                for q in range(NQ):
                    last = pe.transpose(pb[:, P * q:P * q + P], an[t % 2][:, P * q:P * q + P], identb[:])
                last.then_inc(turned, 1)

        @block.scalar
        def _(act):
            act.activation(sg3, xh3, ACT.Sign).then_inc(signs, 1)
            for t in range(NT):
                act.wait_ge(turned, t + 1)
                pb = ps[:, 1 + t % 3, :].bitcast(BF16)
                act.activation(aT[:, :, P * t:P * t + P], pb[:, 0:NQ * P].rearrange("p (q t) -> p q t", q=NQ),
                               ACT.Copy).then_inc(kept, 1)

        @block.vector
        def _(dve):
            dve.wait_ge(loaded, 64)
            dve.wait_ge(logits, 1)
            dve.tensor_scalar(gate, ps[:, 0, 0:NT * E], 0.0, None, ALU.is_gt).then_inc(gates, 1)
            dve.tensor_scalar(pair_sum_big, pair_sum, 1 / TINY, None, ALU.mult).then_inc(gates, 1)
            dve.wait_ge(gates, 2)
            dve.wait_ge(signs, 1)
            for t in range(NT):
                if t >= 2:
                    dve.wait_ge(turned, t - 1)
                dve.tensor_tensor(an[t % 2].rearrange("p (i e) -> p i e", e=E),
                                  sg3[:, t, :].rearrange("p (i o) -> p i o", o=1).broadcast_to([P, IN, E]),
                                  g3[:, t, :].rearrange("p (o e) -> p o e", o=1).broadcast_to([P, IN, E]),
                                  ALU.mult).then_inc(made, 1)

    stacked, mixed = [sem(f"c_stacked_{q}") for q in range(3)], sem("c_mixed")
    sign_act, sign_dve, summed, sum_made, sum_kept = (
        sem("c_" + s) for s in ("sign_act", "sign_dve", "summed", "sum_made", "sum_kept"))
    NCK, PR = N // CH, NP // 2
    Q = 3
    on_dve = [n % 2 == 1 for n in range(PR)]
    ND = sum(on_dve)
    NA = PR - ND
    sum_bank = (6, 7, 6)

    def ahead(n):
        return n - sum(on_dve[:n]), sum(on_dve[:n])

    def wait_signed(eng, ck, n):
        if on_dve[n]:
            eng.wait_ge(sign_dve, ND * ck + ahead(n)[1] + 1 + ND)
        else:
            eng.wait_ge(sign_act, NA * ck + ahead(n)[0] + 1 + NA)

    def wait_free(eng, ck, n):
        eng.wait_ge(summed, PR * ck + n - NS + 1 + PR)

    with nc.Block() as block:
        @block.sync
        def _(sp):
            with sp.Fori(0, NCK // Q) as k:
                for q in range(Q):
                    sp.wait_ge(mixed, PR * (Q * k + q) + PR)
                    settle(sp)
                    for s in range(3):
                        for r in range(4):
                            sp.dma_start(stack[q].rearrange("p (q r) t -> p q r t", r=4)[32 * s:32 * s + 32, :, r, :],
                                         aT[32 * r:32 * r + 32, :, bass.ds((Q * k + q) * CH, CH)]).then_inc(stacked[q], 16)

        @block.tensor
        def _(pe):
            pe.sem_inc(mixed, Q * PR)

            def mix(k, m_):
                q, n = m_ // PR, m_ % PR
                ck = Q * k + q
                if n == 0:
                    pe.wait_ge(stacked[q], 192 * (k + 1))
                wait_signed(pe, ck if n >= 3 else ck - 1, (n - 3) % PR)
                for f in range(2):
                    last = pe.matmul(ps[:, 2 * (m_ % 3) + f, 0:CH], wl[:, P * (2 * n + f):P * (2 * n + f) + P],
                                     stack[q][:, n, :], start=True, stop=True)
                last.then_inc(mixed, 1)

            def add(k, m_):
                q, n = m_ // PR, m_ % PR
                ck = Q * k + q
                if n == 0:
                    pe.wait_ge(sum_kept, ck + (2, 0, 1)[q])
                wait_signed(pe, ck, n)
                settle(pe)
                for f in range(2):
                    last = pe.matmul(ps[0:D, sum_bank[q], 0:CH], pair_sum_big if on_dve[n] else pair_sum, sgn[m_ % NS][:, f, :],
                                     start=(n == 0 and f == 0), stop=(n == PR - 1 and f == 1))
                last.then_inc(summed, 1)

            with pe.Fori(0, NCK // Q) as k:
                mix(k, 0)
                mix(k, 1)
                for m_ in range(Q * PR):
                    if m_ + 2 < Q * PR:
                        mix(k, m_ + 2)
                    add(k, m_)

        @block.scalar
        def _(act):
            act.sem_inc(sign_act, NA)
            act.sem_inc(summed, PR)
            act.sem_inc(sum_kept, 2)
            with act.Fori(0, NCK // Q) as k:
                for m_ in range(Q * PR):
                    q, n = m_ // PR, m_ % PR
                    if not on_dve[n]:
                        wait_free(act, Q * k + q, n)
                        act.wait_ge(mixed, PR * (Q * k + q) + n + 1 + Q * PR)
                        b0 = 2 * (m_ % 3)
                        act.activation(sgn[m_ % NS], ps[:, b0:b0 + 2, 0:CH], ACT.Sign).then_inc(sign_act, 1)

        @block.vector
        def _(dve):
            dve.sem_inc(sign_dve, ND)

            def keep(k, q):
                ck = Q * k + q
                dve.wait_ge(summed, PR * ck + PR + PR)
                dve.tensor_scalar(dT[:, bass.ds(ck * CH, CH)], ps[0:D, sum_bank[q], 0:CH], sc, None,
                                  ALU.mult).then_inc(sum_kept, 1)

            with dve.Fori(0, NCK // Q) as k:
                for m_ in range(Q * PR):
                    q, n = m_ // PR, m_ % PR
                    if on_dve[n]:
                        b0 = 2 * (m_ % 3)
                        wait_free(dve, Q * k + q, n)
                        dve.wait_ge(mixed, PR * (Q * k + q) + n + 1 + Q * PR)
                        dve.tensor_scalar(sgn[m_ % NS], ps[:, b0:b0 + 2, 0:CH], TINY, -TINY, ALU.min, ALU.max).then_inc(sign_dve, 1)
                    if n == 3 and q >= 1:
                        keep(k, q - 1)
                keep(k, Q - 1)


def retention(m):
    nc, a, c, sem, ps, dT, xT = (m[k] for k in ("nc", "a", "c", "sem", "ps", "dT", "xT"))
    ar = Arena(m["arena"])
    xb = [ar.take(D + 1, S) for _ in range(2)]
    q, k = [ar.take(D + 1, S) for _ in range(2)], [ar.take(D + 1, S) for _ in range(2)]
    v = [ar.take(P, SB * D) for _ in range(2)]
    decay = ar.take(P, S)
    NP = 4
    p = [ar.take(P, CH) for _ in range(NP)]
    w = ar.take(D + 1, 3 * D)
    wq, wk, wv = (w[:, D * i:D * i + D] for i in range(3))
    loaded, set_up, xb_in = sem("d_loaded"), sem("d_set_up"), sem("d_xb_in")
    prep, prep_kept, scores, decayed, summed, kept = (
        sem("d_" + s) for s in ("prep", "prep_kept", "scores", "decayed", "summed", "kept"))
    NTL = len(TILES)
    NPR = 8
    LAST_TILE = [max(n for n in range(NTL) if TILES[n][0] == ch) for ch in range(NCH)]

    def loads(sp):
        for dst, name in ((wq, "Wq"), (wk, "Wk"), (wv, "Wv")):
            sp.dma_start(dst[0:D], a["L1_attn_" + name]).then_inc(loaded, 16)
        sp.dma_start(decay, c["decay"]).then_inc(loaded, 16)

    norm(m, 2, loads)
    with nc.Block() as block:
        @block.gpsimd
        def _(pool):
            for n in range(2):
                pool.tensor_copy(xb[n], xT[:, S * n:S * n + S]).then_inc(xb_in, 1)
            with pool.Fori(0, B // 2 - 1) as pair:
                for n in range(2):
                    b = 2 * pair
                    pool.wait_ge(prep, NPR * (b + n + 1))
                    settle(pool)
                    pool.tensor_copy(xb[n], xT[:, bass.ds((b + n + 2) * S, S)]).then_inc(xb_in, 1)

        @block.tensor
        def _(pe):
            pe.wait_ge(loaded, 64)
            pe.wait_ge(set_up, 5)

            def prepare(b, par, n):
                if n == 0:
                    pe.wait_ge(xb_in, b + 1)
                pe.wait_ge(prep_kept, NPR * b + n + 1)
                settle(pe)
                if n < 6:
                    ch = n % 3
                    last = pe.matmul(ps[0:D, 6 + n % 2, 0:CH], (wq, wk)[n // 3], xb[par][:, CH * ch:CH * ch + CH],
                                     start=True, stop=True)
                else:
                    for j in (range(8), range(8, SB))[n - 6]:
                        last = pe.matmul(ps[0:rows(j), 6 + n % 2, D * (j % 8):D * (j % 8) + D],
                                         xb[par][:, P * j:P * j + rows(j)], wv, start=True, stop=True)
                last.then_inc(prep, 1)

            def score(b, par, n):
                ch, j, lo, width = TILES[n]
                if n == 0:
                    pe.wait_ge(prep_kept, NPR * (b + 1) + 2)
                pe.wait_ge(decayed, NTL * b + n + 1)
                r = rows(j)
                pe.matmul(ps[0:r, (NTL * par + n) % 4, 0:width], k[par][:, P * j:P * j + r], q[par][:, lo:lo + width],
                          start=True, stop=True).then_inc(scores, 1)

            def weigh(b, par, n):
                ch, j, lo, width = TILES[n]
                pe.wait_ge(decayed, NTL * b + n + 1 + 4)
                if j == 0:
                    pe.wait_ge(kept, NCH * b + ch + 1)
                settle(pe)
                r, o = rows(j), lo - CH * ch
                pe.matmul(ps[0:D, 4 + (NCH * par + ch) % 2, o:o + width], v[par][0:r, D * j:D * j + D],
                          p[(NTL * par + n) % NP][0:r, 0:width], start=(j == 0), stop=n in LAST_TILE,
                          skip_group_check=True).then_inc(summed, 1)

            for n in range(NPR):
                prepare(0, 0, n)

            def batch(b, par, more):
                score(b, par, 0)
                score(b, par, 1)
                for n in range(NTL):
                    if n + 2 < NTL:
                        score(b, par, n + 2)
                    if more and 4 <= n < 4 + NPR:
                        prepare(b + 1, 1 - par, n - 4)
                    weigh(b, par, n)

            with pe.Fori(0, B // 2 - 1) as pair:
                batch(2 * pair, 0, True)
                batch(2 * pair + 1, 1, True)
            batch(B - 2, 0, True)
            batch(B - 1, 1, False)

        @block.scalar
        def _(act):
            act.sem_inc(prep_kept, 2)
            act.sem_inc(kept, 2)

            def prepare(b, par, n):
                act.wait_ge(prep, NPR * b + n + 1)
                src = ps[:, 6 + n % 2, :]
                if n < 6:
                    ch = n % 3
                    act.activation((q, k)[n // 3][par][0:D, CH * ch:CH * ch + CH], src[0:D, 0:CH], ACT.Copy).then_inc(prep_kept, 1)
                elif n == 6:
                    act.activation(v[par][:, 0:8 * D], src[:, 0:8 * D], ACT.Copy).then_inc(prep_kept, 1)
                else:
                    act.activation(v[par][0:rows(8), 8 * D:9 * D], src[0:rows(8), 0:D], ACT.Copy).then_inc(prep_kept, 1)

            def keep(b, par, ch):
                act.wait_ge(summed, NTL * b + LAST_TILE[ch] + 1 + 4)
                at = b * S + CH * ch
                dst = dT[:, at:at + CH] if isinstance(b, int) else dT[:, bass.ds(at, CH)]
                act.activation(dst, ps[0:D, 4 + (NCH * par + ch) % 2, 0:CH], ACT.Copy).then_inc(kept, 1)

            def batch(b, par, more):
                for n in range(NTL + 2):
                    if more and 4 <= n < 4 + NPR:
                        prepare(b + 1, 1 - par, n - 4)
                    for ch in range(NCH):
                        if n == LAST_TILE[ch] + 2:
                            keep(b, par, ch)

            for n in range(NPR):
                prepare(0, 0, n)
            with act.Fori(0, B // 2 - 1) as pair:
                batch(2 * pair, 0, True)
                batch(2 * pair + 1, 1, True)
            batch(B - 2, 0, True)
            batch(B - 1, 1, False)

        @block.vector
        def _(dve):
            dve.memset(w[D:D + 1, :], 0.0).then_inc(set_up, 1)
            for t in (*q, *k):
                dve.memset(t[D:D + 1, :], 0.0).then_inc(set_up, 1)
            dve.sem_inc(decayed, 4)
            dve.sem_inc(summed, 4)
            dve.wait_ge(loaded, 64)

            def batch(b, par):
                for n in range(NTL):
                    ch, j, lo, width = TILES[n]
                    r = rows(j)
                    i = (NTL * par + n) % 4
                    dve.wait_ge(scores, NTL * b + n + 1)
                    dve.wait_ge(summed, NTL * b + n + 1)
                    dve.tensor_tensor(p[i][0:r, 0:width], ps[0:r, i, 0:width], decay[0:r, lo - P * j:lo - P * j + width],
                                      ALU.mult).then_inc(decayed, 1)

            with dve.Fori(0, B // 2) as pair:
                batch(2 * pair, 0)
                batch(2 * pair + 1, 1)


DEC = 12 + NT


def decode(chain, vector, ends, width, src):
    kint, klo, srci, dhi, ta, tb, kf, dlob = ends
    w = slice(0, width)
    chain(vector.tensor_scalar(kf[:, w], src, float(-(544 << 14)), None, ALU.max))
    chain(vector.tensor_copy(kint[:, w], kf[:, w]))
    chain(vector.tensor_scalar(klo[:, w], kint[:, w], 7, None, ALU.arith_shift_right))
    chain(vector.tensor_scalar(klo[:, w], klo[:, w], P - 1, None, ALU.bitwise_and))
    chain(vector.tensor_copy(dlob[:, w], klo[:, w]))
    chain(vector.tensor_scalar(klo[:, w], kint[:, w], 14, None, ALU.arith_shift_right))
    chain(vector.tensor_scalar(ta[:, w], klo[:, w], 544.0, None, ALU.add))
    chain(vector.tensor_scalar(dhi[:, w], ta[:, w], float(NT), None, ALU.is_ge))
    for v in range(2, NT):
        chain(vector.scalar_tensor_tensor(dhi[:, w], ta[:, w], float(NT * v), dhi[:, w], ALU.is_ge, ALU.add))
    chain(vector.scalar_tensor_tensor(ta[:, w], dhi[:, w], -float(NT), ta[:, w], ALU.mult, ALU.add))
    chain(vector.tensor_scalar(klo[:, w], kint[:, w], P - 1, None, ALU.bitwise_and))
    chain(vector.scalar_tensor_tensor(tb[:, w], ta[:, w], float(P), klo[:, w], ALU.mult, ALU.add))
    chain(vector.tensor_copy(srci[:, w], tb[:, w]))
    chain(vector.tensor_scalar(tb[:, w], src, NONE / 2, -1000.0, ALU.is_lt, ALU.mult))
    chain(vector.tensor_tensor(dhi[:, w], dhi[:, w], tb[:, w], ALU.add))


class NodeTables:

    def __init__(self, m, nodes, dtab, prod, own, bound, t1, t2, lastrow, G4, G4p, att_s, att_d, wg, loaded, tab):
        self.m, self.nodes, self.dtab, self.prod, self.own, self.bound = m, nodes, dtab, prod, own, bound
        self.t1, self.t2, self.lastrow, self.G4, self.G4p = t1, t2, lastrow, G4, G4p
        self.att_s, self.att_d, self.wg, self.loaded, self.tab = att_s, att_d, wg, loaded, tab
        self.gat, self.step, self.tab_out, self.last_in, self.gmax, self.gall, self.expd = (
            m["sem"]("f_" + s) for s in ("gat", "step", "tab_out", "last_in", "gmax", "gall", "expd"))
        self.n = 0

    def chain(self, instruction):
        self.n += 1
        instruction.then_inc(self.step, 1)
        self.m["nc"].vector.wait_ge(self.step, self.n)

    @staticmethod
    def per_head(ap):
        return ap.rearrange("p (o c) -> p o c", o=1).broadcast_to([P, NT, ap.shape[1]])

    @staticmethod
    def split(ap):
        return ap.rearrange("p k (h e) -> p k h e", e=FE)

    @staticmethod
    def spread(w):
        return w.rearrange("p k (h o) -> p k h o", o=1).broadcast_to([P, NT, FE, FE])

    def write(self, sp):
        sp.wait_ge(self.step, 7)
        sp.dma_start(self.tab.rearrange("(k p) c -> p k c", p=P), self.nodes).then_inc(self.tab_out, 16)
        sp.wait_ge(self.tab_out, 16)
        sp.dma_start(self.lastrow, self.tab[N - 1:N, :].broadcast_to([P, CHN])).then_inc(self.last_in, 16)

    def features(self, pe):
        ps, xT = self.m["ps"], self.m["xT"]
        pe.wait_ge(self.loaded, 112)
        pe.wait_ge(self.step, 1)
        for k in range(NT):
            last = pe.matmul(ps[:, k // 32, HE * (k % 32):HE * (k % 32) + HE], xT[:, P * k:P * k + P], self.wg,
                             start=True, stop=True)
        last.then_inc(self.gat, 1)

    def reduce(self, pool):
        pool.wait_ge(self.gmax, 1)
        pool.partition_all_reduce(self.G4, self.G4p, P, bass.bass_isa.ReduceOp.max).then_inc(self.gall, 1)

    def exps(self, act):
        act.wait_ge(self.step, 15)
        act.activation(self.t1, self.t1, ACT.Exp).then_inc(self.expd, 1)
        act.activation(self.t2, self.t2, ACT.Exp).then_inc(self.expd, 1)

    def terms(self, dve):
        ps, chain, nodes, split, per_head = self.m["ps"], self.chain, self.nodes, self.split, self.per_head
        chain(dve.memset(self.wg[D:D + 1], 0.0))
        dve.wait_ge(self.loaded, 112)
        dve.wait_ge(self.gat, 1)
        h16, pr = nodes[:, :, 0:HE], self.prod[:, :, 0:HE]
        chain(dve.tensor_copy(nodes[:, 32:33, 0:HE], ps[:, 1, 0:HE].rearrange("p (k c) -> p k c", k=1)))
        chain(dve.tensor_copy(nodes[:, 0:32, 0:HE], ps[:, 0, :].rearrange("p (k c) -> p k c", k=32)))
        chain(dve.tensor_tensor(pr, h16, per_head(self.att_s), ALU.mult))
        chain(dve.tensor_reduce(nodes[:, :, HE:], split(pr), X, ALU.add))
        chain(dve.tensor_tensor(pr, h16, per_head(self.att_d), ALU.mult))
        chain(dve.tensor_reduce(self.dtab, split(pr), X, ALU.add))
        dve.tensor_reduce(self.G4p, nodes[:, :, HE:].rearrange("p k h -> p h k"), X, ALU.max).then_inc(self.gmax, 1)

    def exponents(self, dve):
        chain, per_head, t1, t2, bound, dtab = self.chain, self.per_head, self.t1, self.t2, self.bound, self.dtab

        def leaky(x):
            chain(dve.scalar_tensor_tensor(x, x, 0.2, x, ALU.mult, ALU.max))

        dve.wait_ge(self.gall, 1)
        dve.wait_ge(self.last_in, 16)
        chain(dve.tensor_tensor(bound, dtab, per_head(self.G4), ALU.add))
        leaky(bound)
        chain(dve.tensor_tensor(t1, self.nodes[:, :, HE:], dtab, ALU.add))
        leaky(t1)
        chain(dve.tensor_tensor(t1, t1, bound, ALU.subtract))
        chain(dve.tensor_tensor(t2, dtab, per_head(self.lastrow[:, HE:]), ALU.add))
        leaky(t2)
        chain(dve.tensor_tensor(t2, t2, bound, ALU.subtract))

    def own_sums(self, dve, cnt):
        chain, split, spread, own, prod = self.chain, self.split, self.spread, self.own, self.prod
        t1, t2 = self.t1, self.t2
        dve.wait_ge(self.expd, 2)
        chain(dve.tensor_tensor(t2, t2, cnt.rearrange("p (k o) -> p k o", o=1).broadcast_to([P, NT, FE]), ALU.mult))
        chain(dve.tensor_tensor(own[:, :, HE:], t1, t2, ALU.add))
        chain(dve.tensor_tensor(split(own[:, :, 0:HE]), split(self.nodes[:, :, 0:HE]), spread(t1), ALU.mult))
        last4 = self.per_head(self.lastrow[:, 0:HE]).rearrange("p k (h e) -> p k h e", e=FE)
        chain(dve.tensor_tensor(split(prod[:, :, 0:HE]), last4, spread(t2), ALU.mult))
        chain(dve.tensor_tensor(own[:, :, 0:HE], own[:, :, 0:HE], prod[:, :, 0:HE], ALU.add))


def count_clamped(m):
    nc, a, sem, ps = (m[k] for k in ("nc", "a", "sem", "ps"))
    ar = Arena(m["arena"])
    keys, picked, cnt = m["keys"], m["picked"], m["cnt"]
    load, products, gelus, credits = m["chunks"]
    tables = m["tables"]
    onehot = [ar.take(P, (LO + HI) * CB, BF16).rearrange("p (v e) -> p v e", e=CB) for _ in range(2)]
    digits = ar.take(P, 2 * EC, BF16)
    cnt64 = ar.take(LO, HI)
    zero = ar.take(P, LO + HI, BF16)
    zeroed = sem("e_zeroed")
    step = sem("e_step")
    edges_in, made, counted, cnt_kept, cnt_in = (sem("e_" + s) for s in ("edges_in", "made", "counted", "cnt_kept", "cnt_in"))
    NB = EC // CB
    NX2 = NXC - NB // 2

    def loads(sp):
        m["load_vectors"](sp)
        sp.dma_start(digits, m["edge_digits"]).then_inc(edges_in, 16)
        sp.dma_start(picked, m["edge_picked"]).then_inc(edges_in, 16)
        sp.dma_start(keys, m["edge_keys"]).then_inc(edges_in, 16)
        load(sp)

    norm(m, 3, loads)

    with nc.Block() as block:
        @block.sync
        def _(sp):
            tables.write(sp)
            sp.wait_ge(cnt_kept, 1)
            for half in range(2):
                sp.dma_start(cnt[LO * half:LO * half + LO, :],
                             cnt64[:, NT * half:NT * half + NT]).then_inc(cnt_in, 16)
            sp.wait_ge(cnt_in, 32)
            sp.wait_ge(edges_in, 48)

        @block.vector
        def _(dve):
            dve.memset(zero, 0.0).then_inc(zeroed, 1)
            tables.terms(dve)
            dve.wait_ge(edges_in, 48)
            dve.sem_inc(counted, 2)
            with dve.Fori(0, NB // 2) as pair:
                for b in range(2):
                    dve.wait_ge(counted, 2 * pair + b + 1)
                    for v in range(LO + HI):
                        which = v // LO if v < 2 * LO else 1
                        last = dve.tensor_scalar(onehot[b][:, v, :], digits[:, bass.ds((2 * pair + b) * CB + EC * which, CB)],
                                                 float(v - LO * which), None, ALU.is_equal)
                    last.then_inc(made, 1)
            n = 0

            def chain(instruction):
                nonlocal n
                n += 1
                instruction.then_inc(step, 1)
                dve.wait_ge(step, n)

            tables.exponents(dve)
            decode(chain, dve, m["ends"], CAP, picked)
            dve.wait_ge(counted, NB + 2)
            dve.tensor_copy(cnt64.rearrange("p (f k) -> p k f", f=2),
                            ps[0:LO, 7, 0:HI].rearrange("p (k f) -> p k f", f=2)).then_inc(cnt_kept, 1)
            dve.wait_ge(cnt_in, 32)
            tables.own_sums(dve, cnt)

        @block.tensor
        def _(pe):
            tables.features(pe)
            pe.wait_ge(zeroed, 1)
            pe.matmul(ps[0:LO, 7, 0:HI], zero[:, 0:LO], zero[:, LO:], start=True, stop=False, skip_group_check=True)

            def count(b, blocks):
                pe.wait_ge(made, blocks)
                settle(pe)
                for e in range(CB):
                    last = pe.matmul(ps[0:LO, 7, 0:HI], onehot[b][:, 0:LO, e], onehot[b][:, LO:, e],
                                     start=False, stop=False, skip_group_check=True)
                last.then_inc(counted, 1)

            with pe.Fori(0, NX2) as pair:
                for b in range(2):
                    products(pe, 2 * pair + b)
                    count(b, 2 * pair + b + 1)
            with pe.Fori(NX2, NB // 2) as pair:
                products(pe, pair + NX2)
                for b in range(2):
                    count(b, 2 * pair + b + 1)

        @block.gpsimd
        def _(pool):
            tables.reduce(pool)

        @block.scalar
        def _(act):
            credits(act)
            with act.Fori(0, NXC) as i:
                gelus(act, i)
            tables.exps(act)


def graph_experts(m):
    nc, a, sem, ps, xT, ident, h3 = (m[k] for k in ("nc", "a", "sem", "ps", "xT", "ident", "h3"))
    ctx = m["ctx"]
    full = Arena(m["arena"])
    m["outE"] = outE = full.take(P, NT * FE * D)
    m["keys"], m["picked"], m["cnt"] = full.take(P, EC), full.take(P, CAP), full.take(P, NT)
    m["ends"] = ([full.take(P, CAP, I32) for _ in range(3)] + [full.take(P, CAP) for _ in range(4)]
                 + [full.take(P, CAP, BF16)])
    m["chunks"] = expert_chunks(m, outE)
    att_s, att_d, bg, gamma, beta = (full.take(P, HE) for _ in range(5))
    b2, wg = full.take(P, FE * D), full.take(D + 1, HE)
    loaded = sem("f_loaded")

    def vec(name, n):
        src = a["L1_ffn_" + name]
        if len(src.shape) == 2:
            src = src.rearrange("h e -> (h e)")
        return src.rearrange("(o d) -> o d", o=1).broadcast_to([P, n])

    def load_vectors(sp):
        sp.dma_start(wg[0:D], a["L1_ffn_W_gat"]).then_inc(loaded, 16)
        for dst, name in ((att_s, "att_src"), (att_d, "att_dst"), (bg, "b_gat"), (gamma, "ln_gamma"), (beta, "ln_beta")):
            sp.dma_start(dst, vec(name, HE)).then_inc(loaded, 16)
        sp.dma_start(b2, vec("b2", FE * D)).then_inc(loaded, 16)

    m["load_vectors"] = load_vectors
    def k3(ap, **kw):
        return ap.rearrange("p (k c) -> p k c", **kw)

    ar = full
    nodes, dtab = k3(ar.take(P, NT * CHN), k=NT), k3(ar.take(P, NT * FE), k=NT)
    prod = k3(ar.take(P, NT * CHN), k=NT)
    own = k3(ar.take(P, NT * CHN), k=NT)
    bound, t1, t2 = (k3(ar.take(P, NT * FE), k=NT) for _ in range(3))
    lastrow, G4, G4p = ar.take(P, CHN), ar.take(P, FE), ar.take(P, FE)
    tab = nc.dram_tensor("node_table", [N, CHN], F32, kind="Internal").ap()
    m["tables"] = NodeTables(m, nodes, dtab, prod, own, bound, t1, t2, lastrow, G4, G4p, att_s, att_d, wg, loaded, tab)
    base = full.at
    count_clamped(dict(m, arena=m["arena"][:, base:]))

    gathered_columns(m, ar, tab, dtab, G4, b2)

    pstep, pgate, fin, outd = sem("g_step"), sem("g_gate"), sem("g_fin"), sem("g_outd")
    gated, pool_step, pool_fin = sem("g_gated"), sem("g_pool_step"), sem("g_pool_fin")
    ON_DVE = 23
    sc = k3(ar.take(P, NT * FE), k=NT)
    rank = k3(ar.take(P, NT * FE), k=NT)
    one = [k3(ar.take(P, NT), k=NT) for _ in range(2)]
    ex = k3(ar.take(P, NT * FE), k=NT)
    o4 = outE.rearrange("p (k e d) -> p k e d", k=NT, e=FE)

    def combine(eng, chain, tiles):
        for e in range(FE):
            share = ex[:, tiles, e:e + 1].broadcast_to([P, tiles.stop - tiles.start, D])
            chain(eng.tensor_tensor(o4[:, tiles, e, :], o4[:, tiles, e, :], share, ALU.mult))
            chain(eng.tensor_tensor(h3[:, tiles, :], h3[:, tiles, :], o4[:, tiles, e, :], ALU.add))

    with nc.Block() as block:
        @block.scalar
        def _(act):
            act.wait_ge(pgate, 1)
            act.activation(one[1], one[1], ACT.Sqrt).then_inc(pgate, 1)
            act.wait_ge(pgate, 3)
            act.activation(ex, sc, ACT.Exp).then_inc(pgate, 1)

        @block.vector
        def _(dve):
            n = 0

            def chain(instruction):
                nonlocal n
                n += 1
                instruction.then_inc(pstep, 1)
                dve.wait_ge(pstep, n)

            def per_row(ap, c):
                return ap.broadcast_to([P, NT, c])

            def vecs(ap):
                return ap.rearrange("p (o c) -> p o c", o=1).broadcast_to([P, NT, ap.shape[1]])

            for b0, lo in ((0, 0), (1, NT // 2 + 1)):
                hi = (NT // 2 + 1, NT)[b0]
                chain(dve.tensor_tensor(own[:, lo:hi, :], own[:, lo:hi, :],
                                        ps[:, b0, 0:(hi - lo) * CHN].rearrange("p (k c) -> p k c", c=CHN), ALU.add))
            chain(dve.reciprocal(t1, own[:, :, HE:]))
            agg = prod[:, :, 0:HE]
            split4 = agg.rearrange("p k (h e) -> p k h e", e=FE)
            chain(dve.tensor_tensor(split4, own[:, :, 0:HE].rearrange("p k (h e) -> p k h e", e=FE),
                                    t1.rearrange("p k (h o) -> p k h o", o=1).broadcast_to([P, NT, FE, FE]), ALU.mult))
            chain(dve.tensor_tensor(agg, agg, vecs(bg), ALU.add))
            chain(dve.tensor_reduce(one[0], agg, X, ALU.add))
            chain(dve.tensor_scalar(one[0], one[0], 1.0 / HE, None, ALU.mult))
            chain(dve.tensor_tensor(agg, agg, per_row(one[0], HE), ALU.subtract))
            sq = own[:, :, 0:HE]
            chain(dve.tensor_tensor(sq, agg, agg, ALU.mult))
            chain(dve.tensor_reduce(one[1], sq, X, ALU.add))
            dve.tensor_scalar(one[1], one[1], 1.0 / HE, EPS, ALU.mult, ALU.add).then_inc(pgate, 1)
            dve.wait_ge(pgate, 2)
            chain(dve.reciprocal(one[0], one[1]))
            chain(dve.tensor_tensor(agg, agg, per_row(one[0], HE), ALU.mult))
            chain(dve.tensor_tensor(agg, agg, vecs(gamma), ALU.mult))
            chain(dve.tensor_tensor(agg, agg, vecs(beta), ALU.add))
            chain(dve.tensor_reduce(sc, agg.rearrange("p k (h e) -> p k e h", e=FE), X, ALU.add))
            chain(dve.tensor_scalar(sc, sc, 1.0 / FE, None, ALU.mult))
            for e in range(FE):
                chain(dve.memset(rank[:, :, e:e + 1], float(FE - 1 - e)))
            for i in range(FE):
                for j in range(i + 1, FE):
                    chain(dve.tensor_tensor(one[0], sc[:, :, i:i + 1], sc[:, :, j:j + 1], ALU.is_ge))
                    chain(dve.tensor_tensor(rank[:, :, j:j + 1], rank[:, :, j:j + 1], one[0], ALU.add))
                    chain(dve.tensor_tensor(rank[:, :, i:i + 1], rank[:, :, i:i + 1], one[0], ALU.subtract))
            chain(dve.tensor_reduce(one[0], sc, X, ALU.max))
            dve.tensor_tensor(sc, sc, per_row(one[0], FE), ALU.subtract).then_inc(pgate, 1)
            dve.wait_ge(pgate, 4)
            chain(dve.scalar_tensor_tensor(ex, rank, 1.5, ex, ALU.is_lt, ALU.mult))
            chain(dve.tensor_reduce(one[0], ex, X, ALU.add))
            chain(dve.reciprocal(one[1], one[0]))
            chain(dve.tensor_tensor(ex, ex, per_row(one[1], FE), ALU.mult))
            dve.sem_inc(gated, 1)
            combine(dve, chain, slice(0, ON_DVE))
            dve.sem_inc(fin, 1)

        @block.gpsimd
        def _(pool):
            n = 0

            def chain(instruction):
                nonlocal n
                n += 1
                instruction.then_inc(pool_step, 1)
                pool.wait_ge(pool_step, n)

            pool.wait_ge(gated, 1)
            combine(pool, chain, slice(ON_DVE, NT))
            pool.sem_inc(pool_fin, 1)

        @block.sync
        def _(sp):
            out = a["out"].rearrange("b s d -> (b s) d").rearrange("(k p) d -> p k d", p=P)
            for done, tiles in ((fin, slice(0, ON_DVE)), (pool_fin, slice(ON_DVE, NT))):
                sp.wait_ge(done, 1)
                sp.dma_start(out[:, tiles, :], h3[:, tiles, :]).then_inc(outd, 16)
            sp.wait_ge(outd, 32)


def gathered_columns(m, ar, tab, dtab, G4, b2):
    nc, sem, ps, identb = (m[k] for k in ("nc", "sem", "ps", "identb"))
    picked, keys = m["picked"], m["keys"]

    def k3(ap, **kw):
        return ap.rearrange("p (k c) -> p k c", **kw)

    kint, klo, srci, dhi, ta, tb, kf, dlob = ends = m["ends"]
    iota, iotab = ar.take(P, P), ar.take(P, P, BF16)
    iotai = ar.take(P, P, I32)
    idx = [ar.take(P, GC, I32) for _ in range(2)]
    rows_ = [k3(ar.take(P, GC * CHN), k=GC) for _ in range(2)]
    hot = k3(ar.take(P, GC * P, BF16), k=GC)
    hot32 = [k3(ar.take(P, GC * P), k=GC) for _ in range(2)]
    hotT = ar.take(P, GC * P, BF16)
    high = [k3(ar.take(P, GC * NT), k=GC) for _ in range(2)]
    dparts = [ar.take(P, NT * FE, BF16) for _ in range(3)]
    drest = ar.take(P, NT * FE)
    looked_up = ar.take(P, 4 * NT * FE).rearrange("p (c k f) -> p c k f", c=4, k=NT)
    dval, za, zb, wt = (k3(ar.take(P, GC * FE), k=GC) for _ in range(4))
    val = k3(ar.take(P, GC * CHN), k=GC)
    NQ = 4
    prod = [ar.take(P, NQ * NT * CHN).rearrange("p (c k f) -> p c k f", c=NQ, k=NT) for _ in range(3)]
    buffer = (0, 1, 0, 2)
    zero = ar.take(P, 330)
    QG = GC // NQ
    SPLIT = NT // 2 + 1
    flag = ar.take(P, 1)
    flagi = ar.take(P, 1, I32)
    rest = ar.take(P, 1)

    def chained(dve, s, base):
        n = 0

        def chain(instruction):
            nonlocal n
            n += 1
            instruction.then_inc(s, 1)
            dve.wait_ge(s, base + n)
        return chain

    def signals(tag):
        names = ("decoded", "idx", "consumed", "hot", "step", "turned", "hotT_kept", "hot32_made", "looked",
                 "selected", "weighable", "weights", "products", "pool_products", "quads")
        s = {n: sem(f"{tag}_{n}") for n in names}
        s["gathered"] = [sem(f"{tag}_gathered_{i}") for i in range(2)]
        return s

    SELECT_AT = 1
    WEIGH_AT = SELECT_AT + 2 * QG
    STEPS = WEIGH_AT + 7


    def fetch(pool, s, g, par, j, at):
        pool.wait_ge(s["consumed"], g + 1)
        settle(pool)
        pool.tensor_copy(idx[par], srci[:, at]).then_inc(s["idx"], 1)
        pool.wait_ge(s["idx"], g + 1)
        settle(pool)
        for c in range(GC):
            pool.indirect_dma_start(rows_[par][:, c, :], None, tab, bass.IndirectOffsetOnAxis(ap=idx[par][:, c:c + 1], axis=0)).then_inc(s["gathered"][par], 16)

    def onehots(dve, s, g, par, at):
        def col(ap, c):
            return ap.rearrange("p (c o) -> p c o", o=1).broadcast_to([P, GC, c])

        dve.wait_ge(s["turned"], 2 * g + 2)
        dve.wait_ge(s["hot32_made"], g + 1)
        dve.tensor_tensor(hot, col(dlob[:, at], P), iotab.rearrange("p (o v) -> p o v", o=1).broadcast_to([P, GC, P]),
                          ALU.is_equal).then_inc(s["hot"], 1)
        dve.tensor_tensor(high[par], col(dhi[:, at], NT), iota[:, 0:NT].rearrange("p (o v) -> p o v", o=1).broadcast_to([P, GC, NT]),
                          ALU.is_equal).then_inc(s["step"], 1)
        dve.wait_ge(s["step"], STEPS * g + 1)

    def turn(pe, s, g):
        pe.wait_ge(s["hot"], g + 1)
        for i in range(2):
            pe.wait_ge(s["hotT_kept"], 2 * g + i + 1)
            settle(pe)
            pb = ps[:, 2 + i, :].bitcast(BF16)
            for c in range(8):
                last = pe.transpose(pb[:, P * c:P * c + P], hot[:, 8 * i + c, :], identb[:])
            last.then_inc(s["turned"], 1)

    def keep(act, s, g, par):
        for i in range(2):
            act.wait_ge(s["turned"], 2 * g + i + 1 + 2)
            act.wait_ge(s["looked"], QG * g + 2 * i + 2)
            act.activation(hotT[:, 8 * P * i:8 * P * i + 8 * P], ps[:, 2 + i, :].bitcast(BF16), ACT.Copy).then_inc(s["hotT_kept"], 1)
        act.wait_ge(s["hot"], g + 1)
        act.wait_ge(s["quads"], QG * g + QG)
        act.activation(hot32[par], hot, ACT.Copy).then_inc(s["hot32_made"], 1)

    def look(pe, s, g, q):
        pe.wait_ge(s["hotT_kept"], 2 * g + q // 2 + 1 + 2)
        pe.wait_ge(s["selected"], QG * g + q + 1)
        settle(pe)
        for c in range(NQ):
            for n, part in enumerate(dparts):
                last = pe.matmul(ps[:, 4 + 2 * (q % 2) + c // 2, 256 * (c % 2):256 * (c % 2) + NT * FE],
                                 hotT[:, P * (NQ * q + c):P * (NQ * q + c) + P], part, start=(n == 0), stop=(n == 2))
        last.then_inc(s["looked"], 1)

    def select(dve, s, g, par, q):
        b = 4 + 2 * (q % 2)
        cs = slice(NQ * q, NQ * q + NQ)
        chain = chained(dve, s["step"], STEPS * g + SELECT_AT + 2 * q)
        dve.wait_ge(s["looked"], QG * g + q + 1 + 4)
        src = ps[:, b:b + 2, :].rearrange("p b (c x) -> p (b c) x", c=2)[:, :, 0:NT * FE].rearrange("p c (k f) -> p c k f", f=FE)
        chain(dve.tensor_tensor(looked_up, src, high[par][:, cs, :].rearrange("p c (k o) -> p c k o", o=1).broadcast_to([P, NQ, NT, FE]), ALU.mult))
        dve.sem_inc(s["selected"], 1)
        chain(dve.tensor_reduce(dval[:, cs, :], looked_up.rearrange("p c k f -> p c f k"), X, ALU.add))

    def weigh(dve, s, g, par, j):
        chain = chained(dve, s["step"], STEPS * g + WEIGH_AT)
        dve.wait_ge(s["gathered"][par], 16 * GC * (j + 1))
        g4 = G4.rearrange("p (o v) -> p o v", o=1).broadcast_to([P, GC, FE])
        chain(dve.tensor_tensor(za, rows_[par][:, :, HE:], dval, ALU.add))
        chain(dve.scalar_tensor_tensor(za, za, 0.2, za, ALU.mult, ALU.max))
        chain(dve.tensor_tensor(zb, dval, g4, ALU.add))
        chain(dve.scalar_tensor_tensor(zb, zb, 0.2, zb, ALU.mult, ALU.max))
        chain(dve.tensor_tensor(za, za, zb, ALU.subtract))
        dve.sem_inc(s["weighable"], 1)
        dve.wait_ge(s["weights"], g + 1)
        dve.wait_ge(s["products"], (QG - 1) * g + QG - 1)
        dve.wait_ge(s["pool_products"], g + 1)
        chain(dve.tensor_copy(val[:, :, HE:], wt))
        chain(dve.tensor_tensor(val[:, :, 0:HE].rearrange("p c (h e) -> p c h e", e=FE),
                                rows_[par][:, :, 0:HE].rearrange("p c (h e) -> p c h e", e=FE),
                                wt.rearrange("p c (h o) -> p c h o", o=1).broadcast_to([P, GC, FE, FE]), ALU.mult))
        dve.sem_inc(s["consumed"], 1)

    def spread(eng, s, g, par, q):
        cs = slice(NQ * q, NQ * q + NQ)
        if q < QG - 1:
            eng.wait_ge(s["quads"], QG * g + (-2, -1, 1)[q] + 2 * QG)
            signal = s["products"]
        else:
            eng.wait_ge(s["consumed"], g + 1 + 2)
            settle(eng)
            eng.wait_ge(s["quads"], QG * g + 2 * QG)
            settle(eng)
            signal = s["pool_products"]
        eng.tensor_tensor(prod[buffer[q]], high[par][:, cs, :].rearrange("p c (k o) -> p c k o", o=1).broadcast_to([P, NQ, NT, CHN]),
                          val[:, cs, :].rearrange("p c (o f) -> p c o f", o=1).broadcast_to([P, NQ, NT, CHN]),
                          ALU.mult).then_inc(signal, 1)

    def exps(act, s, g):
        act.wait_ge(s["weighable"], g + 1)
        act.activation(wt, za, ACT.Exp).then_inc(s["weights"], 1)

    def add(pe, s, g, par, q):
        if q == 0:
            pe.wait_ge(s["hot32_made"], g + 1 + 1)
        if q < QG - 1:
            pe.wait_ge(s["products"], (QG - 1) * (g + 1) + q + 1)
        else:
            pe.wait_ge(s["pool_products"], g + 1 + 1)
        settle(pe)
        for c in range(NQ):
            lhs = hot32[par][:, NQ * q + c, :]
            pe.matmul(ps[:, 0, 0:SPLIT * CHN], lhs, prod[buffer[q]][:, c, 0:SPLIT, :], start=False, stop=False, skip_group_check=True)
            last = pe.matmul(ps[:, 1, 0:(NT - SPLIT) * CHN], lhs, prod[buffer[q]][:, c, SPLIT:, :], start=False, stop=False, skip_group_check=True)
        last.then_inc(s["quads"], 1)

    def dve_credits(dve, s):
        dve.sem_inc(s["quads"], 2 * QG)
        dve.sem_inc(s["products"], QG - 1)
        dve.sem_inc(s["pool_products"], 1)
        dve.sem_inc(s["selected"], 2)

    def act_credits(act, s):
        act.sem_inc(s["hot32_made"], 1)
        act.sem_inc(s["hotT_kept"], 2)
        act.sem_inc(s["turned"], 2)
        act.sem_inc(s["looked"], QG)

    S1 = signals("m")
    step, zeroed = sem("h_step"), sem("h_zeroed")
    GROUPS = CAP // GC

    def at(g):
        return slice(g * GC, g * GC + GC) if isinstance(g, int) else bass.ds(g * GC, GC)

    with nc.Block() as block:
        @block.gpsimd
        def _(pool):
            pool.iota(iotai, [[1, P]], base=0, channel_multiplier=0).then_inc(zeroed, 1)
            pool.sem_inc(S1["consumed"], 2)
            for g in range(2):
                fetch(pool, S1, g, g, 0, at(g))
            with pool.Fori(0, GROUPS // 2 - 1) as pair:
                for par in range(2):
                    g = 2 * pair + par
                    spread(pool, S1, g, par, QG - 1)
                    fetch(pool, S1, g + 2, par, pair + 1, at(g + 2))
            for g in range(GROUPS - 2, GROUPS):
                spread(pool, S1, g, g % 2, QG - 1)
            flat = m["outE"].rearrange("p (k c) -> p k c", k=NT)
            pool.tensor_tensor(flat, flat, b2.rearrange("p (o c) -> p o c", o=1).broadcast_to([P, NT, FE * D]), ALU.add)

        @block.tensor
        def _(pe):
            pe.wait_ge(zeroed, 2)
            pe.matmul(ps[:, 0, 0:330], zero[:, 0:P], zero, start=True, stop=False, skip_group_check=True)
            pe.matmul(ps[:, 1, 0:330], zero[:, 0:P], zero, start=True, stop=False, skip_group_check=True)
            turn(pe, S1, 0)
            for q in range(QG):
                look(pe, S1, 0, q)

            def group(g, par, more):
                add(pe, S1, g, par, 0)
                if more:
                    turn(pe, S1, g + 1)
                add(pe, S1, g, par, 1)
                if more:
                    look(pe, S1, g + 1, 0)
                    look(pe, S1, g + 1, 1)
                add(pe, S1, g, par, 2)
                if more:
                    look(pe, S1, g + 1, 2)
                    look(pe, S1, g + 1, 3)
                add(pe, S1, g, par, 3)

            with pe.Fori(0, GROUPS // 2 - 1) as pair:
                group(2 * pair, 0, True)
                group(2 * pair + 1, 1, True)
            group(GROUPS - 2, 0, True)
            group(GROUPS - 1, 1, False)

        @block.scalar
        def _(act):
            act_credits(act, S1)
            keep(act, S1, 0, 0)
            exps(act, S1, 0)
            with act.Fori(0, GROUPS // 2 - 1) as pair:
                for par in range(2):
                    g = 2 * pair + par + 1
                    keep(act, S1, g, 1 - par)
                    exps(act, S1, g)
            keep(act, S1, GROUPS - 1, 1)
            exps(act, S1, GROUPS - 1)

        @block.vector
        def _(dve):
            dve_credits(dve, S1)
            dve.memset(zero, 0.0).then_inc(zeroed, 1)
            chain = chained(dve, step, 0)
            dve.wait_ge(zeroed, 2)
            chain(dve.tensor_copy(iota, iotai))
            chain(dve.tensor_copy(iotab, iotai))
            chain(dve.tensor_reduce(rest, keys, X, ALU.max))
            flat = dtab.rearrange("p k f -> p (k f)")
            chain(dve.tensor_copy(dparts[0], flat))
            chain(dve.tensor_tensor(drest, flat, dparts[0], ALU.subtract))
            chain(dve.tensor_copy(dparts[1], drest))
            chain(dve.tensor_tensor(drest, drest, dparts[1], ALU.subtract))
            chain(dve.tensor_copy(dparts[2], drest))
            onehots(dve, S1, 0, 0, at(0))
            for q in range(QG):
                select(dve, S1, 0, 0, q)
            weigh(dve, S1, 0, 0, 0)

            def group(g, par, j, more):
                spread(dve, S1, g, par, 0)
                spread(dve, S1, g, par, 1)
                if more:
                    onehots(dve, S1, g + 1, 1 - par, at(g + 1))
                spread(dve, S1, g, par, 2)
                if more:
                    for q in range(QG):
                        select(dve, S1, g + 1, 1 - par, q)
                    weigh(dve, S1, g + 1, 1 - par, j + par)

            with dve.Fori(0, GROUPS // 2 - 1) as pair:
                group(2 * pair, 0, pair, True)
                group(2 * pair + 1, 1, pair, True)
            group(GROUPS - 2, 0, GROUPS // 2 - 1, True)
            group(GROUPS - 1, 1, GROUPS // 2 - 1, False)

    S2 = signals("r")
    all_left, flagged = sem("r_all_left"), sem("r_flagged")
    rstep, m8 = sem("r_keys"), ar.take(P, 8)
    ROUNDS = (EC - CAP) // GC
    ROUND_STEPS = DEC + 3 * (GC // 8)

    def any_left(eng):
        eng.wait_ge(flagged, 1)
        return eng.If(eng.value_load(flagi[0:1, 0:1], min_val=0, max_val=1) > 0)

    with nc.Block() as block:
        @block.gpsimd
        def _(pool):
            pool.partition_all_reduce(flag, rest, P, bass.bass_isa.ReduceOp.max).then_inc(all_left, 1)
            pool.sem_inc(S2["consumed"], 2)
            with any_left(pool):
                with pool.Fori(0, ROUNDS) as g:
                    pool.wait_ge(S2["decoded"], g + 1)
                    fetch(pool, S2, g, 0, g, at(0))
                    spread(pool, S2, g, 0, QG - 1)

        @block.tensor
        def _(pe):
            with any_left(pe):
                with pe.Fori(0, ROUNDS) as g:
                    turn(pe, S2, g)
                    for q in range(QG):
                        look(pe, S2, g, q)
                    for q in range(QG):
                        add(pe, S2, g, 0, q)

        @block.scalar
        def _(act):
            act_credits(act, S2)
            with any_left(act):
                with act.Fori(0, ROUNDS) as g:
                    keep(act, S2, g, 0)
                    exps(act, S2, g)

        @block.vector
        def _(dve):
            dve_credits(dve, S2)
            dve.wait_ge(all_left, 1)
            dve.tensor_scalar(flagi, flag, NONE / 2, None, ALU.is_gt).then_inc(flagged, 1)
            with any_left(dve):
                with dve.Fori(0, ROUNDS) as g:
                    once = chained(dve, rstep, ROUND_STEPS * g)

                    def chain(instruction):
                        once(instruction)
                        settle(dve)

                    for q in range(GC // 8):
                        chain(dve.max(m8, keys))
                        chain(dve.tensor_copy(picked[:, 8 * q:8 * q + 8], m8))
                        chain(dve.match_replace(out=keys, in_to_replace=m8, in_values=keys, imm_value=NONE))
                    decode(chain, dve, ends, GC, picked[:, 0:GC])
                    dve.sem_inc(S2["decoded"], 1)
                    onehots(dve, S2, g, 0, at(0))
                    for q in range(QG):
                        select(dve, S2, g, 0, q)
                    weigh(dve, S2, g, 0, g)
                    for q in range(QG - 1):
                        spread(dve, S2, g, 0, q)
                    dve.wait_ge(S2["quads"], QG * g + QG + 2 * QG)
                    settle(dve)


def expert_chunks(m, outE):
    a, sem, ps, xT = (m[k] for k in ("a", "sem", "ps", "xT"))
    wa = Arena(m["weights"])
    w1, w2 = wa.take(D + 1, FE * P), wa.take(P, FE * D)
    hh = [wa.take(P, 3 * P) for _ in range(2)]
    w_in, hid, gel, used, outm, outk = (sem("x_" + s) for s in ("w_in", "hid", "gel", "used", "outm", "outk"))
    out3 = outE.rearrange("p (k c) -> p k c", k=NT)

    def load(sp):
        sp.dma_start(w1[0:D].rearrange("p (e f) -> p e f", e=FE), a["L1_ffn_W1"].rearrange("e d f -> d e f")).then_inc(w_in, 16)
        sp.dma_start(w1[D:D + 1], a["L1_ffn_b1"].rearrange("e f -> (e f)").rearrange("(o d) -> o d", o=1)).then_inc(w_in, 16)
        sp.dma_start(w2.rearrange("p (e d) -> p e d", e=FE), a["L1_ffn_W2"].rearrange("e f d -> f e d")).then_inc(w_in, 16)

    def products(pe, i):
        pe.wait_ge(w_in, 48)
        settle(pe)

        def hidden(e):
            if e >= 2:
                pe.wait_ge(gel, FE * i + e - 1)
                settle(pe)
            pe.matmul(ps[:, 2 + e % 2, 0:3 * P], w1[:, P * e:P * e + P], xT[:, bass.ds(i * 3 * P, 3 * P)], start=True, stop=True).then_inc(hid, 1)

        def project(e):
            pe.wait_ge(gel, FE * i + e + 1)
            if e == 0:
                pe.wait_ge(outk, i + 1)
            settle(pe)
            for t in range(3):
                last = pe.matmul(ps[:, 4 + t // 2, 256 * (t % 2) + D * e:256 * (t % 2) + D * e + D],
                                 hh[e % 2][:, P * t:P * t + P], w2[:, D * e:D * e + D], start=True, stop=True)
            last.then_inc(outm if e == FE - 1 else used, 1)

        hidden(0)
        hidden(1)
        for e in range(FE):
            if e + 2 < FE:
                hidden(e + 2)
            project(e)

    def gelus(act, i):
        for e in range(FE):
            act.wait_ge(hid, FE * i + e + 1)
            if e >= 2:
                act.wait_ge(used, (FE - 1) * i + e - 1)
            act.activation(hh[e % 2], ps[:, 2 + e % 2, 0:3 * P], ACT.Gelu).then_inc(gel, 1)
        act.wait_ge(outm, i + 2)
        act.activation(out3[:, bass.ds(i * 3, 3), :],
                       ps[:, 4:6, :].rearrange("p b (t c) -> p (b t) c", t=2)[:, 0:3, :], ACT.Copy).then_inc(outk, 1)

    def credits(act):
        act.sem_inc(outm, 1)
        act.sem_inc(outk, 1)

    return load, products, gelus, credits


_TRANSPOSED = ("L1_attn_Wq", "L1_attn_Wk", "L1_attn_Wv", "L0_ffn_proj_w")


def tables():
    bf = mybir.dt.np(BF16)
    i = np.arange(P)
    out = {"ident": np.eye(P, dtype=np.float32), "identb": np.eye(P, dtype=bf)}
    later = i[None, :] > i[:, None]
    out["mask_kq"] = np.where(later.T, MASKED, 0.0).astype(bf)
    out["mask_qk"] = np.where(later, MASKED, 0.0).astype(bf)
    s = np.arange(SP_)
    slopes = 0.5 ** np.arange(1, HEADS + 1)
    hi, lo = s // 32 * 32, s % 32
    one = np.ones(SP_)
    out["bias_k"] = np.stack([np.stack([f * hi, f * lo, one, one, one, one]) for f in slopes], 1).astype(bf)
    out["bias_q"] = np.stack([np.stack([one, one, -f * hi, -f * lo]) for f in slopes], 1).astype(bf)
    d = np.arange(S)[None, :] - i[:, None]
    decay = np.exp(d.astype(np.float32) * np.log(np.float32(GAMMA)))
    out["decay"] = np.where(d >= 0, decay, 0.0).astype(np.float32)
    pair = np.zeros((P, D), bf)
    pair[i, i % D] = 1
    out["pair_sum"] = pair
    row = np.zeros((P, P), bf)
    row[:] = i.astype(bf)
    out["count_row"] = row
    return out


def kernel(**inputs):
    import concourse.bacc as _bacc
    from concourse.bass_utils import run_bass_kernel_spmd as _run

    nc = _bacc.Bacc("TRN2", target_bir_lowering=False, num_devices=1)
    arrays, a, c = {}, {}, {}

    def give(name, x):
        arrays[name] = x
        return nc.dram_tensor(name, x.shape, mybir.dt.from_np(x.dtype), kind="ExternalInput").ap()

    for name, x in inputs.items():
        x = np.asarray(x)
        if name in _TRANSPOSED:
            x = x.T
        a[name] = give(f"in_{name}", np.ascontiguousarray(x).reshape(x.shape or (1,)))
    for name, x in tables().items():
        c[name] = give(f"table_{name}", x)
    a["out"] = nc.dram_tensor("out_h", (B, S, D), F32, kind="ExternalOutput").ap()
    build(nc, a, c)
    r = _run(nc, [arrays], core_ids=[0])
    return r.results[0]["out_h"]
```
